# Optimizing a Trainium2 kernel written in Bass

```python
import numpy as np
import jax
import jax.numpy as jnp

def _softmax(x, axis=-1):
    return jax.nn.softmax(x, axis=axis)

def _gelu(x):
    return jax.nn.gelu(x, approximate=True)

def _silu(x):
    return jax.nn.silu(x)

def _sigmoid(x):
    return jax.nn.sigmoid(x)

def _layernorm(x, axis=-1, eps=1e-05):
    m = jnp.mean(x, axis=axis, keepdims=True)
    v = jnp.var(x, axis=axis, keepdims=True)
    return (x - m) / jnp.sqrt(v + eps)

def _scatter_add(tgt, idx, src, axis=0):
    return tgt.at[idx].add(src)

def _segment_sum(src, seg, n):
    return jax.ops.segment_sum(src, seg, n)
kernel_name = 'mk_decoder_preln_d2_seqx_r8_c9a1c7'

def setup_inputs(seed: int=0):
    np.random.seed(seed)
    _w = jnp.asarray

    def _rec_inputs():
        import jax
        import jax.numpy as jnp
        _rk = jax.random.key(seed)
        x = -0.0005207 + 1.001 * jax.random.normal(jax.random.fold_in(_rk, 1), (8, 128, 128), jnp.float32)
        _lenS = 128 - jax.random.randint(jax.random.fold_in(_rk, 7), (8,), 0, max(1, 128 // 4) + 1, jnp.int32)
        _lenS2 = 128 - jax.random.randint(jax.random.fold_in(_rk, 8), (8,), 0, max(1, 128 // 4) + 1, jnp.int32)
        _ctx_1024P = jax.random.normal(jax.random.fold_in(_rk, 11), (8, 16, 128), jnp.float32)
        _ctx_1024c = jax.random.dirichlet(jax.random.fold_in(_rk, 511), 0.3 * jnp.ones((16,), jnp.float32), (8, 128))
        _ctx_1024t = jnp.einsum('bsk,bkd->bsd', _ctx_1024c, _ctx_1024P)
        _ctx_1024t = _ctx_1024t * jax.lax.rsqrt(jnp.mean(jnp.square(_ctx_1024t)) + 1e-12) * 0.953939
        ctx_1024 = -0.000514642 + 1.00011 * (_ctx_1024t + 0.3 * jax.random.normal(jax.random.fold_in(_rk, 611), (8, 128, 128), jnp.float32))
        return (x, ctx_1024)
    x, ctx_1024 = _rec_inputs()

    def _L0_attn_setup():
        import jax, jax.numpy as jnp
        import numpy as np
        B, L, D = (4, 256, 128)
        E, F, H = (6, 192, 64)
        TOP_K = 2
        LN_EPS = 1e-05
        key = jax.random.key(seed)
        ks = jax.random.split(key, 8)
        s = lambda fan: 1.0 / np.sqrt(fan)
        return {'x': jax.random.normal(ks[0], (B, L, D), jnp.float32), 'r1_w': jax.random.normal(ks[1], (D, H), jnp.float32) * s(D), 'r1_b': jnp.zeros((H,), jnp.float32), 'ln_g': jnp.ones((H,), jnp.float32), 'ln_b': jnp.zeros((H,), jnp.float32), 'r2_w': jax.random.normal(ks[2], (H, E), jnp.float32) * s(H), 'r2_b': jnp.zeros((E,), jnp.float32), 'temp': jnp.ones((1,), jnp.float32), 'route_bias': jnp.zeros((E,), jnp.float32), 'W1': jax.random.normal(ks[3], (E, D, F), jnp.float32) * s(D), 'b1': jnp.zeros((E, F), jnp.float32), 'W2': jax.random.normal(ks[4], (E, F, D), jnp.float32) * s(F), 'b2': jnp.zeros((E, D), jnp.float32)}
    _L0_attn_all = _L0_attn_setup()
    _L0_attn_in = {k: v for k, v in _L0_attn_all.items() if k in ('r1_w', 'r1_b', 'ln_g', 'ln_b', 'r2_w', 'r2_b', 'temp', 'route_bias', 'W1', 'b1', 'W2', 'b2')}
    del _L0_attn_all

    def _L0_xattn_setup():
        import jax, jax.numpy as jnp
        import numpy as np
        import math
        B, S, D, H = (1, 256, 128, 16)
        DK = D // H
        DH = 64
        LOG_T_MIN = math.log(0.1)
        LOG_T_MAX = math.log(10.0)

        def _linear(x, W, b):
            return x @ W.T + b
        key = jax.random.key(seed)
        ks = jax.random.split(key, 20)
        p = 0.02
        return {'query': jax.random.normal(ks[0], (B, S, D), jnp.float32), 'key': jax.random.normal(ks[1], (B, S, D), jnp.float32), 'value': jax.random.normal(ks[2], (B, S, D), jnp.float32), 'Wq': jax.random.normal(ks[3], (D, D), jnp.float32) * p, 'bq': jax.random.normal(ks[4], (D,), jnp.float32) * p, 'Wk': jax.random.normal(ks[5], (D, D), jnp.float32) * p, 'bk': jax.random.normal(ks[6], (D,), jnp.float32) * p, 'Wv': jax.random.normal(ks[7], (D, D), jnp.float32) * p, 'bv': jax.random.normal(ks[8], (D,), jnp.float32) * p, 'Wo': jax.random.normal(ks[9], (D, D), jnp.float32) * p, 'bo': jax.random.normal(ks[10], (D,), jnp.float32) * p, 'w1': jax.random.normal(ks[11], (DH, 3), jnp.float32) * 0.3, 'b1': jax.random.normal(ks[12], (DH,), jnp.float32) * 0.1, 'w2': jax.random.normal(ks[13], (DH, DH), jnp.float32) * 0.1, 'b2': jax.random.normal(ks[14], (DH,), jnp.float32) * 0.1, 'w3': jax.random.normal(ks[15], (1, DH), jnp.float32) * 0.1, 'b3': jnp.full((1,), (LOG_T_MIN + LOG_T_MAX) / 2, jnp.float32)}
    _L0_xattn_all = _L0_xattn_setup()
    _L0_xattn_in = {k: v for k, v in _L0_xattn_all.items() if k in ('Wq', 'bq', 'Wk', 'bk', 'Wv', 'bv', 'Wo', 'bo', 'w1', 'b1', 'w2', 'b2', 'w3', 'b3')}
    del _L0_xattn_all

    def _L0_ffn_setup():
        import jax, jax.numpy as jnp
        import numpy as np

        def fixed_quant(x, width, frac_width):
            scale = jnp.float32(2.0 ** frac_width)
            imax = jnp.float32(2 ** (width - 1) - 1)
            imin = jnp.float32(-2 ** (width - 1))
            return jnp.clip(jnp.round(x * scale), imin, imax) / scale
        IN_F, HID_F, OUT_F = (128, 512, 128)
        B, S = (4, 256)
        ACT_Q = (8, 4)
        W_Q = (8, 6)
        BIAS_Q = (8, 6)

        def quantized_linear(x, w, b):
            xq = fixed_quant(x, *ACT_Q)
            wq = fixed_quant(w, *W_Q)
            bq = fixed_quant(b, *BIAS_Q)
            return jnp.einsum('bsi,oi->bso', xq, wq) + bq

        def quantized_relu(x):
            return jax.nn.relu(fixed_quant(x, *ACT_Q))
        key = jax.random.key(seed)
        k_x, k_w1, k_b1, k_w2, k_b2 = jax.random.split(key, 5)
        x = jax.random.normal(k_x, (B, S, IN_F), dtype=jnp.float32)
        w1 = jax.random.normal(k_w1, (HID_F, IN_F), dtype=jnp.float32) / np.sqrt(IN_F)
        b1 = jax.random.normal(k_b1, (HID_F,), dtype=jnp.float32) / np.sqrt(IN_F)
        w2 = jax.random.normal(k_w2, (OUT_F, HID_F), dtype=jnp.float32) / np.sqrt(HID_F)
        b2 = jax.random.normal(k_b2, (OUT_F,), dtype=jnp.float32) / np.sqrt(HID_F)
        return {'x': x, 'w1': w1, 'b1': b1, 'w2': w2, 'b2': b2}
    _L0_ffn_all = _L0_ffn_setup()
    _L0_ffn_in = {k: v for k, v in _L0_ffn_all.items() if k in ('w1', 'b1', 'w2', 'b2')}
    del _L0_ffn_all

    def _L1_attn_setup():
        import jax, jax.numpy as jnp
        import numpy as np
        D_MODEL = 128
        D_STATE = 16
        D_CONV = 4
        EXPAND = 2
        D_INNER = EXPAND * D_MODEL
        DT_MIN, DT_MAX = (0.001, 0.1)
        BATCH, SEQ = (4, 256)

        def _silu(v):
            return v * jax.nn.sigmoid(v)
        key = jax.random.key(seed)
        ks = jax.random.split(key, 5)
        x = jax.random.normal(ks[0], (BATCH, SEQ, D_MODEL), jnp.float32)
        W_in = jax.random.normal(ks[1], (2 * D_INNER, D_MODEL), jnp.float32) / np.sqrt(D_MODEL)
        conv_w = jax.random.normal(ks[2], (D_INNER, D_CONV), jnp.float32) / np.sqrt(D_CONV)
        conv_b = jnp.zeros((D_INNER,), jnp.float32)
        W_xproj = jax.random.normal(ks[3], (2 * D_STATE + 1, D_INNER), jnp.float32) / np.sqrt(D_INNER)
        A_log = jnp.log(jnp.arange(1, D_STATE + 1, dtype=jnp.float32))
        D_param = jnp.ones((D_INNER,), jnp.float32)
        W_out = jax.random.normal(ks[4], (D_MODEL, D_INNER), jnp.float32) / np.sqrt(D_INNER)
        return dict(x=x, W_in=W_in, conv_w=conv_w, conv_b=conv_b, W_xproj=W_xproj, A_log=A_log, D_param=D_param, W_out=W_out)
    _L1_attn_all = _L1_attn_setup()
    _L1_attn_in = {k: v for k, v in _L1_attn_all.items() if k in ('W_in', 'conv_w', 'conv_b', 'W_xproj', 'A_log', 'D_param', 'W_out')}
    del _L1_attn_all

    def _L1_xattn_setup():
        import jax, jax.numpy as jnp
        import numpy as np
        key = jax.random.key(seed)
        ks = jax.random.split(key, 7)
        B, S, D, H, Dh = (4, 256, 128, 16, 64)
        return {'query_input': jax.random.normal(ks[0], (B, S, D), jnp.float32), 'key_input': jax.random.normal(ks[1], (B, S, D), jnp.float32), 'value_input': jax.random.normal(ks[2], (B, S, D), jnp.float32), 'Wq': jax.random.normal(ks[3], (D, H, Dh), jnp.float32) * 0.03, 'Wk': jax.random.normal(ks[4], (D, H, Dh), jnp.float32) * 0.03, 'Wv': jax.random.normal(ks[5], (D, H, Dh), jnp.float32) * 0.03, 'Wo': jax.random.normal(ks[6], (H, Dh, D), jnp.float32) * 0.03}
    _L1_xattn_all = _L1_xattn_setup()
    _L1_xattn_in = {k: v for k, v in _L1_xattn_all.items() if k in ('Wq', 'Wk', 'Wv', 'Wo')}
    del _L1_xattn_all

    def _L1_ffn_setup():
        import jax, jax.numpy as jnp
        import numpy as np
        import math
        D_MODEL = 128
        N_EXPERTS = 16
        D_FF = 512
        CAP_FACTOR = 1.25
        MIN_CAPACITY = 4

        def _capacity(num_tokens, num_experts):
            cap = math.floor(CAP_FACTOR * num_tokens / num_experts)
            cap += cap % 2
            return max(cap, MIN_CAPACITY)

        def _top1_router(gate_logits, capacity):
            s, e = gate_logits.shape
            probs = jax.nn.softmax(gate_logits, axis=-1)
            top1 = jnp.argmax(gate_logits, axis=-1)
            mask = jax.nn.one_hot(top1, e, dtype=jnp.int32)
            ranks = jnp.cumsum(mask, axis=0) - 1
            mask = mask * (ranks < capacity).astype(jnp.int32)
            rank1 = jnp.sum(mask * ranks, axis=-1)
            ranks_oh = jax.nn.one_hot(rank1, capacity, dtype=probs.dtype)
            weight = mask.astype(probs.dtype) * probs
            combine_weights = weight[:, :, None] * ranks_oh[:, None, :]
            sec_mask = combine_weights > 0
            return (combine_weights, sec_mask)
        key = jax.random.key(seed)
        k1, k2, k3, k4 = jax.random.split(key, 4)
        x = jax.random.normal(k1, (4, 256, D_MODEL), dtype=jnp.float32)
        gate_w = jax.random.normal(k2, (N_EXPERTS, D_MODEL), dtype=jnp.float32) * math.sqrt(0.1 / D_MODEL)
        w1 = jax.random.normal(k3, (N_EXPERTS, D_MODEL, D_FF), dtype=jnp.float32) * (1.0 / math.sqrt(D_MODEL))
        w2 = jax.random.normal(k4, (N_EXPERTS, D_FF, D_MODEL), dtype=jnp.float32) * (1.0 / math.sqrt(D_FF))
        return {'x': x, 'gate_w': gate_w, 'w1': w1, 'w2': w2}
    _L1_ffn_all = _L1_ffn_setup()
    _L1_ffn_in = {k: v for k, v in _L1_ffn_all.items() if k in ('gate_w', 'w1', 'w2')}
    del _L1_ffn_all
    return {'x': x, 'ctx_1024': ctx_1024, 'L0_attn_r1_w': _L0_attn_in['r1_w'], 'L0_attn_r1_b': _L0_attn_in['r1_b'], 'L0_attn_ln_g': _L0_attn_in['ln_g'], 'L0_attn_ln_b': _L0_attn_in['ln_b'], 'L0_attn_r2_w': _L0_attn_in['r2_w'], 'L0_attn_r2_b': _L0_attn_in['r2_b'], 'L0_attn_temp': _L0_attn_in['temp'], 'L0_attn_route_bias': _L0_attn_in['route_bias'], 'L0_attn_W1': _L0_attn_in['W1'], 'L0_attn_b1': _L0_attn_in['b1'], 'L0_attn_W2': _L0_attn_in['W2'], 'L0_attn_b2': _L0_attn_in['b2'], 'L0_xattn_Wq': _L0_xattn_in['Wq'], 'L0_xattn_bq': _L0_xattn_in['bq'], 'L0_xattn_Wk': _L0_xattn_in['Wk'], 'L0_xattn_bk': _L0_xattn_in['bk'], 'L0_xattn_Wv': _L0_xattn_in['Wv'], 'L0_xattn_bv': _L0_xattn_in['bv'], 'L0_xattn_Wo': _L0_xattn_in['Wo'], 'L0_xattn_bo': _L0_xattn_in['bo'], 'L0_xattn_w1': _L0_xattn_in['w1'], 'L0_xattn_b1': _L0_xattn_in['b1'], 'L0_xattn_w2': _L0_xattn_in['w2'], 'L0_xattn_b2': _L0_xattn_in['b2'], 'L0_xattn_w3': _L0_xattn_in['w3'], 'L0_xattn_b3': _L0_xattn_in['b3'], 'L0_ffn_w1': _L0_ffn_in['w1'], 'L0_ffn_b1': _L0_ffn_in['b1'], 'L0_ffn_w2': _L0_ffn_in['w2'], 'L0_ffn_b2': _L0_ffn_in['b2'], 'L1_attn_W_in': _L1_attn_in['W_in'], 'L1_attn_conv_w': _L1_attn_in['conv_w'], 'L1_attn_conv_b': _L1_attn_in['conv_b'], 'L1_attn_W_xproj': _L1_attn_in['W_xproj'], 'L1_attn_A_log': _L1_attn_in['A_log'], 'L1_attn_D_param': _L1_attn_in['D_param'], 'L1_attn_W_out': _L1_attn_in['W_out'], 'L1_xattn_Wq': _L1_xattn_in['Wq'], 'L1_xattn_Wk': _L1_xattn_in['Wk'], 'L1_xattn_Wv': _L1_xattn_in['Wv'], 'L1_xattn_Wo': _L1_xattn_in['Wo'], 'L1_ffn_gate_w': _L1_ffn_in['gate_w'], 'L1_ffn_w1': _L1_ffn_in['w1'], 'L1_ffn_w2': _L1_ffn_in['w2']}

def reference(x, ctx_1024, L0_attn_r1_w, L0_attn_r1_b, L0_attn_ln_g, L0_attn_ln_b, L0_attn_r2_w, L0_attn_r2_b, L0_attn_temp, L0_attn_route_bias, L0_attn_W1, L0_attn_b1, L0_attn_W2, L0_attn_b2, L0_xattn_Wq, L0_xattn_bq, L0_xattn_Wk, L0_xattn_bk, L0_xattn_Wv, L0_xattn_bv, L0_xattn_Wo, L0_xattn_bo, L0_xattn_w1, L0_xattn_b1, L0_xattn_w2, L0_xattn_b2, L0_xattn_w3, L0_xattn_b3, L0_ffn_w1, L0_ffn_b1, L0_ffn_w2, L0_ffn_b2, L1_attn_W_in, L1_attn_conv_w, L1_attn_conv_b, L1_attn_W_xproj, L1_attn_A_log, L1_attn_D_param, L1_attn_W_out, L1_xattn_Wq, L1_xattn_Wk, L1_xattn_Wv, L1_xattn_Wo, L1_ffn_gate_w, L1_ffn_w1, L1_ffn_w2):
    import jax
    import jax.numpy as jnp

    def _L0_attn_ref(x, r1_w, r1_b, ln_g, ln_b, r2_w, r2_b, temp, route_bias, W1, b1, W2, b2):
        import jax, jax.numpy as jnp
        import numpy as np
        B, L, D = (4, 256, 128)
        E, F, H = (6, 192, 64)
        TOP_K = 2
        LN_EPS = 1e-05
        b, l, d = x.shape
        xf = x.reshape(-1, d)
        n = xf.shape[0]
        h = xf @ r1_w + r1_b
        mu = jnp.mean(h, axis=-1, keepdims=True)
        var = jnp.mean((h - mu) ** 2, axis=-1, keepdims=True)
        h = (h - mu) * jax.lax.rsqrt(var + LN_EPS) * ln_g + ln_b
        h = jax.nn.gelu(h, approximate=False)
        logits = (h @ r2_w + r2_b) / temp + route_bias
        p = jax.nn.softmax(logits, axis=-1)
        top_v, top_i = jax.lax.top_k(p, TOP_K)
        probs = jnp.zeros_like(p).at[jnp.arange(n)[:, None], top_i].set(top_v)
        hh = jnp.einsum('nd,edf->enf', xf, W1) + b1[:, None, :]
        even = (jnp.arange(W1.shape[0]) % 2 == 0)[:, None, None]
        act = jnp.where(even, jax.nn.gelu(hh, approximate=False), jax.nn.silu(hh))
        eo = jnp.einsum('enf,efd->end', act, W2) + b2[:, None, :]
        out = jnp.einsum('ne,end->nd', probs, eo)
        return out.reshape(b, l, d)

    def _L0_xattn_ref(query, key, value, Wq, bq, Wk, bk, Wv, bv, Wo, bo, w1, b1, w2, b2, w3, b3):
        import jax, jax.numpy as jnp
        import numpy as np
        import math
        B, S, D, H = (1, 256, 128, 16)
        DK = D // H
        DH = 64
        LOG_T_MIN = math.log(0.1)
        LOG_T_MAX = math.log(10.0)

        def _linear(x, W, b):
            return x @ W.T + b
        b, sq, d = query.shape
        sk = key.shape[1]
        h, dk = (H, DK)
        Q = _linear(query, Wq, bq).reshape(b, sq, h, dk).transpose(0, 2, 1, 3)
        K = _linear(key, Wk, bk).reshape(b, sk, h, dk).transpose(0, 2, 1, 3)
        V = _linear(value, Wv, bv).reshape(b, sk, h, dk).transpose(0, 2, 1, 3)
        qk = jnp.einsum('bhqd,bhkd->bhqk', Q, K)
        scores = qk / math.sqrt(dk)
        mean_sim = scores.mean(axis=(-2, -1))
        max_sim = scores.max(axis=-1).mean(axis=-1)
        probs = jax.nn.softmax(scores, axis=-1)
        entropy_proxy = jnp.var(probs, axis=-1, ddof=1).mean(axis=-1)
        feats = jnp.stack([mean_sim, max_sim, entropy_proxy], axis=-1)
        hidden = jax.nn.gelu(_linear(feats, w1, b1), approximate=False)
        hidden = jax.nn.gelu(_linear(hidden, w2, b2), approximate=False)
        log_t = jnp.clip(_linear(hidden, w3, b3), LOG_T_MIN, LOG_T_MAX)
        t = jnp.exp(log_t)[..., None]
        attn_scores = qk / (2.0 * t)
        attn = jax.nn.softmax(attn_scores, axis=-1)
        attn = jnp.nan_to_num(attn, nan=0.0)
        out = jnp.einsum('bhqk,bhkd->bhqd', attn, V)
        out = out.transpose(0, 2, 1, 3).reshape(b, sq, d)
        return _linear(out, Wo, bo)

    def _L0_ffn_ref(x, w1, b1, w2, b2):
        import jax, jax.numpy as jnp
        import numpy as np

        def fixed_quant(x, width, frac_width):
            scale = jnp.float32(2.0 ** frac_width)
            imax = jnp.float32(2 ** (width - 1) - 1)
            imin = jnp.float32(-2 ** (width - 1))
            return jnp.clip(jnp.round(x * scale), imin, imax) / scale
        IN_F, HID_F, OUT_F = (128, 512, 128)
        B, S = (4, 256)
        ACT_Q = (8, 4)
        W_Q = (8, 6)
        BIAS_Q = (8, 6)

        def quantized_linear(x, w, b):
            xq = fixed_quant(x, *ACT_Q)
            wq = fixed_quant(w, *W_Q)
            bq = fixed_quant(b, *BIAS_Q)
            return jnp.einsum('bsi,oi->bso', xq, wq) + bq

        def quantized_relu(x):
            return jax.nn.relu(fixed_quant(x, *ACT_Q))
        h = quantized_linear(x, w1, b1)
        h = quantized_relu(h)
        out = quantized_linear(h, w2, b2)
        return out

    def _L1_attn_ref(x, W_in, conv_w, conv_b, W_xproj, A_log, D_param, W_out):
        import jax, jax.numpy as jnp
        import numpy as np
        D_MODEL = 128
        D_STATE = 16
        D_CONV = 4
        EXPAND = 2
        D_INNER = EXPAND * D_MODEL
        DT_MIN, DT_MAX = (0.001, 0.1)
        BATCH, SEQ = (4, 256)

        def _silu(v):
            return v * jax.nn.sigmoid(v)
        b, l, d = x.shape
        xz = x @ W_in.T
        x_proj, z = jnp.split(xz, 2, axis=-1)
        xp = jnp.pad(x_proj, ((0, 0), (D_CONV - 1, 0), (0, 0)))
        x_conv = conv_b + sum((xp[:, k:k + l, :] * conv_w[:, k] for k in range(D_CONV)))
        x_conv = _silu(x_conv)
        x_dbl = x_conv @ W_xproj.T
        Bmat = x_dbl[..., :D_STATE]
        Cmat = x_dbl[..., D_STATE:2 * D_STATE]
        dt = jnp.clip(jax.nn.softplus(x_dbl[..., -1]), DT_MIN, DT_MAX)
        A = -jnp.exp(A_log)

        def step(h, inp):
            x_t, dt_t, B_t, C_t = inp
            dt_A = jnp.clip(dt_t[:, None] * A, -20.0, 0.0)
            A_bar = jnp.exp(dt_A)[:, None, :]
            B_bar = jnp.clip(dt_t[:, None] * B_t, -10.0, 10.0)[:, None, :]
            h = jnp.clip(A_bar * h + B_bar * x_t[:, :, None], -100.0, 100.0)
            y_t = jnp.einsum('bds,bs->bd', h, C_t)
            return (h, y_t)
        h0 = jnp.zeros((b, D_INNER, D_STATE), x.dtype)
        xs = (jnp.swapaxes(x_conv, 0, 1), jnp.swapaxes(dt, 0, 1), jnp.swapaxes(Bmat, 0, 1), jnp.swapaxes(Cmat, 0, 1))
        _, ys = jax.lax.scan(step, h0, xs)
        y = jnp.swapaxes(ys, 0, 1)
        y = y * _silu(z) + x_conv * D_param
        return y @ W_out.T

    def _L1_xattn_ref(query_input, key_input, value_input, Wq, Wk, Wv, Wo):
        import jax, jax.numpy as jnp
        import numpy as np
        q = jnp.einsum('bsd,dhk->bshk', query_input, Wq)
        k = jnp.einsum('bsd,dhk->bshk', key_input, Wk)
        v = jnp.einsum('bsd,dhk->bshk', value_input, Wv)
        depth = Wq.shape[-1]
        q = q * depth ** (-0.5)
        logits = jnp.einsum('bthk,bfhk->bhft', k, q)
        weights = jax.nn.softmax(logits, axis=-1)
        ctx = jnp.einsum('bhft,bthk->bfhk', weights, v)
        return jnp.einsum('bfhk,hkd->bfd', ctx, Wo)

    def _L1_ffn_ref(x, gate_w, w1, w2):
        import jax, jax.numpy as jnp
        import numpy as np
        import math
        D_MODEL = 128
        N_EXPERTS = 16
        D_FF = 512
        CAP_FACTOR = 1.25
        MIN_CAPACITY = 4

        def _capacity(num_tokens, num_experts):
            cap = math.floor(CAP_FACTOR * num_tokens / num_experts)
            cap += cap % 2
            return max(cap, MIN_CAPACITY)

        def _top1_router(gate_logits, capacity):
            s, e = gate_logits.shape
            probs = jax.nn.softmax(gate_logits, axis=-1)
            top1 = jnp.argmax(gate_logits, axis=-1)
            mask = jax.nn.one_hot(top1, e, dtype=jnp.int32)
            ranks = jnp.cumsum(mask, axis=0) - 1
            mask = mask * (ranks < capacity).astype(jnp.int32)
            rank1 = jnp.sum(mask * ranks, axis=-1)
            ranks_oh = jax.nn.one_hot(rank1, capacity, dtype=probs.dtype)
            weight = mask.astype(probs.dtype) * probs
            combine_weights = weight[:, :, None] * ranks_oh[:, None, :]
            sec_mask = combine_weights > 0
            return (combine_weights, sec_mask)
        tokens = x.reshape(-1, D_MODEL)
        s = tokens.shape[0]
        capacity = _capacity(s, N_EXPERTS)
        gate_logits = tokens.astype(jnp.float32) @ gate_w.T
        combine_weights, sec_mask = _top1_router(gate_logits, capacity)
        dispatch = jnp.einsum('sec,sd->ecd', sec_mask.astype(tokens.dtype), tokens)
        h = jax.nn.gelu(jnp.einsum('ecd,edf->ecf', dispatch, w1))
        expert_out = jnp.einsum('ecf,efd->ecd', h, w2)
        out = jnp.einsum('sec,ecd->sd', combine_weights.astype(tokens.dtype), expert_out)
        return out.reshape(x.shape)
    x = x + _L0_attn_ref(_layernorm(x, axis=-1), L0_attn_r1_w, L0_attn_r1_b, L0_attn_ln_g, L0_attn_ln_b, L0_attn_r2_w, L0_attn_r2_b, L0_attn_temp, L0_attn_route_bias, L0_attn_W1, L0_attn_b1, L0_attn_W2, L0_attn_b2)
    x = x + _L0_xattn_ref(_layernorm(x, axis=-1), ctx_1024, ctx_1024, L0_xattn_Wq, L0_xattn_bq, L0_xattn_Wk, L0_xattn_bk, L0_xattn_Wv, L0_xattn_bv, L0_xattn_Wo, L0_xattn_bo, L0_xattn_w1, L0_xattn_b1, L0_xattn_w2, L0_xattn_b2, L0_xattn_w3, L0_xattn_b3)
    x = x + _L0_ffn_ref(_layernorm(x, axis=-1), L0_ffn_w1, L0_ffn_b1, L0_ffn_w2, L0_ffn_b2)
    x = x + _L1_attn_ref(_layernorm(x, axis=-1), L1_attn_W_in, L1_attn_conv_w, L1_attn_conv_b, L1_attn_W_xproj, L1_attn_A_log, L1_attn_D_param, L1_attn_W_out)
    x = x + _L1_xattn_ref(_layernorm(x, axis=-1), ctx_1024, ctx_1024, L1_xattn_Wq, L1_xattn_Wk, L1_xattn_Wv, L1_xattn_Wo)
    x = x + _L1_ffn_ref(_layernorm(x, axis=-1), L1_ffn_gate_w, L1_ffn_w1, L1_ffn_w2)
    return x

_drawn_inputs = setup_inputs


def setup_inputs(seed=0):
    import zlib

    import numpy as np

    out = dict(_drawn_inputs(seed))
    spreads = {'L0_attn_r1_b': (0.0, 0.1),
     'L0_attn_ln_g': (1.0, 0.2),
     'L0_attn_ln_b': (0.0, 0.1),
     'L0_attn_r2_b': (0.0, 0.1),
     'L0_attn_route_bias': (0.0, 0.1),
     'L0_attn_b1': (0.0, 0.1),
     'L0_attn_b2': (0.0, 0.1),
     'L1_attn_conv_b': (0.0, 0.1),
     'L1_attn_D_param': (1.0, 0.2)}
    factors = {'L0_xattn_Wq': 6.886,
     'L0_xattn_bq': 8.0,
     'L0_xattn_Wk': 6.684,
     'L0_xattn_bk': 8.0,
     'L0_xattn_bv': 4.014,
     'L0_xattn_w1': 8.0,
     'L0_xattn_b1': 8.0,
     'L0_xattn_w2': 8.0,
     'L0_xattn_b2': 8.0,
     'L0_xattn_w3': 8.0,
     'L1_xattn_Wq': 8.0,
     'L1_xattn_Wk': 8.0}
    for name, (base, spread) in spreads.items():
        noise = np.random.default_rng([zlib.crc32(name.encode()), seed]).standard_normal(out[name].shape)
        drawn = base * np.exp(spread * noise) if base else spread * noise
        out[name] = jnp.asarray(drawn.astype(out[name].dtype))
    for name, factor in factors.items():
        out[name] = (out[name] * factor).astype(out[name].dtype)
    return out
```

```python
from contextlib import ExitStack

import concourse.bass as bass
from concourse import mybir
import numpy as np

F32 = mybir.dt.float32
BF16 = mybir.dt.bfloat16
I32 = mybir.dt.int32
ALU = mybir.AluOpType
ACT = mybir.ActivationFunctionType
AX = mybir.AxisListType.X

B, T, D = 8, 128, 128
N = B * T
HALF = N // 2
HB = B // 2
EPS = 1e-5

E0, F0, R0 = 6, 192, 64
C0 = E0 * F0 // 128
MIXED = C0 // 2
ORDER = [0, 2, 4, 1, 3, 5]

H1, K1 = 16, 8
M1 = 64
SC1 = float(K1) ** -0.5
FQ = 512
QC = FQ // 128
ROUND = 12582912.0

DI, NS = 256, 16
DC = DI // 128
DT_MIN, DT_MAX = 0.001, 0.1
LOOK = 4
STEPS = 8

H2, K2 = 16, 64
SC2 = float(K2) ** -0.5
HT = H2 * K2 // 128

E2, F2, CAP = 16, 512, 80
FC = F2 // 128
SLOTS = E2 * CAP

LOG_T_MIN, LOG_T_MAX = float(np.log(0.1)), float(np.log(10.0))

CONSTS = [("ident", 128), ("head", H1), ("batch", B), ("tri", 128), ("prio6", E0), ("prio16", E2),
          ("ebase", E2), ("select", C0 * 128), ("iota", SLOTS)]
COLS = [("r1_b", 1), ("ln_g", 1), ("ln_b", 1), ("b1", C0), ("bq", 1), ("bk", 1), ("bo", 1), ("m1", 1),
        ("m2", 1), ("fb1", QC), ("fb2", 1), ("conv_w", 4 * DC), ("conv_b", DC), ("dskip", DC), ("alog", 1)]
ROWS = [("r2_b", E0), ("route", E0), ("temp", 1), ("bv", D), ("b3", 1)]
WA = [("r1_w", R0), ("r2_w", E0), ("W1", C0 * 128), ("W2", C0 * 128), ("b2", D)]
WB = [("Wq", D), ("Wk", D), ("Wv", D), ("Wo", D), ("mw1", M1), ("mw2", M1), ("mw3", 128)]
WC = [("fw1", FQ), ("fw2", QC * 128)]
WD = [("Win", 2 * DI), ("Wx", DC * 80), ("Wout", DC * 128)]
WE = [("Xq", H2 * K2), ("Xk", H2 * K2), ("Xv", H2 * K2), ("Xo", HT * 128)]
WF = [("gate", E2)]
PACKS = {"consts": CONSTS, "small": COLS + ROWS, "wa": WA, "wb": WB, "wc": WC, "wd": WD, "we": WE, "wf": WF}


FB_AT = sum(n for _, n in COLS[:[k for k, _ in COLS].index("fb1")])


def width(pack):
    return sum(n for _, n in PACKS[pack])


def program(nc, d, out, stop):
    with ExitStack() as ctx:
        def sb(name, shape, dt=F32):
            return ctx.enter_context(nc.sbuf_tensor(name, shape, dt))

        sems = {}

        def sem(name):
            if name not in sems:
                sems[name] = ctx.enter_context(nc.semaphore(name))
            return sems[name]

        P = ctx.enter_context(nc.psum_tensor("P", [128, 8, 512], F32))

        arena1 = sb("arena1", [128, 16640])
        arena2 = sb("arena2", [128, 16384])
        packs = {k: sb("pack_" + k, [128, width(k)]) for k in ("consts", "small", "wa", "wb", "wc", "wd", "wf")}
        if stop >= 5:
            pass

        def w(pack, name, rows=128):
            at = 0
            for n, k in PACKS[pack]:
                if n == name:
                    return packs[pack][0:rows, at:at + k]
                at += k
            raise KeyError(name)

        def c(name, rows=128):
            return w("consts", name, rows)

        def col(name, rows=128):
            return w("small", name, rows)

        ident = c("ident")
        mean128 = sb("mean128", [128, 128])
        mean64 = sb("mean64", [R0, R0])
        eps = sb("eps", [128, 1])
        xT = sb("xT", [128, N])
        xn = sb("xn", [128, N])
        lnbuf = sb("lnbuf", [128, 2 * N])
        xc = lnbuf[:, 0:N]
        sq = lnbuf[:, N:2 * N]
        ctxT = sb("ctxT", [128, N])

        def half(t, h):
            return t[:, h * HALF:(h + 1) * HALF]

        def heads(t, k, n):
            return t.rearrange("p (k n) -> p k n", k=k)

        at1 = [0]

        def a1(n, dt=F32):
            t = arena1[:, at1[0]:at1[0] + n]
            at1[0] += n
            return t
        xtok = a1(N)
        ctok = a1(N)
        rh = a1(N)[0:R0, :]
        rc = a1(N)[0:R0, :]
        rs = a1(N)[0:R0, :]
        rg = a1(N)[0:R0, :]
        lg = [heads(a1(B * E0), B, E0) for _ in range(12)]
        red = [a1(B).unsqueeze(2) for _ in range(6)]
        rtemp = a1(1)
        probsT = a1(N)[0:E0, :]
        act0 = [a1(HALF) for _ in range(3)]
        wact0 = [a1(HALF) for _ in range(3)]
        W1 = heads(w("wa", "W1"), C0, 128)
        W2 = heads(w("wa", "W2"), C0, 128)
        SEL = heads(c("select", E0), C0, 128)

        Kexp = arena2[:, :]
        Dall = arena1[:, 0:16384]
        kT1 = sb("kT1", [128, N])
        qT1 = sb("qT1", [128, N])
        V1 = sb("V1", [128, B * H1 * (K1 + 1)])
        qs1 = [sb(f"qs1_{j}", [128, T]) for j in range(2)]
        HTK = H1 * T
        exp1 = [packs["wa"][:, 0:HTK], lnbuf[:, :]]
        st1 = [sb(f"st1_{j}", [128, H1, 6]) for j in range(2)]
        BH = B * H1
        stats1 = sb("stats1", [128, BH, 6])
        max1 = sb("max1", [128, BH])
        smax1 = [sb(f"smax1_{j}", [128, H1]) for j in range(2)]
        wts1 = [arena2[:, j * HTK:(j + 1) * HTK] for j in range(2)]
        wtT1 = [arena2[:, (2 + j) * HTK:(3 + j) * HTK] for j in range(2)]
        at2 = [4 * HTK]

        def a2(n):
            t = arena2[:, at2[0]:at2[0] + n]
            at2[0] += n
            return t
        tmp1 = [a2(BH) for _ in range(6)]
        ent1 = a2(BH)
        simrow1 = a2(BH)
        qsum1, ksum1, sim1 = a2(B), a2(B), a2(B)
        featw = a2(9).rearrange("p (f m) -> p f m", f=3)
        feats1, hid1, hid2 = a2(BH)[0:3, :], a2(BH)[0:M1, :], a2(BH)[0:M1, :]
        logt1, temper1, cool1 = a2(BH), a2(BH), a2(BH)
        rz1 = [a2(H1) for _ in range(2)]
        raw1 = [a2(D) for _ in range(2)]
        same1 = [a2(D).bitcast(I32) for _ in range(2)]
        o1 = [a2(D) for _ in range(2)]
        oT1 = a2(N)

        fw1q = sb("fw1q", [128, FQ], BF16)
        fw2q = sb("fw2q", [128, QC * 128], BF16)
        fbq = sb("fbq", [128, QC + 1])
        ftmp = [sb(f"ftmp{k}", [128, FQ]) for k in range(2)]
        xq = arena1[:, 0:N // 2].bitcast(BF16)
        xr = arena1[:, N:2 * N]
        hraw = [arena1[:, (4 + u) * HALF:(5 + u) * HALF] for u in range(2)]
        hclip = [arena1[:, (6 + u) * HALF:(7 + u) * HALF] for u in range(2)]
        hq = arena1[:, 8 * HALF:12 * HALF].bitcast(BF16).rearrange("p (u n) -> p u n", u=2 * QC)
        yq = arena1[:, 12 * HALF:14 * HALF]

        at3 = [0]

        def a3(n, cols=None):
            t = arena2[:, at3[0]:at3[0] + n]
            at3[0] += n
            return t
        PADT = T + 3
        xpad = a3(DC * B * PADT).rearrange("p (c b t) -> p c b t", c=DC, b=B)
        conv = [a3(DC * N).rearrange("p (c b t) -> p c b t", c=DC, b=B) for _ in range(2)]
        xcv = a3(DC * N)
        sz = a3(DC * N)
        dbl = a3(N)[0:80, :]
        Bst, Cst, dtst = a3(T), a3(T), a3(T)
        dstep = [a3(T) for _ in range(4)]
        Abar, Bbar = a3(T), a3(T)
        negA = a3(1)
        Cm = a3(T * B)
        xe3 = [a3(DI) for _ in range(LOOK)]
        U3 = [a3(DI) for _ in range(4)]
        hraw3 = [a3(DI) for _ in range(2)]
        h3 = [arena1[:, 15360 + k * DI:15360 + (k + 1) * DI] for k in range(4)]
        yT3 = arena1[:, 9216:9216 + DC * N]
        yg3 = [arena1[:, 11264 + k * DC * N:11264 + (k + 1) * DC * N] for k in range(2)]
        scratch = nc.dram_tensor("states_scratch", (80, N), F32, kind="Internal").ap()

        kT4 = arena1[:, 0:HT * N].rearrange("p (m n) -> p m n", m=HT)
        VW = H2 * (K2 + 1)
        V4 = arena1[:, HT * N:HT * N + B * VW]
        we = arena2[:, 0:width("we")]
        Xq, Xk, Xv, Xo = (we[:, k * 1024:(k + 1) * 1024] for k in range(4))
        at4 = [width("we")]

        def a4(n):
            t = arena2[:, at4[0]:at4[0] + n]
            at4[0] += n
            return t
        q4 = [lnbuf[:, j * N:(j + 1) * N] for j in range(2)]
        ks4 = [kT1, qT1]
        wts4 = [a4(H2 * T) for _ in range(2)]
        wtT4 = [a4(H2 * T) for _ in range(2)]
        o4 = [a4(H2 * K2) for _ in range(2)]
        oT4 = [a4(H2 * K2) for _ in range(2)]
        smax4 = [sb(f"smax4_{j}", [128, H2]) for j in range(2)]
        rz4 = [sb(f"rz4_{j}", [128, H2]) for j in range(2)]

        RW = 8
        wring = heads(arena1[:, 0:RW * 1024], RW, 1024)
        w1r = [arena1[:, k * 1024:k * 1024 + F2] for k in range(RW)]
        w2r = [arena1[:, k * 1024 + F2:(k + 1) * 1024] for k in range(RW)]
        at5 = [RW * 1024]

        def a5(n):
            t = arena1[:, at5[0]:at5[0] + n]
            at5[0] += n
            return t
        g5 = [heads(a5(B * E2), B, E2) for _ in range(8)]
        v5 = [a5(B) for _ in range(8)]
        idx5 = a5(B).bitcast(mybir.dt.uint32)
        zero5 = a5(128)
        xrest = [arena2[:, k * N:(k + 1) * N] for k in range(2)]
        xpart = arena2[:, 2 * N:2 * N + 3 * N // 2].bitcast(BF16)
        hot5 = [arena2[:, 4096 + k * SLOTS // 2:4096 + (k + 1) * SLOTS // 2].bitcast(BF16) for k in range(4)]
        dT5 = arena2[:, 7168:7168 + SLOTS]
        hT5 = [arena2[:, 8704 + k * FC * CAP:8704 + (k + 1) * FC * CAP] for k in range(2)]
        eo5 = arena2[0:CAP, 10240:10240 + E2 * D].rearrange("p (e d) -> p e d", e=E2)
        yg5 = arena2[:, 12288:12288 + N]
        final = arena2[:, 13312:13312 + N]
        slots_dram = nc.dram_tensor("slots_scratch", (SLOTS + 1, D), F32, kind="Internal").ap()

        block = ctx.enter_context(nc.Block())

        def pe_norm(pe, k):
            for h in range(2):
                pe.wait_ge(sem("x_ready"), 2 * k + h + 1)
                nc.tensor.matmul(P[:, 4 + h, :], mean128[:, :], half(xT, h), start=True, stop=True)\
                    .then_inc(sem("ln_mean"), 1)
            for h in range(2):
                pe.wait_ge(sem("ln_squared"), 2 * k + h + 1)
                nc.tensor.matmul(P[:, 6 + h, :], mean128[:, :], half(sq, h), start=True, stop=True)\
                    .then_inc(sem("ln_var"), 1)

        def act_norm(act, k):
            for h in range(2):
                act.wait_ge(sem("ln_centred"), 2 * k + h + 1)
                nc.scalar.activation(half(sq, h), half(xc, h), ACT.Square).then_inc(sem("ln_squared"), 1)
            for h in range(2):
                act.wait_ge(sem("ln_var"), 2 * k + h + 1)
                nc.scalar.activation(half(sq, h), P[:, 6 + h, :], ACT.Sqrt, bias=eps[:, :])\
                    .then_inc(sem("ln_std"), 1)

        def dve_norm(dve, k):
            for h in range(2):
                dve.wait_ge(sem("ln_mean"), 2 * k + h + 1)
                nc.vector.tensor_tensor(half(xc, h), half(xT, h), P[:, 4 + h, :], ALU.subtract)\
                    .then_inc(sem("ln_centred"), 1)
            for h in range(2):
                dve.wait_ge(sem("ln_std"), 2 * k + h + 1)
                nc.vector.reciprocal(half(sq, h), half(sq, h)).then_inc(sem("ln_rstd"), 1)
                dve.wait_ge(sem("ln_rstd"), 2 * k + h + 1)
                nc.vector.tensor_tensor(half(xn, h), half(xc, h), half(sq, h), ALU.mult)\
                    .then_inc(sem("xn_ready"), 1)

        steps = [0]

        def chain(dve, ins):
            steps[0] += 1
            ins.then_inc(sem("dve_step"), 1)
            dve.wait_ge(sem("dve_step"), steps[0])

        UNITS = [(cc, h) for cc in range(C0) for h in range(2)]

        def pe_stage0(pe):
            pe_norm(pe, 0)
            pe.wait_ge(sem("wa_loaded"), 16)
            for h in range(2):
                pe.wait_ge(sem("xn_ready"), h + 1)
                nc.tensor.matmul(P[0:R0, h, :], w("wa", "r1_w"), half(xn, h), start=True, stop=True)\
                    .then_inc(sem("r_hidden"), 1)
            for h in range(2):
                pe.wait_ge(sem("r_biased"), h + 1)
                nc.tensor.matmul(P[0:R0, 2 + h, :], mean64[:, :], half(rh, h), start=True, stop=True)\
                    .then_inc(sem("r_mean"), 1)
            for h in range(2):
                pe.wait_ge(sem("r_squared"), h + 1)
                nc.tensor.matmul(P[0:R0, 4 + h, :], mean64[:, :], half(rs, h), start=True, stop=True)\
                    .then_inc(sem("r_var"), 1)
            LGT = heads(P[:, 0, 0:B * E0], B, E0)
            for b in range(B):
                if b % HB == 0:
                    pe.wait_ge(sem("r_act"), b // HB + 1)
                mm = nc.tensor.matmul(LGT[:, b, :], rg[:, b * T:(b + 1) * T], w("wa", "r2_w", R0),
                                      start=True, stop=True)
            mm.then_inc(sem("logits"), 1)
            pe.wait_ge(sem("probs"), 1)
            for b in range(B):
                mm = nc.tensor.transpose(P[0:E0, 2 + b // HB, (b % HB) * T:(b % HB + 1) * T], lg[11][:, b, :], ident)
                if b % HB == HB - 1:
                    mm.then_inc(sem("probs_turned"), 1)

            def down(u):
                cc, h = UNITS[u]
                pe.wait_ge(sem("e_weighted"), u + 1)
                nc.tensor.matmul(P[:, 6 + h, :], W2[:, cc, :], wact0[u % 3], start=(cc == 0), stop=False)\
                    .then_inc(sem("e_used"), 1)
            for u, (cc, h) in enumerate(UNITS):
                if u == 0:
                    pe.wait_ge(sem("probs_copied"), 2)
                if u >= 3:
                    pe.wait_ge(sem("e_act"), u - 2)
                nc.tensor.matmul(P[:, u % 3, :], W1[:, cc, :], half(xn, h), start=True, stop=True)\
                    .then_inc(sem("e_hidden"), 1)
                if u >= 3:
                    pe.wait_ge(sem("e_weighted"), u - 2)
                nc.tensor.matmul(P[:, 3 + u % 3, :], SEL[:, cc, :], half(probsT, h), start=True, stop=True)\
                    .then_inc(sem("e_prob"), 1)
                if u >= 2:
                    down(u - 2)
            down(len(UNITS) - 2)
            down(len(UNITS) - 1)
            for h in range(2):
                nc.tensor.matmul(P[:, 6 + h, :], w("wa", "b2", E0), half(probsT, h), start=False, stop=True)\
                    .then_inc(sem("stage_out"), 1)

        def act_stage0(act):
            act_norm(act, 0)
            for h in range(2):
                act.wait_ge(sem("r_hidden"), h + 1)
                nc.scalar.activation(half(rh, h), P[0:R0, h, :], ACT.Identity, bias=col("r1_b", R0))\
                    .then_inc(sem("r_biased"), 1)
            for h in range(2):
                act.wait_ge(sem("r_centred"), h + 1)
                nc.scalar.activation(half(rs, h), half(rc, h), ACT.Square).then_inc(sem("r_squared"), 1)
            for h in range(2):
                act.wait_ge(sem("r_var"), h + 1)
                nc.scalar.activation(half(rs, h), P[0:R0, 4 + h, :], ACT.Sqrt, bias=eps[0:R0, :])\
                    .then_inc(sem("r_std"), 1)
            for h in range(2):
                act.wait_ge(sem("r_normed"), h + 1)
                nc.scalar.activation(half(rg, h), half(rg, h), ACT.Gelu, bias=col("ln_b", R0),
                                     scale=col("ln_g", R0)).then_inc(sem("r_act"), 1)
            act.wait_ge(sem("route_shift"), 1)
            nc.scalar.activation(lg[3], lg[2], ACT.Exp).then_inc(sem("route_exp"), 1)
            for h in range(2):
                act.wait_ge(sem("probs_turned"), h + 1)
                nc.scalar.copy(half(probsT, h), P[0:E0, 2 + h, :]).then_inc(sem("probs_copied"), 1)

            def unit(u, fn, lo, hi, last=True):
                cc, h = UNITS[u]
                ins = nc.scalar.activation(act0[u % 3][lo:hi, :], P[lo:hi, u % 3, :], fn,
                                           bias=col("b1")[lo:hi, cc:cc + 1])
                if last:
                    ins.then_inc(sem("e_act"), 1)
            for u, (cc, h) in enumerate(UNITS):
                if cc == MIXED and h == 1:
                    continue
                act.wait_ge(sem("e_hidden"), u + 1 + (cc == MIXED))
                if u >= 3:
                    act.wait_ge(sem("e_weighted"), u - 2 + (cc == MIXED))
                if cc == MIXED:
                    unit(u, ACT.Gelu, 0, 64, False)
                    unit(u + 1, ACT.Gelu, 0, 64, False)
                    unit(u, ACT.Silu, 64, 128)
                    unit(u + 1, ACT.Silu, 64, 128)
                else:
                    unit(u, ACT.Gelu if cc < MIXED else ACT.Silu, 0, 128)

        def dve_stage0(dve):
            dve_norm(dve, 0)
            for h in range(2):
                dve.wait_ge(sem("r_mean"), h + 1)
                nc.vector.tensor_tensor(half(rc, h), half(rh, h), P[0:R0, 2 + h, :], ALU.subtract)\
                    .then_inc(sem("r_centred"), 1)
            for h in range(2):
                dve.wait_ge(sem("r_std"), h + 1)
                nc.vector.reciprocal(half(rs, h), half(rs, h)).then_inc(sem("r_rstd"), 1)
                dve.wait_ge(sem("r_rstd"), h + 1)
                nc.vector.tensor_tensor(half(rg, h), half(rc, h), half(rs, h), ALU.mult)\
                    .then_inc(sem("r_normed"), 1)
            LGT = heads(P[:, 0, 0:B * E0], B, E0)

            def row(name):
                return col(name).unsqueeze(1).broadcast_to([128, B, E0])

            def per_token(i):
                return red[i].broadcast_to([128, B, E0])
            prio = c("prio6").unsqueeze(1).broadcast_to([128, B, E0])
            chain(dve, nc.vector.reciprocal(rtemp, col("temp")))
            dve.wait_ge(sem("logits"), 1)
            chain(dve, nc.vector.tensor_tensor(lg[0], LGT, row("r2_b"), ALU.add))
            chain(dve, nc.vector.scalar_tensor_tensor(lg[1], lg[0], rtemp, row("route"), ALU.mult, ALU.add))
            chain(dve, nc.vector.tensor_reduce(red[0], lg[1], AX, ALU.max))
            nc.vector.tensor_tensor(lg[2], lg[1], per_token(0), ALU.subtract).then_inc(sem("route_shift"), 1)
            dve.wait_ge(sem("route_exp"), 1)
            chain(dve, nc.vector.tensor_reduce(red[1], lg[3], AX, ALU.add))
            chain(dve, nc.vector.reciprocal(red[1], red[1]))
            chain(dve, nc.vector.tensor_tensor(lg[4], lg[3], per_token(1), ALU.mult))
            src = lg[4]
            for r in range(2):
                hit, mark, best = lg[5 + r], lg[7 + r], lg[9 + r]
                chain(dve, nc.vector.tensor_reduce(red[2 + r], src, AX, ALU.max))
                chain(dve, nc.vector.tensor_tensor(hit, src, per_token(2 + r), ALU.is_equal))
                chain(dve, nc.vector.tensor_tensor(mark, hit, prio, ALU.mult))
                chain(dve, nc.vector.tensor_reduce(red[4 + r], mark, AX, ALU.max))
                chain(dve, nc.vector.tensor_tensor(best, mark, per_token(4 + r), ALU.is_equal))
                if r == 0:
                    chain(dve, nc.vector.scalar_tensor_tensor(lg[2], best, -2.0, src, ALU.mult, ALU.add))
                    src = lg[2]
            chain(dve, nc.vector.tensor_tensor(lg[5], lg[9], lg[10], ALU.add))
            nc.vector.tensor_tensor(lg[11], lg[4], lg[5], ALU.mult).then_inc(sem("probs"), 1)
            for u, (cc, h) in enumerate(UNITS):
                dve.wait_ge(sem("e_act"), u + 1)
                dve.wait_ge(sem("e_prob"), u + 1)
                if u >= 3:
                    dve.wait_ge(sem("e_used"), u - 2)
                nc.vector.tensor_tensor(wact0[u % 3], act0[u % 3], P[:, 3 + u % 3, :], ALU.mult)\
                    .then_inc(sem("e_weighted"), 1)
            for h in range(2):
                dve.wait_ge(sem("stage_out"), h + 1)
                nc.vector.tensor_tensor(half(xT, h), half(xT, h), P[:, 6 + h, :], ALU.add)\
                    .then_inc(sem("x_ready"), 1)

        V1v = V1[:, :].rearrange("p (b h k) -> p b h k", b=B, h=H1)

        def pe_keys1(pe):
            pe.wait_ge(sem("wb_loaded"), 16)
            pe.wait_ge(sem("x_ready"), 2)
            for h in range(2):
                pe.wait_ge(sem("ctx_ready"), h + 1)
                nc.tensor.matmul(P[:, h, :], w("wb", "Wk"), half(ctxT, h), start=True, stop=True)\
                    .then_inc(sem("k1_made"), 1)
            for b in range(B):
                mm = nc.tensor.matmul(P[:, 2 + b // HB, (b % HB) * D:(b % HB + 1) * D],
                                      ctxT[:, b * T:(b + 1) * T], w("wb", "Wv"), start=True, stop=True)
            mm.then_inc(sem("v1_made"), 1)
            pe.wait_ge(sem("k1_ready"), 2)
            pe.wait_ge(sem("v1_ready"), 1)

        def act_keys1(act):
            for h in range(2):
                act.wait_ge(sem("k1_made"), h + 1)
                nc.scalar.activation(half(kT1, h), P[:, h, :], ACT.Identity, bias=col("bk"))\
                    .then_inc(sem("k1_ready"), 1)

        def dve_keys1(dve):
            nc.vector.memset(V1[:, :], 1.0).then_inc(sem("v1_ones"), 1)
            dve.wait_ge(sem("v1_made"), 1)
            dve.wait_ge(sem("v1_ones"), 1)
            for h in range(2):
                ins = nc.vector.tensor_tensor(
                    V1v[:, h * HB:(h + 1) * HB, :, 0:K1],
                    P[:, 2 + h, :].rearrange("p (b h k) -> p b h k", b=HB, h=H1),
                    heads(col("bv"), H1, K1).unsqueeze(1).broadcast_to([128, HB, H1, K1]), ALU.add)
            dve.drain().then_inc(sem("v1_ready"), 1)

        def pool_stage0(pool):
            pool.wait_ge(sem("consts_loaded"), 16)
            pool.wait_ge(sem("k1_ready"), 2)
            with pool.Fori(0, B) as b:
                nc.gpsimd.tensor_tensor(
                    heads(Kexp[:, bass.ds(b * HTK, HTK)], H1, T),
                    kT1[:, bass.ds(b * T, T)].unsqueeze(1).broadcast_to([128, H1, T]),
                    c("head").unsqueeze(2).broadcast_to([128, H1, T]), ALU.mult)
            pool.drain().then_inc(sem("k1_spread"), 1)

        def pool_stage1(pool):
            pool.wait_ge(sem("q1_ready"), 2)
            with pool.Fori(0, B // 2) as i:
                for j in range(2):
                    pool.wait_ge(sem("s1_scored"), 2 * i + j + 1)
                    nc.gpsimd.tensor_copy(qs1[j][:, :], qT1[:, bass.ds(2 * i * T + j * T, T)])\
                        .then_inc(sem("s1_staged"), 1)
            pool.wait_ge(sem("wc_loaded"), 16)
            n = 0
            for src, dst in ((w("wc", "fw1"), fw1q[:, :]), (w("wc", "fw2"), fw2q[:, :])):
                nc.gpsimd.tensor_scalar(ftmp[0][:, :], src, 64.0, 127.0, ALU.mult, ALU.min)\
                    .then_inc(sem("fw_step"), 1)
                pool.wait_ge(sem("fw_step"), n + 1)
                nc.gpsimd.tensor_scalar(ftmp[1][:, :], ftmp[0][:, :], -128.0, ROUND, ALU.max, ALU.add)\
                    .then_inc(sem("fw_step"), 1)
                pool.wait_ge(sem("fw_step"), n + 2)
                nc.gpsimd.tensor_scalar(dst, ftmp[1][:, :], ROUND, None, ALU.subtract).then_inc(sem("fw_step"), 1)
                pool.wait_ge(sem("fw_step"), n + 3)
                n += 3
            nb = QC + 1
            fb = packs["small"][:, FB_AT:FB_AT + nb]
            nc.gpsimd.tensor_scalar(ftmp[0][:, 0:nb], fb, 64.0, 127.0, ALU.mult, ALU.min).then_inc(sem("fw_step"), 1)
            pool.wait_ge(sem("fw_step"), n + 1)
            nc.gpsimd.tensor_scalar(ftmp[1][:, 0:nb], ftmp[0][:, 0:nb], -128.0, ROUND, ALU.max, ALU.add)\
                .then_inc(sem("fw_step"), 1)
            pool.wait_ge(sem("fw_step"), n + 2)
            nc.gpsimd.tensor_scalar(fbq[:, 0:QC], ftmp[1][:, 0:QC], ROUND, 16.0 / 64, ALU.subtract, ALU.mult)
            nc.gpsimd.tensor_scalar(fbq[:, QC:nb], ftmp[1][:, QC:nb], ROUND, 1.0 / 64, ALU.subtract, ALU.mult)
            pool.drain().then_inc(sem("fw_ready"), 1)

        RING = 2

        def pe_stage1(pe):
            pe_norm(pe, 1)
            for h in range(2):
                pe.wait_ge(sem("xn_ready"), 2 + h + 1)
                nc.tensor.matmul(P[:, h, :], w("wb", "Wq"), half(xn, h), start=True, stop=True)\
                    .then_inc(sem("q1_made"), 1)
            pe.sem_inc(sem("s1_scored"), RING)
            pe.wait_ge(sem("q1_ready"), 2)
            pe.wait_ge(sem("k1_spread"), 1)
            with pe.Fori(0, B // 2) as i:
                for j in range(2):
                    pe.wait_ge(sem("s1_staged"), 2 * i + j + 1)
                    pe.wait_ge(sem("s1_shifted"), 2 * i + j + 1)
                    for g in range(4):
                        mm = nc.tensor.matmul(P[:, 4 * j + g, :], qs1[j][:, :],
                                              Kexp[:, bass.ds(2 * i * HTK + j * HTK + g * 512, 512)],
                                              start=True, stop=True)
                    mm.then_inc(sem("s1_scored"), 1)
            pe.wait_ge(sem("s1_shifted"), B + RING)
            pe.wait_ge(sem("feat_rows"), 1)
            for f, row in enumerate((simrow1, max1[:, :], ent1)):
                mm = nc.tensor.matmul(P[0:3, 0, 0:BH], featw[:, f, :], row, start=(f == 0), stop=(f == 2))
            mm.then_inc(sem("feats"), 1)
            pe.wait_ge(sem("feats_copied"), 1)
            nc.tensor.matmul(P[0:M1, 1, 0:BH], w("wb", "mw1", 3), feats1, start=True, stop=True)\
                .then_inc(sem("mlp_made"), 1)
            pe.wait_ge(sem("mlp_act"), 1)
            nc.tensor.matmul(P[0:M1, 2, 0:BH], w("wb", "mw2", M1), hid1, start=True, stop=True)\
                .then_inc(sem("mlp_made"), 1)
            pe.wait_ge(sem("mlp_act"), 2)
            nc.tensor.matmul(P[:, 3, 0:BH], w("wb", "mw3", M1), hid2, start=True, stop=True)\
                .then_inc(sem("mlp_made"), 1)
            pe.wait_ge(sem("logt"), 1)
            pe.sem_inc(sem("s2_mixed"), RING)
            with pe.Fori(0, B // 2) as i:
                for j in range(2):
                    pe.wait_ge(sem("s2_exp"), 2 * i + j + 1)
                    for g in range(4):
                        freed = sem("s2_evac_a") if g % 2 == 0 else sem("s2_evac_d")
                        pe.wait_ge(freed, 4 * i + 2 * j + g // 2 + 1)
                        for k in range(4):
                            h = 4 * g + k
                            mm = nc.tensor.transpose(P[:, g, k * T:(k + 1) * T], wts1[j][:, h * T:(h + 1) * T], ident)
                        mm.then_inc(sem("s2_turned"), 1)
                for j in range(2):
                    pe.wait_ge(sem("s2_evac_a"), 4 * i + 2 * j + 2 + 2)
                    pe.wait_ge(sem("s2_evac_d"), 4 * i + 2 * j + 2 + 2)
                    pe.wait_ge(sem("s2_normed"), 2 * i + j + 1)
                    for h in range(H1):
                        mm = nc.tensor.matmul(P[:, 4 + j, h * (K1 + 1):(h + 1) * (K1 + 1)],
                                              wtT1[j][:, h * T:(h + 1) * T],
                                              V1[:, bass.ds(2 * i * H1 * 9 + j * H1 * 9 + h * 9, 9)],
                                              start=True, stop=True)
                    mm.then_inc(sem("s2_mixed"), 1)
                for j in range(2):
                    pe.wait_ge(sem("s2_normed"), 2 * i + j + 1 + RING)
                    pe.wait_ge(sem("s2_kept"), 2 * i + j + 1)
                    nc.tensor.transpose(P[:, 6 + j, 0:T], o1[j], ident).then_inc(sem("s2_oturned"), 1)
            for h in range(2):
                pe.wait_ge(sem("s2_kept"), RING + B)
                nc.tensor.matmul(P[:, h, :], w("wb", "Wo"), half(oT1, h), start=True, stop=True)\
                    .then_inc(sem("stage_out"), 1)

        def act_stage1(act):
            act_norm(act, 1)
            for h in range(2):
                act.wait_ge(sem("q1_made"), h + 1)
                nc.scalar.activation(half(qT1, h), P[:, h, :], ACT.Identity, bias=col("bq"))\
                    .then_inc(sem("q1_ready"), 1)
            with act.Fori(0, B // 2) as i:
                for j in range(2):
                    act.wait_ge(sem("s1_shifted"), 2 * i + j + 1 + RING)
                    act.wait_ge(sem("s1_stats"), 2 * i + j + 1)
                    nc.scalar.activation(exp1[j], Dall[:, bass.ds(2 * i * HTK + j * HTK, HTK)], ACT.Exp, scale=SC1)\
                        .then_inc(sem("s1_exp"), 1)
            act.wait_ge(sem("mlp_made"), 1)
            nc.scalar.activation(hid1, P[0:M1, 1, 0:BH], ACT.Gelu, bias=col("m1", M1)).then_inc(sem("mlp_act"), 1)
            act.wait_ge(sem("mlp_made"), 2)
            nc.scalar.activation(hid2, P[0:M1, 2, 0:BH], ACT.Gelu, bias=col("m2", M1)).then_inc(sem("mlp_act"), 1)
            act.wait_ge(sem("logt"), 1)
            nc.scalar.activation(temper1, logt1, ACT.Exp, scale=-1.0).then_inc(sem("temper"), 1)
            act.sem_inc(sem("s2_evac_a"), 2)
            act.sem_inc(sem("s2_kept"), RING)
            with act.Fori(0, B // 2) as i:
                for j in range(2):
                    act.wait_ge(sem("s2_scaled"), 2 * i + j + 1)
                    nc.scalar.activation(wts1[j], wts1[j], ACT.Exp).then_inc(sem("s2_exp"), 1)
                for j in range(2):
                    act.wait_ge(sem("s2_mixed"), 2 * i + j + 1)
                    for g in (0, 2):
                        act.wait_ge(sem("s2_turned"), 8 * i + 4 * j + g + 1)
                        nc.scalar.copy(wtT1[j][:, g * 512:(g + 1) * 512], P[:, g, :]).then_inc(sem("s2_evac_a"), 1)
                for j in range(2):
                    act.wait_ge(sem("s2_oturned"), 2 * i + j + 1)
                    nc.scalar.copy(oT1[:, bass.ds(2 * i * T + j * T, T)], P[:, 6 + j, 0:T]).then_inc(sem("s2_kept"), 1)

        def dve_stage1(dve):
            dve_norm(dve, 1)
            dve.sem_inc(sem("s1_shifted"), RING)
            dve.sem_inc(sem("s1_stats"), RING)
            with dve.Fori(0, B // 2) as i:
                for j in range(2):
                    dve.wait_ge(sem("s1_scored"), 2 * i + j + 1 + RING)
                    S = P[:, 4 * j:4 * j + 4, :].rearrange("p g (h k) -> p (g h) k", k=T)
                    nc.vector.tensor_reduce(smax1[j][:, :], S, AX, ALU.max).then_inc(sem("s1_max"), 1)
                    dve.wait_ge(sem("s1_max"), 2 * i + j + 1)
                    nc.vector.tensor_copy(max1[:, bass.ds(2 * i * H1 + j * H1, H1)], smax1[j][:, :])
                    nc.vector.tensor_tensor(heads(Dall[:, bass.ds(2 * i * HTK + j * HTK, HTK)], H1, T), S,
                                            smax1[j][:, :].unsqueeze(2).broadcast_to([128, H1, T]), ALU.subtract)\
                        .then_inc(sem("s1_shifted"), 1)
                for j in range(2):
                    dve.wait_ge(sem("s1_exp"), 2 * i + j + 1)
                    for h in range(H1):
                        bn = nc.vector.bn_stats(st1[j][:, h, :], exp1[j][:, h * T:(h + 1) * T])
                    bn.then_inc(sem("s1_bn"), 1)
                    dve.wait_ge(sem("s1_bn"), 2 * i + j + 1)
                    nc.vector.tensor_copy(stats1[:, bass.ds(2 * i * H1 + j * H1, H1), :], st1[j][:, :, :])\
                        .then_inc(sem("s1_stats"), 1)
            dve.wait_ge(sem("s1_stats"), B + RING)
            me, ve, mo, vo = stats1[:, :, 1], stats1[:, :, 2], stats1[:, :, 4], stats1[:, :, 5]
            chain(dve, nc.vector.tensor_tensor(tmp1[0], me, mo, ALU.subtract))
            chain(dve, nc.vector.tensor_tensor(tmp1[0], tmp1[0], tmp1[0], ALU.mult))
            chain(dve, nc.vector.tensor_tensor(tmp1[1], ve, vo, ALU.add))
            chain(dve, nc.vector.scalar_tensor_tensor(tmp1[2], tmp1[0], T / 4.0, tmp1[1], ALU.mult, ALU.add))
            chain(dve, nc.vector.tensor_tensor(tmp1[3], me, mo, ALU.add))
            chain(dve, nc.vector.reciprocal(tmp1[4], tmp1[3]))
            chain(dve, nc.vector.tensor_tensor(tmp1[5], tmp1[2], tmp1[4], ALU.mult))
            chain(dve, nc.vector.scalar_tensor_tensor(ent1, tmp1[5], 4.0 / T / T / (T - 1), tmp1[4], ALU.mult, ALU.mult))
            chain(dve, nc.vector.tensor_reduce(qsum1, heads(qT1[:, :], B, T), AX, ALU.add))
            chain(dve, nc.vector.tensor_reduce(ksum1, heads(kT1[:, :], B, T), AX, ALU.add))
            chain(dve, nc.vector.tensor_tensor(sim1, qsum1, ksum1, ALU.mult))
            chain(dve, nc.vector.tensor_tensor(heads(simrow1, B, H1), sim1.unsqueeze(2).broadcast_to([128, B, H1]),
                                          c("head").unsqueeze(1).broadcast_to([128, B, H1]), ALU.mult))
            chain(dve, nc.vector.memset(featw, 0.0))
            chain(dve, nc.vector.memset(featw[:, 0, 0:1], SC1 / T / T))
            chain(dve, nc.vector.memset(featw[:, 1, 1:2], SC1 / T))
            nc.vector.memset(featw[:, 2, 2:3], 1.0 / T).then_inc(sem("feat_rows"), 1)
            dve.wait_ge(sem("feats"), 1)
            nc.vector.tensor_copy(feats1, P[0:3, 0, 0:BH]).then_inc(sem("feats_copied"), 1)
            dve.wait_ge(sem("mlp_made"), 3)
            chain(dve, nc.vector.tensor_scalar(logt1, P[:, 3, 0:BH], col("b3"), LOG_T_MIN, ALU.add, ALU.max))
            nc.vector.tensor_scalar(logt1, logt1, LOG_T_MAX, None, ALU.min).then_inc(sem("logt"), 1)
            dve.wait_ge(sem("temper"), 1)
            chain(dve, nc.vector.tensor_scalar(cool1, temper1, 0.5, None, ALU.mult))
            dve.sem_inc(sem("s2_evac_d"), 2)
            dve.sem_inc(sem("s2_normed"), RING)
            with dve.Fori(0, B // 2) as i:
                for j in range(2):
                    dve.wait_ge(sem("s2_mixed"), 2 * i + j + 1)
                    nc.vector.tensor_tensor(
                        heads(wts1[j], H1, T), heads(Dall[:, bass.ds(2 * i * HTK + j * HTK, HTK)], H1, T),
                        cool1[:, bass.ds(2 * i * H1 + j * H1, H1)].unsqueeze(2).broadcast_to([128, H1, T]), ALU.mult)\
                        .then_inc(sem("s2_scaled"), 1)
                for j in range(2):
                    for g in (1, 3):
                        dve.wait_ge(sem("s2_turned"), 8 * i + 4 * j + g + 1)
                        nc.vector.tensor_copy(wtT1[j][:, g * 512:(g + 1) * 512], P[:, g, :])\
                            .then_inc(sem("s2_evac_d"), 1)
                for j in range(2):
                    dve.wait_ge(sem("s2_mixed"), 2 * i + j + 1 + RING)
                    O = P[:, 4 + j, 0:H1 * (K1 + 1)].rearrange("p (h k) -> p h k", h=H1)
                    nc.vector.reciprocal(rz1[j], O[:, :, K1]).then_inc(sem("s2_rz"), 1)
                    nc.vector.memset(o1[j], 0.0).then_inc(sem("s2_rz"), 1)
                    dve.wait_ge(sem("s2_rz"), 8 * i + 4 * j + 2)
                    nc.vector.tensor_tensor(heads(raw1[j], H1, K1), O[:, :, 0:K1],
                                            rz1[j].unsqueeze(2).broadcast_to([128, H1, K1]), ALU.mult)\
                        .then_inc(sem("s2_rz"), 1)
                    dve.wait_ge(sem("s2_rz"), 8 * i + 4 * j + 3)
                    nc.vector.tensor_tensor(same1[j], raw1[j], raw1[j], ALU.is_equal).then_inc(sem("s2_rz"), 1)
                    dve.wait_ge(sem("s2_rz"), 8 * i + 4 * j + 4)
                    dve.sem_inc(sem("s2_guarded"), 1)
                    nc.vector.copy_predicated(o1[j], same1[j], raw1[j]).then_inc(sem("s2_normed"), 1)
            for h in range(2):
                dve.wait_ge(sem("stage_out"), 2 + h + 1)
                nc.vector.scalar_tensor_tensor(half(xT, h), P[:, h, :], col("bo"), half(xT, h), ALU.add, ALU.add)\
                    .then_inc(sem("x_ready"), 1)

        def pe_stage2(pe):
            pe_norm(pe, 2)
            pe.wait_ge(sem("fw_ready"), 1)

            def down(h):
                for cc in range(QC):
                    u = QC * h + cc
                    pe.wait_ge(sem("f_quant"), u + 1)
                    mm = nc.tensor.matmul(P[:, 4 + h, :], fw2q[:, cc * 128:(cc + 1) * 128], hq[:, u, :],
                                          start=(cc == 0), stop=(cc == QC - 1))
                mm.then_inc(sem("stage_out"), 1)
            for h in range(2):
                pe.wait_ge(sem("f_xq"), h + 1)
                for cc in range(QC):
                    u = QC * h + cc
                    if u >= 4:
                        pe.wait_ge(sem("f_copied"), u - 3)
                    nc.tensor.matmul(P[:, u % 4, :], fw1q[:, cc * 128:(cc + 1) * 128], half(xq, h),
                                     start=True, stop=True).then_inc(sem("f_hidden"), 1)
            down(0)
            down(1)

        def act_stage2(act):
            act_norm(act, 2)
            act.wait_ge(sem("fw_ready"), 1)
            for u in range(2 * QC):
                act.wait_ge(sem("f_hidden"), u + 1)
                if u >= 2:
                    act.wait_ge(sem("f_clipped"), u - 1)
                nc.scalar.activation(hraw[u % 2], P[:, u % 4, :], ACT.Identity, scale=1.0 / 64,
                                     bias=fbq[:, u % QC:u % QC + 1]).then_inc(sem("f_copied"), 1)

        def dve_stage2(dve):
            dve_norm(dve, 2)
            n = 0
            for h in range(2):
                dve.wait_ge(sem("xn_ready"), 4 + h + 1)
                nc.vector.tensor_scalar(half(xr, h), half(xn, h), 16.0, 127.0, ALU.mult, ALU.min)\
                    .then_inc(sem("f_step"), 1)
                dve.wait_ge(sem("f_step"), n + 1)
                nc.vector.tensor_scalar(half(xr, h), half(xr, h), -128.0, ROUND, ALU.max, ALU.add)\
                    .then_inc(sem("f_step"), 1)
                dve.wait_ge(sem("f_step"), n + 2)
                nc.vector.tensor_scalar(half(xq, h), half(xr, h), ROUND, None, ALU.subtract)\
                    .then_inc(sem("f_xq"), 1)
                n += 2
            for u in range(2 * QC):
                dve.wait_ge(sem("f_copied"), u + 1)
                nc.vector.tensor_scalar(hclip[u % 2], hraw[u % 2], 127.0, 0.0, ALU.min, ALU.max)\
                    .then_inc(sem("f_clipped"), 1)
                dve.wait_ge(sem("f_clipped"), u + 1)
                nc.vector.tensor_scalar(hq[:, u, :], hclip[u % 2], ROUND, ROUND, ALU.add, ALU.subtract)\
                    .then_inc(sem("f_quant"), 1)
            for h in range(2):
                dve.wait_ge(sem("stage_out"), 4 + h + 1)
                nc.vector.tensor_scalar(half(yq, h), P[:, 4 + h, :], 1.0 / 1024, fbq[:, QC:QC + 1],
                                        ALU.mult, ALU.add).then_inc(sem("f_out"), 1)
                dve.wait_ge(sem("f_out"), h + 1)
                nc.vector.tensor_tensor(half(xT, h), half(xT, h), half(yq, h), ALU.add)\
                    .then_inc(sem("x_ready"), 1)

        def sp_stage3(sp):
            sp.wait_ge(sem("dbl_copied"), 2)
            sp.dma_start(scratch, dbl).then_inc(sem("dbl_stored"), 16)
            sp.wait_ge(sem("dbl_stored"), 16)
            for dst, r in ((dtst, 64), (Bst, 0), (Cst, 32)):
                for b in range(B):
                    sp.dma_start(dst[b * NS:(b + 1) * NS, :], scratch[r:r + NS, b * T:(b + 1) * T])\
                        .then_inc(sem("states_loaded"), 16)

        def pe_stage3(pe):
            pe_norm(pe, 3)
            pe.wait_ge(sem("wd_loaded"), 16)
            for cc in range(2 * DC):
                for h in range(2):
                    u = 2 * cc + h
                    if u < 2:
                        pe.wait_ge(sem("xn_ready"), 6 + h + 1)
                    if u >= 4:
                        pe.wait_ge(sem("xz_copied"), u - 3)
                    nc.tensor.matmul(P[:, u % 4, :], w("wd", "Win")[:, cc * 128:(cc + 1) * 128], half(xn, h),
                                     start=True, stop=True).then_inc(sem("xz_made"), 1)
            pe.wait_ge(sem("conv_act"), DC)
            pe.wait_ge(sem("ln_rstd"), 8)
            for h in range(2):
                for cc in range(DC):
                    mm = nc.tensor.matmul(P[0:80, 4 + h, :], w("wd", "Wx")[:, cc * 80:(cc + 1) * 80],
                                          xcv[:, cc * N + h * HALF:cc * N + (h + 1) * HALF],
                                          start=(cc == 0), stop=(cc == DC - 1))
                mm.then_inc(sem("dbl_made"), 1)
            pe.wait_ge(sem("xz_copied"), 4 * DC)

            def spread(t):
                if t >= LOOK:
                    pe.wait_ge(sem("u_made"), t - LOOK + 1)
                pe.wait_ge(sem("x_repeated"), t + 1)
                for cc in range(DC):
                    mm = nc.tensor.transpose(P[:, t % LOOK, cc * 128:(cc + 1) * 128],
                                             xe3[t % LOOK][:, cc * 128:(cc + 1) * 128], ident)
                mm.then_inc(sem("x_spread"), 1)
            for t in range(LOOK):
                spread(t)
            for t in range(T):
                if t == 0:
                    pe.wait_ge(sem("cm_ready"), 1)
                    pe.wait_ge(sem("dbl_copied"), 2)
                g = t // STEPS
                if t % STEPS == 0 and g >= 2:
                    pe.wait_ge(sem("y3_copied"), g - 1)
                for cc in range(DC):
                    pe.wait_ge(sem("h_clipped"), DC * t + cc + 1)
                    at = (cc * STEPS + t % STEPS) * B
                    mm = nc.tensor.matmul(P[:, 4 + g % 2, at:at + B], h3[t % 4][:, cc * 128:(cc + 1) * 128],
                                          Cm[:, t * B:(t + 1) * B], start=True, stop=True)
                mm.then_inc(sem("y_step"), 1)
                if t + LOOK < T:
                    spread(t + LOOK)
            pe.wait_ge(sem("y3_gated"), DC)
            for h in range(2):
                for cc in range(DC):
                    mm = nc.tensor.matmul(P[:, 6 + h, :], w("wd", "Wout")[:, cc * 128:(cc + 1) * 128],
                                          yg3[1][:, cc * N + h * HALF:cc * N + (h + 1) * HALF],
                                          start=(cc == 0), stop=(cc == DC - 1))
                mm.then_inc(sem("stage_out"), 1)

        def pool_stage3(pool):
            pool.wait_ge(sem("conv_act"), DC)
            xv = xcv.rearrange("p (m t) -> p m t", t=T)
            for t in range(T):
                if t >= LOOK:
                    pool.wait_ge(sem("x_spread"), t - LOOK + 1)
                nc.gpsimd.tensor_copy(xe3[t % LOOK].rearrange("p (m s) -> p m s", s=NS),
                                      xv[:, :, t:t + 1].broadcast_to([128, DC * B, NS])).then_inc(sem("x_repeated"), 1)

        def act_stage3(act):
            act_norm(act, 3)
            for cc in range(2 * DC):
                for h in range(2):
                    u = 2 * cc + h
                    act.wait_ge(sem("xz_made"), u + 1)
                    if cc < DC:
                        nc.scalar.copy(xpad[:, cc, h * HB:(h + 1) * HB, 3:PADT],
                                       P[:, u % 4, :].rearrange("p (b t) -> p b t", b=HB)).then_inc(sem("xz_copied"), 1)
                    else:
                        at = (cc - DC) * N + h * HALF
                        nc.scalar.activation(sz[:, at:at + HALF], P[:, u % 4, :], ACT.Silu)\
                            .then_inc(sem("xz_copied"), 1)
            for cc in range(DC):
                act.wait_ge(sem("conv_done"), cc + 1)
                nc.scalar.activation(xcv[:, cc * N:(cc + 1) * N].rearrange("p (b t) -> p b t", b=B),
                                     conv[1][:, cc, :, :], ACT.Silu).then_inc(sem("conv_act"), 1)
            for h in range(2):
                act.wait_ge(sem("dbl_made"), h + 1)
                nc.scalar.copy(half(dbl, h), P[0:80, 4 + h, :]).then_inc(sem("dbl_copied"), 1)
            act.wait_ge(sem("states_loaded"), 16 * 3 * B)
            nc.scalar.activation(dstep[0], dtst, ACT.Exp).then_inc(sem("dt_exp"), 1)
            nc.scalar.activation(negA, col("alog"), ACT.Exp).then_inc(sem("dt_exp"), 1)
            act.wait_ge(sem("decay"), 1)
            nc.scalar.activation(Abar, dstep[3], ACT.Exp).then_inc(sem("abar"), 1)
            act.wait_ge(sem("bbar"), 1)
            for t in range(T):
                act.wait_ge(sem("x_spread"), t + 1)
                if t >= LOOK:
                    act.wait_ge(sem("h_raw"), DC * (t - LOOK + 1))
                nc.scalar.activation(U3[t % LOOK], P[:, t % LOOK, 0:DI], ACT.Copy, scale=Bbar[:, t:t + 1])\
                    .then_inc(sem("u_made"), 1)
                g = t // STEPS - 1
                if t % STEPS == LOOK and g >= 0:
                    collect(act, g)
            collect(act, T // STEPS - 1)

        def collect(act, g):
            act.wait_ge(sem("y_step"), (g + 1) * STEPS)
            nc.scalar.copy(yT3.rearrange("p (c b t) -> p c b t", c=DC, b=B)[:, :, :, g * STEPS:(g + 1) * STEPS],
                           P[:, 4 + g % 2, 0:DC * STEPS * B].rearrange("p (c t b) -> p c b t", c=DC, b=B))\
                .then_inc(sem("y3_copied"), 1)

        def dve_stage3(dve):
            dve_norm(dve, 3)
            nc.vector.memset(xpad[:, :, :, 0:3], 0.0).then_inc(sem("xpad_zero"), 1)
            dve.wait_ge(sem("xpad_zero"), 1)
            for cc in range(DC):
                dve.wait_ge(sem("xz_copied"), 2 * cc + 2)
                wv = col("conv_w")[:, 4 * cc:4 * cc + 4]
                chain(dve, nc.vector.tensor_scalar(conv[0][:, cc, :, :], xpad[:, cc, :, 0:T], wv[:, 0:1],
                                              col("conv_b")[:, cc:cc + 1], ALU.mult, ALU.add))
                for k in range(1, 4):
                    ins = nc.vector.scalar_tensor_tensor(conv[k % 2][:, cc, :, :], xpad[:, cc, :, k:k + T], wv[:, k:k + 1],
                                                         conv[(k + 1) % 2][:, cc, :, :], ALU.mult, ALU.add)
                    if k < 3:
                        chain(dve, ins)
                    else:
                        ins.then_inc(sem("conv_done"), 1)
            dve.wait_ge(sem("dt_exp"), 2)
            e, acc, tmp, dec = dstep
            chain(dve, nc.vector.tensor_scalar(e, e, 0.12, None, ALU.min))
            chain(dve, nc.vector.tensor_scalar(acc, e, -1.0 / 8, 1.0 / 7, ALU.mult, ALU.add))
            for k in range(6, 0, -1):
                chain(dve, nc.vector.tensor_tensor(tmp, acc, e, ALU.mult))
                chain(dve, nc.vector.tensor_scalar(acc, tmp, -1.0, 1.0 / k, ALU.mult, ALU.add))
            chain(dve, nc.vector.tensor_tensor(tmp, acc, e, ALU.mult))
            chain(dve, nc.vector.tensor_scalar(acc, tmp, DT_MIN, DT_MAX, ALU.max, ALU.min))
            chain(dve, nc.vector.tensor_scalar(tmp, acc, negA, -1.0, ALU.mult, ALU.mult))
            nc.vector.tensor_scalar(dec, tmp, -20.0, 0.0, ALU.max, ALU.min).then_inc(sem("decay"), 1)
            chain(dve, nc.vector.tensor_tensor(e, acc, Bst, ALU.mult))
            nc.vector.tensor_scalar(Bbar, e, -10.0, 10.0, ALU.max, ALU.min).then_inc(sem("bbar"), 1)
            nc.vector.tensor_tensor(Cm.rearrange("p (t b) -> p t b", b=B), Cst.unsqueeze(2).broadcast_to([128, T, B]),
                                    c("batch").unsqueeze(1).broadcast_to([128, T, B]), ALU.mult).then_inc(sem("cm_ready"), 1)
            chain(dve, nc.vector.memset(h3[3], 0.0))
            dve.wait_ge(sem("abar"), 1)
            for t in range(T):
                dve.wait_ge(sem("u_made"), t + 1)
                for cc in range(DC):
                    cs = slice(cc * 128, (cc + 1) * 128)
                    if t:
                        dve.wait_ge(sem("h_clipped"), DC * (t - 1) + cc + 1)
                    nc.vector.scalar_tensor_tensor(hraw3[t % 2][:, cs], h3[(t - 1) % 4][:, cs], Abar[:, t:t + 1],
                                                   U3[t % LOOK][:, cs], ALU.mult, ALU.add).then_inc(sem("h_raw"), 1)
                if t >= 4:
                    dve.wait_ge(sem("y_step"), t - 3)
                for cc in range(DC):
                    cs = slice(cc * 128, (cc + 1) * 128)
                    dve.wait_ge(sem("h_raw"), DC * t + cc + 1)
                    nc.vector.tensor_scalar(h3[t % 4][:, cs], hraw3[t % 2][:, cs], 100.0, -100.0, ALU.min, ALU.max)\
                        .then_inc(sem("h_clipped"), 1)
            dve.wait_ge(sem("y3_copied"), T // STEPS)
            for cc in range(DC):
                cs = slice(cc * N, (cc + 1) * N)
                chain(dve, nc.vector.tensor_tensor(yg3[0][:, cs], yT3[:, cs], sz[:, cs], ALU.mult))
                nc.vector.scalar_tensor_tensor(yg3[1][:, cs], xcv[:, cs], col("dskip")[:, cc:cc + 1], yg3[0][:, cs],
                                               ALU.mult, ALU.add).then_inc(sem("y3_gated"), 1)
            for h in range(2):
                dve.wait_ge(sem("stage_out"), 6 + h + 1)
                nc.vector.tensor_tensor(half(xT, h), half(xT, h), P[:, 6 + h, :], ALU.add)\
                    .then_inc(sem("x_ready"), 1)

        def slot_head(g, k):
            tile = 4 * (g // 2) + k
            return tile, 64 * (g % 2), 2 * tile + g % 2

        OH = 6

        def pe_stage4(pe):
            pe.wait_ge(sem("we_loaded"), 16)
            pe.wait_ge(sem("y3_gated"), DC)
            pe.wait_ge(sem("x_ready"), 8 + 2)
            for u in range(4 * HT):
                if u >= 4:
                    pe.wait_ge(sem("kv_copied_a" if u % 2 == 0 else "kv_copied_d"), (u - 4) // 2 + 1)
                if u < 2 * HT:
                    nc.tensor.matmul(P[:, u % 4, :], Xk[:, (u // 2) * 128:(u // 2 + 1) * 128], half(ctxT, u % 2),
                                     start=True, stop=True).then_inc(sem("kv_made"), 1)
                else:
                    b, r = divmod(u - 2 * HT, 2)
                    nc.tensor.matmul(P[:, u % 4, :], ctxT[:, b * T:(b + 1) * T], Xv[:, r * 512:(r + 1) * 512],
                                     start=True, stop=True).then_inc(sem("kv_made"), 1)
            pe_norm(pe, 4)
            pe.wait_ge(sem("kv_copied_a"), 2 * HT)
            pe.wait_ge(sem("kv_copied_d"), 2 * HT)
            pe.wait_ge(sem("xn_ready"), 10)
            pe.wait_ge(sem("ln_rstd"), 10)

            pe.sem_inc(sem("s4_scored"), 8)

            def queries(i, j, r):
                if j == 0 and r == 0:
                    pe.wait_ge(sem("s4_added"), 2 * i + 1)
                else:
                    pe.wait_ge(sem("q4_ready"), 4 * i + 2 * j + r)
                for k in range(4):
                    tile = 4 * r + k
                    mm = nc.tensor.matmul(P[:, 7, k * T:(k + 1) * T], Xq[:, tile * 128:(tile + 1) * 128],
                                          xn[:, bass.ds(2 * i * T + j * T, T)], start=True, stop=True)
                mm.then_inc(sem("q4_made"), 1)

            def scores(i, j, g):
                pe.wait_ge(sem("q4_ready"), 4 * i + 2 * j + g // 2 + 1)
                pe.wait_ge(sem("s4_shifted"), 8 * i + 4 * j + g + 1)
                if g == 0:
                    pe.wait_ge(sem("k4_staged"), 2 * i + j + 1)
                for k in range(4):
                    tile, row, _ = slot_head(g, k)
                    mm = nc.tensor.matmul(P[:, g % 2, k * T:(k + 1) * T], q4[j][row:row + K2, tile * T:(tile + 1) * T],
                                          ks4[j][row:row + K2, tile * T:(tile + 1) * T], start=True, stop=True)
                mm.then_inc(sem("s4_scored"), 1)

            def turn(i, j, g):
                freed = sem("s4_evac_a") if g % 2 == 0 else sem("s4_evac_d")
                pe.wait_ge(sem("s4_exp"), 8 * i + 4 * j + g + 1)
                pe.wait_ge(freed, 4 * i + 2 * j + g // 2 + 1)
                for k in range(4):
                    s = 4 * g + k
                    mm = nc.tensor.transpose(P[:, 2 + g % 2, k * T:(k + 1) * T], wts4[j][:, s * T:(s + 1) * T], ident)
                mm.then_inc(sem("s4_turned"), 1)

            def mix(i, j):
                pe.wait_ge(sem("s4_evac_a"), 4 * i + 2 * j + 2 + 1)
                pe.wait_ge(sem("s4_evac_d"), 4 * i + 2 * j + 2 + 1)
                pe.wait_ge(sem("s4_normed"), 2 * i + j + 1)
                for s in range(H2):
                    h = slot_head(s // 4, s % 4)[2]
                    at = (h % OH) * (K2 + 1)
                    mm = nc.tensor.matmul(P[:, 4 + h // OH, at:at + K2 + 1], wtT4[j][:, s * T:(s + 1) * T],
                                          V4[:, bass.ds(2 * i * VW + j * VW + h * (K2 + 1), K2 + 1)],
                                          start=True, stop=True)
                mm.then_inc(sem("s4_mixed"), 1)

            def project(i, j):
                pe.wait_ge(sem("s4_normed"), 2 * i + j + 1 + 1)
                for r in range(2):
                    if j == 0 and r == 0:
                        pe.wait_ge(sem("q4_ready"), 4 * i + 4)
                    elif r == 0:
                        pe.wait_ge(sem("s4_added"), 2 * i + 1 + 1)
                    else:
                        pe.wait_ge(sem("s4_ocopied"), 4 * i + 2 * j + 1)
                    for k in range(4):
                        tile = 4 * r + k
                        mm = nc.tensor.transpose(P[:, 7, k * T:(k + 1) * T], o4[j][:, tile * T:(tile + 1) * T], ident)
                    mm.then_inc(sem("s4_oturned"), 1)
                pe.wait_ge(sem("s4_ocopied"), 4 * i + 2 * j + 2)
                for tile in range(HT):
                    mm = nc.tensor.matmul(P[:, 7, 0:T], Xo[:, tile * 128:(tile + 1) * 128],
                                          oT4[j][:, tile * T:(tile + 1) * T], start=(tile == 0), stop=(tile == HT - 1))
                mm.then_inc(sem("y4"), 1)

            with pe.Fori(0, B // 2) as i:
                queries(i, 0, 0)
                queries(i, 0, 1)
                scores(i, 0, 0)
                scores(i, 0, 1)
                scores(i, 0, 2)
                turn(i, 0, 0)
                scores(i, 0, 3)
                turn(i, 0, 1)
                queries(i, 1, 0)
                queries(i, 1, 1)
                scores(i, 1, 0)
                turn(i, 0, 2)
                scores(i, 1, 1)
                turn(i, 0, 3)
                scores(i, 1, 2)
                turn(i, 1, 0)
                mix(i, 0)
                scores(i, 1, 3)
                turn(i, 1, 1)
                project(i, 0)
                turn(i, 1, 2)
                turn(i, 1, 3)
                mix(i, 1)
                project(i, 1)

        def pool_stage4(pool):
            pool.wait_ge(sem("kv_copied_a"), HT)
            pool.wait_ge(sem("kv_copied_d"), HT)
            with pool.Fori(0, B // 2) as i:
                for j in range(2):
                    pool.wait_ge(sem("s4_scored"), 8 * i + 4 * j + 4)
                    nc.gpsimd.tensor_copy(heads(ks4[j][:, :], HT, T), kT4[:, :, bass.ds(2 * i * T + j * T, T)])\
                        .then_inc(sem("k4_staged"), 1)

        def kv_copy(copy, u):
            if u < 2 * HT:
                copy(kT4[:, u // 2, (u % 2) * HALF:(u % 2 + 1) * HALF], P[:, u % 4, :])
            else:
                b, r = divmod(u - 2 * HT, 2)
                dst = V4.rearrange("p (b h k) -> p b h k", b=B, h=H2)[:, b, r * 8:(r + 1) * 8, 0:K2]
                copy(dst, heads(P[:, u % 4, :], 8, K2))

        def act_stage4(act):
            for u in range(0, 4 * HT, 2):
                act.wait_ge(sem("kv_made"), u + 1)
                if u == 0:
                    act.wait_ge(sem("v4_ones"), 1)
                kv_copy(lambda o, i: nc.scalar.copy(o, i).then_inc(sem("kv_copied_a"), 1), u)
            act_norm(act, 4)
            act.wait_ge(sem("xn_ready"), 10)
            act.sem_inc(sem("s4_evac_a"), 1)

            def queries(i, j):
                for r in range(2):
                    act.wait_ge(sem("q4_made"), 4 * i + 2 * j + r + 1)
                    nc.scalar.copy(q4[j][:, r * 512:(r + 1) * 512], P[:, 7, :]).then_inc(sem("q4_ready"), 1)

            def exps(i, j, g):
                act.wait_ge(sem("s4_shifted"), 8 * i + 4 * j + g + 1 + 2)
                nc.scalar.activation(wts4[j][:, g * 512:(g + 1) * 512], wts4[j][:, g * 512:(g + 1) * 512], ACT.Exp,
                                     scale=SC2).then_inc(sem("s4_exp"), 1)

            def evac(i, j, g):
                act.wait_ge(sem("s4_turned"), 8 * i + 4 * j + g + 1)
                nc.scalar.copy(wtT4[j][:, g * 512:(g + 1) * 512], P[:, 2, :]).then_inc(sem("s4_evac_a"), 1)

            def outs(i, j):
                for r in range(2):
                    act.wait_ge(sem("s4_oturned"), 4 * i + 2 * j + r + 1)
                    nc.scalar.copy(oT4[j][:, r * 512:(r + 1) * 512], P[:, 7, :]).then_inc(sem("s4_ocopied"), 1)
            with act.Fori(0, B // 2) as i:
                queries(i, 0)
                exps(i, 0, 0)
                exps(i, 0, 1)
                exps(i, 0, 2)
                evac(i, 0, 0)
                exps(i, 0, 3)
                queries(i, 1)
                exps(i, 1, 0)
                evac(i, 0, 2)
                exps(i, 1, 1)
                exps(i, 1, 2)
                evac(i, 1, 0)
                exps(i, 1, 3)
                outs(i, 0)
                evac(i, 1, 2)
                outs(i, 1)

        def dve_stage4(dve):
            dve.wait_ge(sem("y3_gated"), DC)
            nc.vector.memset(V4.rearrange("p (n k) -> p n k", k=K2 + 1)[:, :, K2:K2 + 1], 1.0).then_inc(sem("v4_ones"), 1)
            for u in range(1, 4 * HT, 2):
                dve.wait_ge(sem("kv_made"), u + 1)
                kv_copy(lambda o, i: nc.vector.tensor_copy(o, i).then_inc(sem("kv_copied_d"), 1), u)
            dve_norm(dve, 4)
            dve.sem_inc(sem("s4_shifted"), 2)
            dve.sem_inc(sem("s4_evac_d"), 1)
            dve.sem_inc(sem("s4_normed"), 1)
            dve.sem_inc(sem("s4_added"), 1)

            def shift(i, j, g):
                dve.wait_ge(sem("s4_scored"), 8 * i + 4 * j + g + 1 + 8)
                S = heads(P[:, g % 2, :], 4, T)
                mx = smax4[j][:, 4 * g:4 * g + 4]
                nc.vector.tensor_reduce(mx, S, AX, ALU.max).then_inc(sem("s4_max"), 1)
                dve.wait_ge(sem("s4_max"), 8 * i + 4 * j + g + 1)
                nc.vector.tensor_tensor(heads(wts4[j][:, g * 512:(g + 1) * 512], 4, T), S,
                                        mx.unsqueeze(2).broadcast_to([128, 4, T]), ALU.subtract)\
                    .then_inc(sem("s4_shifted"), 1)

            def evac(i, j, g):
                dve.wait_ge(sem("s4_turned"), 8 * i + 4 * j + g + 1)
                nc.vector.tensor_copy(wtT4[j][:, g * 512:(g + 1) * 512], P[:, 3, :]).then_inc(sem("s4_evac_d"), 1)

            def norm(i, j):
                dve.wait_ge(sem("s4_mixed"), 2 * i + j + 1)
                parts = [(k, min(OH, H2 - k * OH)) for k in range(3)]
                for k, n in parts:
                    O = P[:, 4 + k, 0:n * (K2 + 1)].rearrange("p (h k) -> p h k", h=n)
                    nc.vector.reciprocal(rz4[j][:, k * OH:k * OH + n], O[:, :, K2]).then_inc(sem("s4_rz"), 1)
                for k, n in parts:
                    dve.wait_ge(sem("s4_rz"), 6 * i + 3 * j + k + 1)
                    O = P[:, 4 + k, 0:n * (K2 + 1)].rearrange("p (h k) -> p h k", h=n)
                    ins = nc.vector.tensor_tensor(heads(o4[j][:, k * OH * K2:(k * OH + n) * K2], n, K2), O[:, :, 0:K2],
                                                  rz4[j][:, k * OH:k * OH + n].unsqueeze(2).broadcast_to([128, n, K2]),
                                                  ALU.mult)
                    ins.then_inc(sem("s4_normed" if k == 2 else "s4_part"), 1)

            def add(i, j):
                dve.wait_ge(sem("y4"), 2 * i + j + 1)
                xb = xT[:, bass.ds(2 * i * T + j * T, T)]
                nc.vector.tensor_tensor(xb, xb, P[:, 7, 0:T], ALU.add).then_inc(sem("s4_added"), 1)
            with dve.Fori(0, B // 2) as i:
                shift(i, 0, 0)
                shift(i, 0, 1)
                shift(i, 0, 2)
                shift(i, 0, 3)
                evac(i, 0, 1)
                shift(i, 1, 0)
                shift(i, 1, 1)
                evac(i, 0, 3)
                shift(i, 1, 2)
                norm(i, 0)
                shift(i, 1, 3)
                evac(i, 1, 1)
                add(i, 0)
                evac(i, 1, 3)
                norm(i, 1)
                add(i, 1)
            dve.drain().then_inc(sem("x_ready"), 2)

        def sp_stage5(sp):
            sp.wait_ge(sem("x_ready"), 12)
            for i in range(E2 // RW):
                for k in range(RW // 2):
                    e = RW * i + 2 * k
                    if i:
                        sp.wait_ge(sem("e5_out"), e - RW + 2)
                    sp.dma_start(wring[:, 2 * k:2 * k + 2, :], d["moe"][e:e + 2].rearrange("e p n -> p e n"))\
                        .then_inc(sem(f"moe_loaded{k}"), 16)
            sp.wait_ge(sem("zero5"), 1)
            sp.dma_start(slots_dram[SLOTS:SLOTS + 1, :], zero5[0:1, :]).then_inc(sem("slots_stored"), 16)
            for i in range(2):
                ne = E2 // 2
                sp.wait_ge(sem("e5_kept"), ne * (i + 1))
                sp.dma_start(slots_dram[i * ne * CAP:(i + 1) * ne * CAP, :].rearrange("(e s) d -> s e d", s=CAP),
                             eo5[:, i * ne:(i + 1) * ne, :]).then_inc(sem("slots_stored"), 16)

        def pe_stage5(pe):
            pe_norm(pe, 5)
            for b in range(B):
                if b % HB == 0:
                    pe.wait_ge(sem("xn_ready"), 10 + b // HB + 1)
                mm = nc.tensor.matmul(heads(P[:, 0, 0:B * E2], B, E2)[:, b, :], xn[:, b * T:(b + 1) * T],
                                      w("wf", "gate"), start=True, stop=True)
            mm.then_inc(sem("gates"), 1)
            for b in range(B):
                mm = nc.tensor.transpose(P[:, 3 + b // HB, (b % HB) * T:(b % HB + 1) * T], xn[:, b * T:(b + 1) * T], ident)
            mm.then_inc(sem("tokens"), 1)
            pe.wait_ge(sem("top1"), 1)
            nc.tensor.matmul(P[:, 1, 0:B * E2], c("tri"), g5[3].rearrange("p b e -> p (b e)"), start=True, stop=True)\
                .then_inc(sem("counts"), 1)
            nc.tensor.matmul(P[:, 2, 0:B * E2], mean128[:, :], g5[3].rearrange("p b e -> p (b e)"), start=True, stop=True)\
                .then_inc(sem("counts"), 1)
            pe.wait_ge(sem("xpart"), 3)
            chunks = [(0, 512), (512, 512), (1024, SLOTS - 1024)]
            for b in range(B):
                pe.wait_ge(sem("hot"), b + 1)
                for part in range(3):
                    lhs = xpart[:, part * N + b * T:part * N + (b + 1) * T]
                    for k, (a, n) in enumerate(chunks):
                        mm = nc.tensor.matmul(P[:, 5 + k, 0:n], lhs, hot5[b % 4][:, a:a + n],
                                              start=(b == 0 and part == 0), stop=(b == B - 1 and part == 2))
                mm.then_inc(sem("hot_used"), 1)

            def up(e):
                pe.wait_ge(sem(f"moe_loaded{e % RW // 2}"), 16 * (e // RW + 1))
                if e == 0:
                    pe.wait_ge(sem("dispatched"), 3)
                if e >= 2:
                    pe.wait_ge(sem("e5_act"), e - 1)
                for k in range(FC):
                    mm = nc.tensor.matmul(P[:, e % 2, k * CAP:(k + 1) * CAP], w1r[e % RW][:, k * 128:(k + 1) * 128],
                                          dT5[:, e * CAP:(e + 1) * CAP], start=True, stop=True)
                mm.then_inc(sem("e5_hidden"), 1)

            def down(e):
                pe.wait_ge(sem("e5_act"), e + 1)
                if e >= 2:
                    pe.wait_ge(sem("e5_kept"), e - 1)
                for k in range(FC):
                    mm = nc.tensor.matmul(P[0:CAP, 2 + e % 2, 0:D], hT5[e % 2][:, k * CAP:(k + 1) * CAP],
                                          w2r[e % RW][:, k * D:(k + 1) * D], start=(k == 0), stop=(k == FC - 1))
                mm.then_inc(sem("e5_out"), 1)
            up(0)
            for e in range(E2):
                if e + 1 < E2:
                    up(e + 1)
                down(e)
            for b in range(B):
                mm = nc.tensor.transpose(P[:, 5 + b // HB, (b % HB) * T:(b % HB + 1) * T], xT[:, b * T:(b + 1) * T], ident)
            mm.then_inc(sem("out_turned"), 1)

        def act_stage5(act):
            act_norm(act, 5)
            act.wait_ge(sem("gate_shift"), 1)
            nc.scalar.activation(g5[5], g5[4], ACT.Exp).then_inc(sem("gate_exp"), 1)
            for part in range(3):
                if part == 0:
                    act.wait_ge(sem("tokens"), 1)
                    for r in range(2):
                        nc.scalar.copy(xpart[:, r * HALF:(r + 1) * HALF], P[:, 3 + r, :])
                    act.drain().then_inc(sem("xpart"), 1)
                else:
                    act.wait_ge(sem("xrest"), part)
                    nc.scalar.copy(xpart[:, part * N:(part + 1) * N], xrest[part - 1]).then_inc(sem("xpart"), 1)
            for k, (a, n) in enumerate([(0, 512), (512, 512), (1024, SLOTS - 1024)]):
                act.wait_ge(sem("hot_used"), B)
                nc.scalar.copy(dT5[:, a:a + n], P[:, 5 + k, 0:n]).then_inc(sem("dispatched"), 1)
            for e in range(E2):
                act.wait_ge(sem("e5_hidden"), e + 1)
                if e >= 2:
                    act.wait_ge(sem("e5_out"), e - 1)
                nc.scalar.activation(hT5[e % 2], P[:, e % 2, 0:FC * CAP], ACT.Gelu_apprx_tanh).then_inc(sem("e5_act"), 1)

        def dve_stage5(dve):
            dve_norm(dve, 5)

            def per(v, n=E2):
                return v.unsqueeze(2).broadcast_to([128, B, n])

            def row(name):
                return c(name).unsqueeze(1).broadcast_to([128, B, E2])
            nc.vector.memset(zero5, 0.0).then_inc(sem("zero5"), 1)
            dve.wait_ge(sem("gates"), 1)
            G = heads(P[:, 0, 0:B * E2], B, E2)
            chain(dve, nc.vector.tensor_reduce(v5[0], G, AX, ALU.max))
            nc.vector.tensor_tensor(g5[4], G, per(v5[0]), ALU.subtract).then_inc(sem("gate_shift"), 1)
            dve.wait_ge(sem("gate_shift"), 1)
            chain(dve, nc.vector.tensor_scalar(g5[0], g5[4], 0.0, None, ALU.is_equal))
            chain(dve, nc.vector.tensor_tensor(g5[1], g5[0], row("prio16"), ALU.mult))
            chain(dve, nc.vector.tensor_reduce(v5[1], g5[1], AX, ALU.max))
            nc.vector.tensor_tensor(g5[3], g5[1], per(v5[1]), ALU.is_equal).then_inc(sem("top1"), 1)
            dve.wait_ge(sem("xpart"), 1)
            for r in range(2):
                nc.vector.tensor_tensor(half(xrest[0], r), P[:, 3 + r, :], half(xpart, r), ALU.subtract)
            dve.drain().then_inc(sem("xrest"), 1)
            dve.wait_ge(sem("counts"), 2)
            chain(dve, nc.vector.memset(g5[2][:, 0, :], 0.0))
            M = heads(P[:, 2, 0:B * E2], B, E2)
            for b in range(1, B):
                chain(dve, nc.vector.scalar_tensor_tensor(g5[2][:, b, :], M[:, b - 1, :], float(D), g5[2][:, b - 1, :],
                                                     ALU.mult, ALU.add))
            chain(dve, nc.vector.tensor_tensor(g5[6], heads(P[:, 1, 0:B * E2], B, E2), g5[2], ALU.add))
            chain(dve, nc.vector.tensor_tensor(g5[7], g5[6], g5[3], ALU.mult))
            chain(dve, nc.vector.tensor_reduce(v5[2], g5[7], AX, ALU.add))
            chain(dve, nc.vector.tensor_tensor(g5[6], row("ebase"), g5[3], ALU.mult))
            chain(dve, nc.vector.tensor_reduce(v5[3], g5[6], AX, ALU.add))
            chain(dve, nc.vector.tensor_scalar(v5[4], v5[2], float(CAP), 2.0 * SLOTS, ALU.is_gt, ALU.mult))
            chain(dve, nc.vector.scalar_tensor_tensor(v5[5], v5[2], -1.0, v5[3], ALU.add, ALU.add))
            chain(dve, nc.vector.tensor_tensor(v5[6], v5[5], v5[4], ALU.add))
            nc.vector.tensor_scalar(idx5, v5[6], float(SLOTS), None, ALU.min).then_inc(sem("slots"), 1)
            dve.wait_ge(sem("xpart"), 2)
            chain(dve, nc.vector.tensor_tensor(xrest[1], xrest[0], xpart[:, N:2 * N], ALU.subtract))
            dve.drain().then_inc(sem("xrest"), 1)
            for b in range(B):
                if b >= 4:
                    dve.wait_ge(sem("hot_used"), b - 3)
                nc.vector.tensor_scalar(hot5[b % 4], c("iota"), v5[6][:, b:b + 1], None, ALU.is_equal)\
                    .then_inc(sem("hot"), 1)
            dve.wait_ge(sem("gate_exp"), 1)
            chain(dve, nc.vector.tensor_reduce(v5[0], g5[5], AX, ALU.add))
            chain(dve, nc.vector.reciprocal(v5[7], v5[0]))
            for e in range(E2):
                dve.wait_ge(sem("e5_out"), e + 1)
                nc.vector.tensor_copy(eo5[:, e, :], P[0:CAP, 2 + e % 2, 0:D]).then_inc(sem("e5_kept"), 1)
            dve.wait_ge(sem("out_turned"), 1)
            for b in range(B):
                if b == 0:
                    dve.wait_ge(sem("gathered"), 16 * B)
                ins = nc.vector.scalar_tensor_tensor(
                    final[:, b * D:(b + 1) * D], yg5[:, b * D:(b + 1) * D], v5[7][:, b:b + 1],
                    P[:, 5 + b // HB, (b % HB) * D:(b % HB + 1) * D], ALU.mult, ALU.add)
            dve.drain().then_inc(sem("out_ready"), 1)

        def pool_stage5(pool):
            pool.wait_ge(sem("slots"), 1)
            pool.wait_ge(sem("slots_stored"), 48)
            for b in range(B):
                pool.indirect_dma_start(yg5[:, b * D:(b + 1) * D], None, slots_dram,
                                        bass.IndirectOffsetOnAxis(ap=idx5[:, b:b + 1], axis=0)).then_inc(sem("gathered"), 16)

        nothing = lambda engine: None
        pe_stages = [pe_stage0, pe_stage1, pe_stage2, pe_stage3, pe_stage4, pe_stage5]
        act_stages = [act_stage0, act_stage1, act_stage2, act_stage3, act_stage4, act_stage5]
        dve_stages = [dve_stage0, dve_stage1, dve_stage2, dve_stage3, dve_stage4, dve_stage5]
        pool_stages = [pool_stage0 if stop > 1 else nothing, pool_stage1, nothing, pool_stage3, pool_stage4, pool_stage5]

        @block.sync
        def _(sp):
            sp.dma_start(heads(xtok, B, D), d["x"].rearrange("b t d -> t b d")).then_inc(sem("x_loaded"), 16)
            sp.dma_start(packs["consts"][:, :], d["consts"]).then_inc(sem("consts_loaded"), 16)
            sp.dma_start(packs["small"][:, :], d["small"]).then_inc(sem("small_loaded"), 16)
            sp.dma_start(packs["wa"][:, :], d["wa"]).then_inc(sem("wa_loaded"), 16)
            sp.dma_start(heads(ctok, B, D), d["ctx"].rearrange("b t d -> t b d")).then_inc(sem("ctx_loaded"), 16)
            for k in ("wb", "wc", "wd", "wf"):
                sp.dma_start(packs[k][:, :], d[k]).then_inc(sem(k + "_loaded"), 16)
            if stop > 3:
                sp_stage3(sp)
            if stop > 4:
                sp.wait_ge(sem("conv_act"), DC)
                sp.dma_start(we, d["we"]).then_inc(sem("we_loaded"), 16)
            if stop > 5:
                sp_stage5(sp)
            sp.wait_ge(sem("out_ready"), 1)
            sp.dma_start(out.rearrange("b t d -> t b d"), heads(final if stop > 5 else xc, B, D))\
                .then_inc(sem("stored"), 16)
            sp.wait_ge(sem("stored"), 16)

        @block.tensor
        def _(pe):
            pe.wait_ge(sem("consts_loaded"), 16)
            pe.wait_ge(sem("x_loaded"), 16)
            for b in range(B):
                mm = nc.tensor.transpose(P[:, b // HB, (b % HB) * T:(b % HB + 1) * T], xtok[:, b * D:(b + 1) * D], ident)
                if b % HB == HB - 1:
                    mm.then_inc(sem("x_turned"), 1)
            pe.wait_ge(sem("ctx_loaded"), 16)
            for b in range(B):
                mm = nc.tensor.transpose(P[:, 2 + b // HB, (b % HB) * T:(b % HB + 1) * T], ctok[:, b * D:(b + 1) * D], ident)
                if b % HB == HB - 1:
                    mm.then_inc(sem("ctx_turned"), 1)
            pe.wait_ge(sem("means_set"), 3)
            if stop > 1:
                pe_keys1(pe)
            for f in pe_stages[:stop]:
                f(pe)
            if stop > 5:
                return
            for h in range(2):
                pe.wait_ge(sem("x_ready"), 2 * stop + h + 1)
            for b in range(B):
                mm = nc.tensor.transpose(P[:, b // HB, (b % HB) * T:(b % HB + 1) * T], xT[:, b * T:(b + 1) * T], ident)
            mm.then_inc(sem("out_turned"), 1)

        @block.scalar
        def _(act):
            act.wait_ge(sem("small_loaded"), 16)
            act.wait_ge(sem("means_set"), 3)
            for h in range(2):
                act.wait_ge(sem("ctx_turned"), h + 1)
                nc.scalar.copy(half(ctxT, h), P[:, 2 + h, :]).then_inc(sem("ctx_ready"), 1)
            if stop > 1:
                act_keys1(act)
            for f in act_stages[:stop]:
                f(act)
            if stop > 5:
                return
            act.wait_ge(sem("out_turned"), 1)
            act.wait_ge(sem("ln_rstd"), 2 * stop)
            for h in range(2):
                nc.scalar.copy(half(xc, h), P[:, h, :])
            act.drain().then_inc(sem("out_ready"), 1)

        @block.vector
        def _(dve):
            nc.vector.memset(mean128[:, :], 1.0 / D).then_inc(sem("means_set"), 1)
            nc.vector.memset(mean64[:, :], 1.0 / R0).then_inc(sem("means_set"), 1)
            nc.vector.memset(eps[:, :], EPS).then_inc(sem("means_set"), 1)
            dve.wait_ge(sem("small_loaded"), 16)
            for h in range(2):
                dve.wait_ge(sem("x_turned"), h + 1)
                nc.vector.tensor_copy(half(xT, h), P[:, h, :]).then_inc(sem("x_ready"), 1)
            if stop > 1:
                dve_keys1(dve)
            for f in dve_stages[:stop]:
                f(dve)

        @block.gpsimd
        def _(pool):
            for f in pool_stages[:stop]:
                f(pool)


_INS = ["x", "ctx", "consts", "small", "wa", "wb", "wc", "wd", "we", "wf", "moe"]


def constants():
    p = np.arange(128)
    c = {
        "ident": np.eye(128), "head": p[:, None] // K1 == np.arange(H1), "batch": p[:, None] // NS == np.arange(B),
        "tri": p[:, None] <= p[None, :], "prio6": np.tile(E0 - np.arange(E0), (128, 1)),
        "prio16": np.tile(E2 - np.arange(E2), (128, 1)), "ebase": np.tile(CAP * np.arange(E2), (128, 1)),
        "iota": np.tile(np.arange(SLOTS), (128, 1)),
    }
    owner = np.repeat(ORDER, F0)
    c["select"] = p[:, None] == owner[None, :]
    return np.concatenate([np.asarray(c[n], np.float32).reshape(128, k) for n, k in CONSTS], 1)


def pack(pieces):
    return np.concatenate([np.pad(a, ((0, 128 - a.shape[0]), (0, 0))) for a in pieces], 1)


def kernel(**inputs):
    import concourse.bacc as _bacc
    from concourse.bass_utils import run_bass_kernel_spmd as _run
    i = {k: np.asarray(v) for k, v in inputs.items()}

    def v(name):
        a = i[name].reshape(-1)
        return a.reshape(-1, min(128, a.size)).T

    def r(name):
        return np.broadcast_to(i[name].reshape(1, -1), (128, i[name].size))

    def tiles(a):
        return a.reshape(-1, 128, a.shape[1]).transpose(1, 0, 2).reshape(128, -1)
    W1 = i["L0_attn_W1"][ORDER]
    cw = i["L1_attn_conv_w"].reshape(DC, 128, 4).transpose(1, 0, 2).reshape(128, -1)
    Wx = i["L1_attn_W_xproj"]
    zx = np.zeros((16, DI), np.float32)
    wx = np.concatenate([Wx[0:NS], zx, Wx[NS:2 * NS], zx, np.broadcast_to(Wx[2 * NS:], (NS, DI))], 0)
    arrays = {
        "x": i["x"], "ctx": i["ctx_1024"], "consts": constants(),
        "small": pack([v("L0_attn_r1_b"), v("L0_attn_ln_g"), v("L0_attn_ln_b"),
                       i["L0_attn_b1"][ORDER].reshape(C0, 128).T, v("L0_xattn_bq"), v("L0_xattn_bk"),
                       v("L0_xattn_bo"), v("L0_xattn_b1"), v("L0_xattn_b2"), v("L0_ffn_b1"), v("L0_ffn_b2"),
                       cw, v("L1_attn_conv_b"), v("L1_attn_D_param"),
                       np.tile(i["L1_attn_A_log"], B).reshape(128, 1),
                       r("L0_attn_r2_b"), r("L0_attn_route_bias"), r("L0_attn_temp"), r("L0_xattn_bv"),
                       r("L0_xattn_b3")]),
        "wa": pack([i["L0_attn_r1_w"], i["L0_attn_r2_w"], W1.transpose(1, 0, 2).reshape(D, -1),
                    tiles(i["L0_attn_W2"][ORDER].reshape(-1, D)), i["L0_attn_b2"]]),
        "wb": pack([i["L0_xattn_Wq"].T, i["L0_xattn_Wk"].T, i["L0_xattn_Wv"].T, i["L0_xattn_Wo"].T,
                    i["L0_xattn_w1"].T, i["L0_xattn_w2"].T, np.broadcast_to(i["L0_xattn_w3"].T, (M1, 128))]),
        "wc": pack([i["L0_ffn_w1"].T, tiles(i["L0_ffn_w2"].T)]),
        "wd": pack([i["L1_attn_W_in"].T, tiles(wx.T), tiles(i["L1_attn_W_out"].T)]),
        "we": pack([i["L1_xattn_" + n].reshape(D, -1) for n in ("Wq", "Wk", "Wv")]
                   + [tiles(i["L1_xattn_Wo"].reshape(-1, D))]),
        "wf": pack([i["L1_ffn_gate_w"].T]),
        "moe": np.concatenate([i["L1_ffn_w1"], i["L1_ffn_w2"].reshape(E2, FC, 128, D).transpose(0, 2, 1, 3)
                               .reshape(E2, 128, FC * D)], 2),
    }
    nc = _bacc.Bacc("TRN2", target_bir_lowering=False, num_devices=1)
    feed, d = {}, {}
    for name in _INS:
        feed[f"in_{name}_dram"] = np.ascontiguousarray(arrays[name])
        d[name] = nc.dram_tensor(f"in_{name}_dram", feed[f"in_{name}_dram"].shape, F32, kind="ExternalInput").ap()
    out = nc.dram_tensor("out_0_dram", (B, T, D), F32, kind="ExternalOutput").ap()
    program(nc, d, out, 6)
    res = _run(nc, [feed], core_ids=[0])
    return res.results[0]["out_0_dram"]
```

```python
from contextlib import ExitStack

import concourse.bass as bass
from concourse import mybir
import numpy as np

F32 = mybir.dt.float32
BF16 = mybir.dt.bfloat16
I32 = mybir.dt.int32
ALU = mybir.AluOpType
ACT = mybir.ActivationFunctionType
AX = mybir.AxisListType.X

B, T, D = 8, 128, 128
N = B * T
HALF = N // 2
HB = B // 2
EPS = 1e-5

E0, F0, R0 = 6, 192, 64
C0 = E0 * F0 // 128
MIXED = C0 // 2
ORDER = [0, 2, 4, 1, 3, 5]

H1, K1 = 16, 8
M1 = 64
SC1 = float(K1) ** -0.5
FQ = 512
QC = FQ // 128
ROUND = 12582912.0

DI, NS = 256, 16
DC = DI // 128
DT_MIN, DT_MAX = 0.001, 0.1
LOOK = 4
STEPS = 16
PLACED = 8

H2, K2 = 16, 64
SC2 = float(K2) ** -0.5
HT = H2 * K2 // 128

E2, F2, CAP = 16, 512, 80
FC = F2 // 128
SLOTS = E2 * CAP

LOG_T_MIN, LOG_T_MAX = float(np.log(0.1)), float(np.log(10.0))

CONSTS = [("ident", 128), ("head", H1), ("batch", B), ("tri", 128), ("prio6", E0), ("prio16", E2),
          ("ebase", E2), ("select", C0 * 128), ("iota", SLOTS)]
COLS = [("r1_b", 1), ("ln_g", 1), ("ln_b", 1), ("b1", C0), ("bq", 1), ("bk", 1), ("bo", 1), ("m1", 1),
        ("m2", 1), ("fb1", QC), ("fb2", 1), ("conv_w", 4 * DC), ("conv_b", DC), ("dskip", DC), ("alog", 1)]
ROWS = [("r2_b", E0), ("route", E0), ("temp", 1), ("bv", D), ("b3", 1)]
WA = [("r1_w", R0), ("r2_w", E0), ("W1", C0 * 128), ("W2", C0 * 128), ("b2", D)]
WB = [("Wq", D), ("Wk", D), ("Wv", D), ("Wo", D), ("mw1", M1), ("mw2", M1), ("mw3", 128)]
WC = [("fw1", FQ), ("fw2", QC * 128)]
WD = [("Win", 2 * DI), ("Wx", DC * 80), ("Wout", DC * 128)]
WE = [("Xq", H2 * K2), ("Xk", H2 * K2), ("Xv", H2 * K2), ("Xo", HT * 128)]
WF = [("gate", E2)]
PACKS = {"consts": CONSTS, "small": COLS + ROWS, "wa": WA, "wb": WB, "wc": WC, "wd": WD, "we": WE, "wf": WF}


FB_AT = sum(n for _, n in COLS[:[k for k, _ in COLS].index("fb1")])


def width(pack):
    return sum(n for _, n in PACKS[pack])


def program(nc, d, out, stop):
    with ExitStack() as ctx:
        def sb(name, shape, dt=F32):
            return ctx.enter_context(nc.sbuf_tensor(name, shape, dt))

        sems = {}

        def sem(name):
            if name not in sems:
                sems[name] = ctx.enter_context(nc.semaphore(name))
            return sems[name]

        P = ctx.enter_context(nc.psum_tensor("P", [128, 8, 512], F32))

        arena1 = sb("arena1", [128, 16640])
        arena2 = sb("arena2", [128, 16384])
        packs = {k: sb("pack_" + k, [128, width(k)]) for k in ("consts", "small", "wa", "wb", "wc", "wd", "wf")}
        if stop >= 5:
            pass

        def w(pack, name, rows=128):
            at = 0
            for n, k in PACKS[pack]:
                if n == name:
                    return packs[pack][0:rows, at:at + k]
                at += k
            raise KeyError(name)

        def c(name, rows=128):
            return w("consts", name, rows)

        def col(name, rows=128):
            return w("small", name, rows)

        ident = c("ident")
        mean128 = sb("mean128", [128, 128])
        mean64 = sb("mean64", [R0, R0])
        eps = sb("eps", [128, 1])
        xT = sb("xT", [128, N])
        xn = sb("xn", [128, N])
        lnbuf = sb("lnbuf", [128, 2 * N])
        xc = lnbuf[:, 0:N]
        sq = lnbuf[:, N:2 * N]
        ctxT = sb("ctxT", [128, N])

        def half(t, h):
            return t[:, h * HALF:(h + 1) * HALF]

        def heads(t, k, n):
            return t.rearrange("p (k n) -> p k n", k=k)

        at1 = [0]

        def a1(n, dt=F32):
            t = arena1[:, at1[0]:at1[0] + n]
            at1[0] += n
            return t
        xtok = a1(N)
        ctok = a1(N)
        rh = a1(N)[0:R0, :]
        rc = a1(N)[0:R0, :]
        rs = a1(N)[0:R0, :]
        rg = a1(N)[0:R0, :]
        lg = [heads(a1(B * E0), B, E0) for _ in range(12)]
        red = [a1(B).unsqueeze(2) for _ in range(6)]
        rtemp = a1(1)
        probsT = a1(N)[0:E0, :]
        act0 = [a1(HALF) for _ in range(3)]
        wact0 = [a1(HALF) for _ in range(3)]
        W1 = heads(w("wa", "W1"), C0, 128)
        W2 = heads(w("wa", "W2"), C0, 128)
        SEL = heads(c("select", E0), C0, 128)

        Kexp = arena2[:, :]
        Dall = arena1[:, 0:16384]
        kT1 = sb("kT1", [128, N])
        qT1 = sb("qT1", [128, N])
        V1 = sb("V1", [128, B * H1 * (K1 + 1)])
        qs1 = [sb(f"qs1_{j}", [128, T]) for j in range(2)]
        HTK = H1 * T
        exp1 = [packs["wa"][:, 0:HTK], lnbuf[:, :]]
        st1 = [sb(f"st1_{j}", [128, H1, 6]) for j in range(2)]
        BH = B * H1
        stats1 = sb("stats1", [128, BH, 6])
        max1 = sb("max1", [128, BH])
        smax1 = [sb(f"smax1_{j}", [128, H1]) for j in range(2)]
        wts1 = [arena2[:, j * HTK:(j + 1) * HTK] for j in range(2)]
        wtT1 = [arena2[:, (2 + j) * HTK:(3 + j) * HTK] for j in range(2)]
        at2 = [4 * HTK]

        def a2(n):
            t = arena2[:, at2[0]:at2[0] + n]
            at2[0] += n
            return t
        tmp1 = [a2(BH) for _ in range(6)]
        ent1 = a2(BH)
        simrow1 = a2(BH)
        qsum1, ksum1, sim1 = a2(B), a2(B), a2(B)
        featw = a2(9).rearrange("p (f m) -> p f m", f=3)
        feats1, hid1, hid2 = a2(BH)[0:3, :], a2(BH)[0:M1, :], a2(BH)[0:M1, :]
        logt1, temper1, cool1 = a2(BH), a2(BH), a2(BH)
        rz1 = [a2(H1) for _ in range(2)]
        raw1 = [a2(D) for _ in range(2)]
        same1 = [a2(D).bitcast(I32) for _ in range(2)]
        o1 = [a2(D) for _ in range(2)]
        oT1 = a2(N)

        fw1q = sb("fw1q", [128, FQ], BF16)
        fw2q = sb("fw2q", [128, QC * 128], BF16)
        fbq = sb("fbq", [128, QC + 1])
        ftmp = [sb(f"ftmp{k}", [128, FQ]) for k in range(2)]
        xq = arena1[:, 0:N // 2].bitcast(BF16)
        xr = arena1[:, N:2 * N]
        hraw = [arena1[:, (4 + u) * HALF:(5 + u) * HALF] for u in range(2)]
        hclip = [arena1[:, (6 + u) * HALF:(7 + u) * HALF] for u in range(2)]
        hq = arena1[:, 8 * HALF:12 * HALF].bitcast(BF16).rearrange("p (u n) -> p u n", u=2 * QC)
        yq = arena1[:, 12 * HALF:14 * HALF]

        at3 = [0]

        def a3(n, cols=None):
            t = arena2[:, at3[0]:at3[0] + n]
            at3[0] += n
            return t
        PADT = T + 3
        xpad = a3(DC * B * PADT).rearrange("p (c b t) -> p c b t", c=DC, b=B)
        conv = [a3(DC * N).rearrange("p (c b t) -> p c b t", c=DC, b=B) for _ in range(2)]
        xcv = a3(DC * N)
        sz = a3(DC * N)
        dbl = a3(N)[0:80, :]
        Bst, Cst, dtst = a3(T), a3(T), a3(T)
        dstep = [a3(T) for _ in range(4)]
        Abar, Bbar = a3(T), a3(T)
        negA = a3(1)
        Cpad = arena1[:, 0:STEPS * 128]
        Cdiag = arena1[:, 0:STEPS * (128 + B)].rearrange("p (k r) -> p k r", k=STEPS)[:, :, 0:B]
        ysum3 = [arena1[:, 2304 + k * DI:2304 + (k + 1) * DI] for k in range(2)]
        xe3 = [a3(DI) for _ in range(LOOK)]
        U3 = [a3(DI) for _ in range(4)]
        hraw3 = [a3(DI) for _ in range(2)]
        h3 = [arena1[:, 15360 + k * DI:15360 + (k + 1) * DI] for k in range(4)]
        yT3 = arena1[:, 9216:9216 + DC * N]
        yg3 = [arena1[:, 11264 + k * DC * N:11264 + (k + 1) * DC * N] for k in range(2)]
        scratch = nc.dram_tensor("states_scratch", (3, B, NS, T), F32, kind="Internal").ap()

        kT4 = arena1[:, 0:HT * N].rearrange("p (m n) -> p m n", m=HT)
        VW = H2 * (K2 + 1)
        V4 = arena1[:, HT * N:HT * N + B * VW]
        we = arena2[:, 0:width("we")]
        Xq, Xk, Xv, Xo = (we[:, k * 1024:(k + 1) * 1024] for k in range(4))
        at4 = [width("we")]

        def a4(n):
            t = arena2[:, at4[0]:at4[0] + n]
            at4[0] += n
            return t
        q4 = [lnbuf[:, j * N:(j + 1) * N] for j in range(2)]
        ks4 = [kT1, qT1]
        wts4 = [a4(H2 * T) for _ in range(2)]
        wtT4 = [a4(H2 * T) for _ in range(2)]
        o4 = [a4(H2 * K2) for _ in range(2)]
        oT4 = [a4(H2 * K2) for _ in range(2)]
        smax4 = [sb(f"smax4_{j}", [128, H2]) for j in range(2)]
        rz4 = [sb(f"rz4_{j}", [128, H2]) for j in range(2)]

        RW = 8
        wring = heads(arena1[:, 0:RW * 1024], RW, 1024)
        w1r = [arena1[:, k * 1024:k * 1024 + F2] for k in range(RW)]
        w2r = [arena1[:, k * 1024 + F2:(k + 1) * 1024] for k in range(RW)]
        at5 = [RW * 1024]

        def a5(n):
            t = arena1[:, at5[0]:at5[0] + n]
            at5[0] += n
            return t
        g5 = [heads(a5(B * E2), B, E2) for _ in range(8)]
        v5 = [a5(B) for _ in range(8)]
        idx5 = a5(B).bitcast(mybir.dt.uint32)
        zero5 = a5(128)
        xrest = [arena2[:, k * N:(k + 1) * N] for k in range(2)]
        xpart = arena2[:, 2 * N:2 * N + 3 * N // 2].bitcast(BF16)
        hot5 = [arena2[:, 4096 + k * SLOTS // 2:4096 + (k + 1) * SLOTS // 2].bitcast(BF16) for k in range(4)]
        dT5 = arena2[:, 7168:7168 + SLOTS]
        hT5 = [arena2[:, 8704 + k * FC * CAP:8704 + (k + 1) * FC * CAP] for k in range(2)]
        eo5 = arena2[0:CAP, 10240:10240 + E2 * D].rearrange("p (e d) -> p e d", e=E2)
        yg5 = arena2[:, 12288:12288 + N]
        final = arena2[:, 13312:13312 + N]
        slots_dram = nc.dram_tensor("slots_scratch", (SLOTS + 1, D), F32, kind="Internal").ap()

        block = ctx.enter_context(nc.Block())

        def pe_norm(pe, k):
            for h in range(2):
                pe.wait_ge(sem("x_ready"), 2 * k + h + 1)
                nc.tensor.matmul(P[:, 4 + h, :], mean128[:, :], half(xT, h), start=True, stop=True)\
                    .then_inc(sem("ln_mean"), 1)
            for h in range(2):
                pe.wait_ge(sem("ln_squared"), 2 * k + h + 1)
                nc.tensor.matmul(P[:, 6 + h, :], mean128[:, :], half(sq, h), start=True, stop=True)\
                    .then_inc(sem("ln_var"), 1)

        def act_norm(act, k):
            for h in range(2):
                act.wait_ge(sem("ln_centred"), 2 * k + h + 1)
                nc.scalar.activation(half(sq, h), half(xc, h), ACT.Square).then_inc(sem("ln_squared"), 1)
            for h in range(2):
                act.wait_ge(sem("ln_var"), 2 * k + h + 1)
                nc.scalar.activation(half(sq, h), P[:, 6 + h, :], ACT.Sqrt, bias=eps[:, :])\
                    .then_inc(sem("ln_std"), 1)

        def dve_norm(dve, k):
            for h in range(2):
                dve.wait_ge(sem("ln_mean"), 2 * k + h + 1)
                nc.vector.tensor_tensor(half(xc, h), half(xT, h), P[:, 4 + h, :], ALU.subtract)\
                    .then_inc(sem("ln_centred"), 1)
            for h in range(2):
                dve.wait_ge(sem("ln_std"), 2 * k + h + 1)
                nc.vector.reciprocal(half(sq, h), half(sq, h)).then_inc(sem("ln_rstd"), 1)
                dve.wait_ge(sem("ln_rstd"), 2 * k + h + 1)
                nc.vector.tensor_tensor(half(xn, h), half(xc, h), half(sq, h), ALU.mult)\
                    .then_inc(sem("xn_ready"), 1)

        steps = [0]

        def chain(dve, ins):
            steps[0] += 1
            ins.then_inc(sem("dve_step"), 1)
            dve.wait_ge(sem("dve_step"), steps[0])

        UNITS = [(cc, h) for cc in range(C0) for h in range(2)]

        def pe_stage0(pe):
            pe_norm(pe, 0)
            pe.wait_ge(sem("wa_loaded"), 16)
            for h in range(2):
                pe.wait_ge(sem("xn_ready"), h + 1)
                nc.tensor.matmul(P[0:R0, h, :], w("wa", "r1_w"), half(xn, h), start=True, stop=True)\
                    .then_inc(sem("r_hidden"), 1)
            for h in range(2):
                pe.wait_ge(sem("r_biased"), h + 1)
                nc.tensor.matmul(P[0:R0, 2 + h, :], mean64[:, :], half(rh, h), start=True, stop=True)\
                    .then_inc(sem("r_mean"), 1)
            for h in range(2):
                pe.wait_ge(sem("r_squared"), h + 1)
                nc.tensor.matmul(P[0:R0, 4 + h, :], mean64[:, :], half(rs, h), start=True, stop=True)\
                    .then_inc(sem("r_var"), 1)
            LGT = heads(P[:, 0, 0:B * E0], B, E0)
            for b in range(B):
                if b % HB == 0:
                    pe.wait_ge(sem("r_act"), b // HB + 1)
                mm = nc.tensor.matmul(LGT[:, b, :], rg[:, b * T:(b + 1) * T], w("wa", "r2_w", R0),
                                      start=True, stop=True)
            mm.then_inc(sem("logits"), 1)
            pe.wait_ge(sem("probs"), 1)
            for b in range(B):
                mm = nc.tensor.transpose(P[0:E0, 2 + b // HB, (b % HB) * T:(b % HB + 1) * T], lg[11][:, b, :], ident)
                if b % HB == HB - 1:
                    mm.then_inc(sem("probs_turned"), 1)

            def down(u):
                cc, h = UNITS[u]
                pe.wait_ge(sem("e_weighted"), u + 1)
                nc.tensor.matmul(P[:, 6 + h, :], W2[:, cc, :], wact0[u % 3], start=(cc == 0), stop=False)\
                    .then_inc(sem("e_used"), 1)
            for u, (cc, h) in enumerate(UNITS):
                if u == 0:
                    pe.wait_ge(sem("probs_copied"), 2)
                if u >= 3:
                    pe.wait_ge(sem("e_act"), u - 2)
                nc.tensor.matmul(P[:, u % 3, :], W1[:, cc, :], half(xn, h), start=True, stop=True)\
                    .then_inc(sem("e_hidden"), 1)
                if u >= 3:
                    pe.wait_ge(sem("e_weighted"), u - 2)
                nc.tensor.matmul(P[:, 3 + u % 3, :], SEL[:, cc, :], half(probsT, h), start=True, stop=True)\
                    .then_inc(sem("e_prob"), 1)
                if u >= 2:
                    down(u - 2)
            down(len(UNITS) - 2)
            down(len(UNITS) - 1)
            for h in range(2):
                nc.tensor.matmul(P[:, 6 + h, :], w("wa", "b2", E0), half(probsT, h), start=False, stop=True)\
                    .then_inc(sem("stage_out"), 1)

        def act_stage0(act):
            act_norm(act, 0)
            for h in range(2):
                act.wait_ge(sem("r_hidden"), h + 1)
                nc.scalar.activation(half(rh, h), P[0:R0, h, :], ACT.Identity, bias=col("r1_b", R0))\
                    .then_inc(sem("r_biased"), 1)
            for h in range(2):
                act.wait_ge(sem("r_centred"), h + 1)
                nc.scalar.activation(half(rs, h), half(rc, h), ACT.Square).then_inc(sem("r_squared"), 1)
            for h in range(2):
                act.wait_ge(sem("r_var"), h + 1)
                nc.scalar.activation(half(rs, h), P[0:R0, 4 + h, :], ACT.Sqrt, bias=eps[0:R0, :])\
                    .then_inc(sem("r_std"), 1)
            for h in range(2):
                act.wait_ge(sem("r_normed"), h + 1)
                nc.scalar.activation(half(rg, h), half(rg, h), ACT.Gelu, bias=col("ln_b", R0),
                                     scale=col("ln_g", R0)).then_inc(sem("r_act"), 1)
            act.wait_ge(sem("route_shift"), 1)
            nc.scalar.activation(lg[3], lg[2], ACT.Exp).then_inc(sem("route_exp"), 1)
            for h in range(2):
                act.wait_ge(sem("probs_turned"), h + 1)
                nc.scalar.copy(half(probsT, h), P[0:E0, 2 + h, :]).then_inc(sem("probs_copied"), 1)

            def unit(u, fn, lo, hi, last=True):
                cc, h = UNITS[u]
                ins = nc.scalar.activation(act0[u % 3][lo:hi, :], P[lo:hi, u % 3, :], fn,
                                           bias=col("b1")[lo:hi, cc:cc + 1])
                if last:
                    ins.then_inc(sem("e_act"), 1)
            for u, (cc, h) in enumerate(UNITS):
                if cc == MIXED and h == 1:
                    continue
                act.wait_ge(sem("e_hidden"), u + 1 + (cc == MIXED))
                if u >= 3:
                    act.wait_ge(sem("e_weighted"), u - 2 + (cc == MIXED))
                if cc == MIXED:
                    unit(u, ACT.Gelu, 0, 64, False)
                    unit(u + 1, ACT.Gelu, 0, 64, False)
                    unit(u, ACT.Silu, 64, 128)
                    unit(u + 1, ACT.Silu, 64, 128)
                else:
                    unit(u, ACT.Gelu if cc < MIXED else ACT.Silu, 0, 128)

        def dve_stage0(dve):
            dve_norm(dve, 0)
            for h in range(2):
                dve.wait_ge(sem("r_mean"), h + 1)
                nc.vector.tensor_tensor(half(rc, h), half(rh, h), P[0:R0, 2 + h, :], ALU.subtract)\
                    .then_inc(sem("r_centred"), 1)
            for h in range(2):
                dve.wait_ge(sem("r_std"), h + 1)
                chain(dve, nc.vector.reciprocal(half(rs, h), half(rs, h)))
                nc.vector.tensor_tensor(half(rg, h), half(rc, h), half(rs, h), ALU.mult)\
                    .then_inc(sem("r_normed"), 1)
            LGT = heads(P[:, 0, 0:B * E0], B, E0)

            def row(name):
                return col(name).unsqueeze(1).broadcast_to([128, B, E0])

            def per_token(i):
                return red[i].broadcast_to([128, B, E0])
            prio = c("prio6").unsqueeze(1).broadcast_to([128, B, E0])
            chain(dve, nc.vector.reciprocal(rtemp, col("temp")))
            dve.wait_ge(sem("logits"), 1)
            chain(dve, nc.vector.tensor_tensor(lg[0], LGT, row("r2_b"), ALU.add))
            chain(dve, nc.vector.scalar_tensor_tensor(lg[1], lg[0], rtemp, row("route"), ALU.mult, ALU.add))
            chain(dve, nc.vector.tensor_reduce(red[0], lg[1], AX, ALU.max))
            nc.vector.tensor_tensor(lg[2], lg[1], per_token(0), ALU.subtract).then_inc(sem("route_shift"), 1)
            dve.wait_ge(sem("route_exp"), 1)
            chain(dve, nc.vector.tensor_reduce(red[1], lg[3], AX, ALU.add))
            chain(dve, nc.vector.reciprocal(red[1], red[1]))
            chain(dve, nc.vector.tensor_tensor(lg[4], lg[3], per_token(1), ALU.mult))
            src = lg[4]
            for r in range(2):
                hit, mark, best = lg[5 + r], lg[7 + r], lg[9 + r]
                chain(dve, nc.vector.tensor_reduce(red[2 + r], src, AX, ALU.max))
                chain(dve, nc.vector.tensor_tensor(hit, src, per_token(2 + r), ALU.is_equal))
                chain(dve, nc.vector.tensor_tensor(mark, hit, prio, ALU.mult))
                chain(dve, nc.vector.tensor_reduce(red[4 + r], mark, AX, ALU.max))
                chain(dve, nc.vector.tensor_tensor(best, mark, per_token(4 + r), ALU.is_equal))
                if r == 0:
                    chain(dve, nc.vector.scalar_tensor_tensor(lg[2], best, -2.0, src, ALU.mult, ALU.add))
                    src = lg[2]
            chain(dve, nc.vector.tensor_tensor(lg[5], lg[9], lg[10], ALU.add))
            nc.vector.tensor_tensor(lg[11], lg[4], lg[5], ALU.mult).then_inc(sem("probs"), 1)
            for u, (cc, h) in enumerate(UNITS):
                dve.wait_ge(sem("e_act"), u + 1)
                dve.wait_ge(sem("e_prob"), u + 1)
                if u >= 3:
                    dve.wait_ge(sem("e_used"), u - 2)
                nc.vector.tensor_tensor(wact0[u % 3], act0[u % 3], P[:, 3 + u % 3, :], ALU.mult)\
                    .then_inc(sem("e_weighted"), 1)
            for h in range(2):
                dve.wait_ge(sem("stage_out"), h + 1)
                nc.vector.tensor_tensor(half(xT, h), half(xT, h), P[:, 6 + h, :], ALU.add)\
                    .then_inc(sem("x_ready"), 1)

        V1v = V1[:, :].rearrange("p (b h k) -> p b h k", b=B, h=H1)

        def pe_keys1(pe):
            pe.wait_ge(sem("wb_loaded"), 16)
            pe.wait_ge(sem("x_ready"), 2)
            for h in range(2):
                pe.wait_ge(sem("ctx_ready"), h + 1)
                nc.tensor.matmul(P[:, h, :], w("wb", "Wk"), half(ctxT, h), start=True, stop=True)\
                    .then_inc(sem("k1_made"), 1)
            for b in range(B):
                mm = nc.tensor.matmul(P[:, 2 + b // HB, (b % HB) * D:(b % HB + 1) * D],
                                      ctxT[:, b * T:(b + 1) * T], w("wb", "Wv"), start=True, stop=True)
            mm.then_inc(sem("v1_made"), 1)
            pe.wait_ge(sem("k1_ready"), 2)
            pe.wait_ge(sem("v1_ready"), 1)

        def act_keys1(act):
            for h in range(2):
                act.wait_ge(sem("k1_made"), h + 1)
                nc.scalar.activation(half(kT1, h), P[:, h, :], ACT.Identity, bias=col("bk"))\
                    .then_inc(sem("k1_ready"), 1)

        def dve_keys1(dve):
            nc.vector.memset(V1[:, :], 1.0).then_inc(sem("v1_ones"), 1)
            dve.wait_ge(sem("v1_made"), 1)
            dve.wait_ge(sem("v1_ones"), 1)
            for h in range(2):
                ins = nc.vector.tensor_tensor(
                    V1v[:, h * HB:(h + 1) * HB, :, 0:K1],
                    P[:, 2 + h, :].rearrange("p (b h k) -> p b h k", b=HB, h=H1),
                    heads(col("bv"), H1, K1).unsqueeze(1).broadcast_to([128, HB, H1, K1]), ALU.add)
            dve.drain().then_inc(sem("v1_ready"), 1)

        def pool_stage0(pool):
            pool.wait_ge(sem("consts_loaded"), 16)
            pool.wait_ge(sem("k1_ready"), 2)
            with pool.Fori(0, B) as b:
                nc.gpsimd.tensor_tensor(
                    heads(Kexp[:, bass.ds(b * HTK, HTK)], H1, T),
                    kT1[:, bass.ds(b * T, T)].unsqueeze(1).broadcast_to([128, H1, T]),
                    c("head").unsqueeze(2).broadcast_to([128, H1, T]), ALU.mult)
            pool.drain().then_inc(sem("k1_spread"), 1)

        def pool_stage1(pool):
            pool.wait_ge(sem("q1_ready"), 2)
            with pool.Fori(0, B // 2) as i:
                for j in range(2):
                    pool.wait_ge(sem("s1_scored"), 2 * i + j + 1)
                    nc.gpsimd.tensor_copy(qs1[j][:, :], qT1[:, bass.ds(2 * i * T + j * T, T)])\
                        .then_inc(sem("s1_staged"), 1)
            pool.wait_ge(sem("wc_loaded"), 16)
            n = 0
            for src, dst in ((w("wc", "fw1"), fw1q[:, :]), (w("wc", "fw2"), fw2q[:, :])):
                nc.gpsimd.tensor_scalar(ftmp[0][:, :], src, 64.0, 127.0, ALU.mult, ALU.min)\
                    .then_inc(sem("fw_step"), 1)
                pool.wait_ge(sem("fw_step"), n + 1)
                nc.gpsimd.tensor_scalar(ftmp[1][:, :], ftmp[0][:, :], -128.0, ROUND, ALU.max, ALU.add)\
                    .then_inc(sem("fw_step"), 1)
                pool.wait_ge(sem("fw_step"), n + 2)
                nc.gpsimd.tensor_scalar(dst, ftmp[1][:, :], ROUND, None, ALU.subtract).then_inc(sem("fw_step"), 1)
                pool.wait_ge(sem("fw_step"), n + 3)
                n += 3
            nb = QC + 1
            fb = packs["small"][:, FB_AT:FB_AT + nb]
            nc.gpsimd.tensor_scalar(ftmp[0][:, 0:nb], fb, 64.0, 127.0, ALU.mult, ALU.min).then_inc(sem("fw_step"), 1)
            pool.wait_ge(sem("fw_step"), n + 1)
            nc.gpsimd.tensor_scalar(ftmp[1][:, 0:nb], ftmp[0][:, 0:nb], -128.0, ROUND, ALU.max, ALU.add)\
                .then_inc(sem("fw_step"), 1)
            pool.wait_ge(sem("fw_step"), n + 2)
            nc.gpsimd.tensor_scalar(fbq[:, 0:QC], ftmp[1][:, 0:QC], ROUND, 16.0 / 64, ALU.subtract, ALU.mult)
            nc.gpsimd.tensor_scalar(fbq[:, QC:nb], ftmp[1][:, QC:nb], ROUND, 1.0 / 64, ALU.subtract, ALU.mult)
            pool.drain().then_inc(sem("fw_ready"), 1)

        RING = 2

        def pe_stage1(pe):
            pe_norm(pe, 1)
            for h in range(2):
                pe.wait_ge(sem("xn_ready"), 2 + h + 1)
                nc.tensor.matmul(P[:, h, :], w("wb", "Wq"), half(xn, h), start=True, stop=True)\
                    .then_inc(sem("q1_made"), 1)
            pe.sem_inc(sem("s1_scored"), RING)
            pe.wait_ge(sem("q1_ready"), 2)
            pe.wait_ge(sem("k1_spread"), 1)
            with pe.Fori(0, B // 2) as i:
                for j in range(2):
                    pe.wait_ge(sem("s1_staged"), 2 * i + j + 1)
                    pe.wait_ge(sem("s1_shifted"), 2 * i + j + 1)
                    for g in range(4):
                        mm = nc.tensor.matmul(P[:, 4 * j + g, :], qs1[j][:, :],
                                              Kexp[:, bass.ds(2 * i * HTK + j * HTK + g * 512, 512)],
                                              start=True, stop=True)
                    mm.then_inc(sem("s1_scored"), 1)
            pe.wait_ge(sem("s1_shifted"), B + RING)
            pe.wait_ge(sem("feat_rows"), 1)
            for f, row in enumerate((simrow1, max1[:, :], ent1)):
                mm = nc.tensor.matmul(P[0:3, 0, 0:BH], featw[:, f, :], row, start=(f == 0), stop=(f == 2))
            mm.then_inc(sem("feats"), 1)
            pe.wait_ge(sem("feats_copied"), 1)
            nc.tensor.matmul(P[0:M1, 1, 0:BH], w("wb", "mw1", 3), feats1, start=True, stop=True)\
                .then_inc(sem("mlp_made"), 1)
            pe.wait_ge(sem("mlp_act"), 1)
            nc.tensor.matmul(P[0:M1, 2, 0:BH], w("wb", "mw2", M1), hid1, start=True, stop=True)\
                .then_inc(sem("mlp_made"), 1)
            pe.wait_ge(sem("mlp_act"), 2)
            nc.tensor.matmul(P[:, 3, 0:BH], w("wb", "mw3", M1), hid2, start=True, stop=True)\
                .then_inc(sem("mlp_made"), 1)
            pe.wait_ge(sem("logt"), 1)
            pe.sem_inc(sem("s2_mixed"), RING)
            with pe.Fori(0, B // 2) as i:
                for j in range(2):
                    pe.wait_ge(sem("s2_exp"), 2 * i + j + 1)
                    for g in range(4):
                        freed = sem("s2_evac_a") if g % 2 == 0 else sem("s2_evac_d")
                        pe.wait_ge(freed, 4 * i + 2 * j + g // 2 + 1)
                        for k in range(4):
                            h = 4 * g + k
                            mm = nc.tensor.transpose(P[:, g, k * T:(k + 1) * T], wts1[j][:, h * T:(h + 1) * T], ident)
                        mm.then_inc(sem("s2_turned"), 1)
                for j in range(2):
                    pe.wait_ge(sem("s2_evac_a"), 4 * i + 2 * j + 2 + 2)
                    pe.wait_ge(sem("s2_evac_d"), 4 * i + 2 * j + 2 + 2)
                    pe.wait_ge(sem("s2_normed"), 2 * i + j + 1)
                    for h in range(H1):
                        mm = nc.tensor.matmul(P[:, 4 + j, h * (K1 + 1):(h + 1) * (K1 + 1)],
                                              wtT1[j][:, h * T:(h + 1) * T],
                                              V1[:, bass.ds(2 * i * H1 * 9 + j * H1 * 9 + h * 9, 9)],
                                              start=True, stop=True)
                    mm.then_inc(sem("s2_mixed"), 1)
                for j in range(2):
                    pe.wait_ge(sem("s2_normed"), 2 * i + j + 1 + RING)
                    pe.wait_ge(sem("s2_kept"), 2 * i + j + 1)
                    nc.tensor.transpose(P[:, 6 + j, 0:T], o1[j], ident).then_inc(sem("s2_oturned"), 1)
            for h in range(2):
                pe.wait_ge(sem("s2_kept"), RING + B)
                nc.tensor.matmul(P[:, h, :], w("wb", "Wo"), half(oT1, h), start=True, stop=True)\
                    .then_inc(sem("stage_out"), 1)

        def act_stage1(act):
            act_norm(act, 1)
            for h in range(2):
                act.wait_ge(sem("q1_made"), h + 1)
                nc.scalar.activation(half(qT1, h), P[:, h, :], ACT.Identity, bias=col("bq"))\
                    .then_inc(sem("q1_ready"), 1)
            with act.Fori(0, B // 2) as i:
                for j in range(2):
                    act.wait_ge(sem("s1_shifted"), 2 * i + j + 1 + RING)
                    act.wait_ge(sem("s1_stats"), 2 * i + j + 1)
                    nc.scalar.activation(exp1[j], Dall[:, bass.ds(2 * i * HTK + j * HTK, HTK)], ACT.Exp, scale=SC1)\
                        .then_inc(sem("s1_exp"), 1)
            act.wait_ge(sem("mlp_made"), 1)
            nc.scalar.activation(hid1, P[0:M1, 1, 0:BH], ACT.Gelu, bias=col("m1", M1)).then_inc(sem("mlp_act"), 1)
            act.wait_ge(sem("mlp_made"), 2)
            nc.scalar.activation(hid2, P[0:M1, 2, 0:BH], ACT.Gelu, bias=col("m2", M1)).then_inc(sem("mlp_act"), 1)
            act.wait_ge(sem("logt"), 1)
            nc.scalar.activation(temper1, logt1, ACT.Exp, scale=-1.0).then_inc(sem("temper"), 1)
            act.sem_inc(sem("s2_evac_a"), 2)
            act.sem_inc(sem("s2_kept"), RING)
            with act.Fori(0, B // 2) as i:
                for j in range(2):
                    act.wait_ge(sem("s2_scaled"), 2 * i + j + 1)
                    nc.scalar.activation(wts1[j], wts1[j], ACT.Exp).then_inc(sem("s2_exp"), 1)
                for j in range(2):
                    act.wait_ge(sem("s2_mixed"), 2 * i + j + 1)
                    for g in (0, 2):
                        act.wait_ge(sem("s2_turned"), 8 * i + 4 * j + g + 1)
                        nc.scalar.copy(wtT1[j][:, g * 512:(g + 1) * 512], P[:, g, :]).then_inc(sem("s2_evac_a"), 1)
                for j in range(2):
                    act.wait_ge(sem("s2_oturned"), 2 * i + j + 1)
                    nc.scalar.copy(oT1[:, bass.ds(2 * i * T + j * T, T)], P[:, 6 + j, 0:T]).then_inc(sem("s2_kept"), 1)

        def dve_stage1(dve):
            dve_norm(dve, 1)
            dve.sem_inc(sem("s1_shifted"), RING)
            dve.sem_inc(sem("s1_stats"), RING)
            with dve.Fori(0, B // 2) as i:
                for j in range(2):
                    dve.wait_ge(sem("s1_scored"), 2 * i + j + 1 + RING)
                    S = P[:, 4 * j:4 * j + 4, :].rearrange("p g (h k) -> p (g h) k", k=T)
                    nc.vector.tensor_reduce(smax1[j][:, :], S, AX, ALU.max).then_inc(sem("s1_max"), 1)
                    dve.wait_ge(sem("s1_max"), 2 * i + j + 1)
                    nc.vector.tensor_copy(max1[:, bass.ds(2 * i * H1 + j * H1, H1)], smax1[j][:, :])
                    nc.vector.tensor_tensor(heads(Dall[:, bass.ds(2 * i * HTK + j * HTK, HTK)], H1, T), S,
                                            smax1[j][:, :].unsqueeze(2).broadcast_to([128, H1, T]), ALU.subtract)\
                        .then_inc(sem("s1_shifted"), 1)
                for j in range(2):
                    dve.wait_ge(sem("s1_exp"), 2 * i + j + 1)
                    for h in range(H1):
                        bn = nc.vector.bn_stats(st1[j][:, h, :], exp1[j][:, h * T:(h + 1) * T])
                    bn.then_inc(sem("s1_bn"), 1)
                    dve.wait_ge(sem("s1_bn"), 2 * i + j + 1)
                    nc.vector.tensor_copy(stats1[:, bass.ds(2 * i * H1 + j * H1, H1), :], st1[j][:, :, :])\
                        .then_inc(sem("s1_stats"), 1)
            dve.wait_ge(sem("s1_stats"), B + RING)
            me, ve, mo, vo = stats1[:, :, 1], stats1[:, :, 2], stats1[:, :, 4], stats1[:, :, 5]
            chain(dve, nc.vector.tensor_tensor(tmp1[0], me, mo, ALU.subtract))
            chain(dve, nc.vector.tensor_tensor(tmp1[0], tmp1[0], tmp1[0], ALU.mult))
            chain(dve, nc.vector.tensor_tensor(tmp1[1], ve, vo, ALU.add))
            chain(dve, nc.vector.scalar_tensor_tensor(tmp1[2], tmp1[0], T / 4.0, tmp1[1], ALU.mult, ALU.add))
            chain(dve, nc.vector.tensor_tensor(tmp1[3], me, mo, ALU.add))
            chain(dve, nc.vector.reciprocal(tmp1[4], tmp1[3]))
            chain(dve, nc.vector.tensor_tensor(tmp1[5], tmp1[2], tmp1[4], ALU.mult))
            chain(dve, nc.vector.scalar_tensor_tensor(ent1, tmp1[5], 4.0 / T / T / (T - 1), tmp1[4], ALU.mult, ALU.mult))
            chain(dve, nc.vector.tensor_reduce(qsum1, heads(qT1[:, :], B, T), AX, ALU.add))
            chain(dve, nc.vector.tensor_reduce(ksum1, heads(kT1[:, :], B, T), AX, ALU.add))
            chain(dve, nc.vector.tensor_tensor(sim1, qsum1, ksum1, ALU.mult))
            chain(dve, nc.vector.tensor_tensor(heads(simrow1, B, H1), sim1.unsqueeze(2).broadcast_to([128, B, H1]),
                                          c("head").unsqueeze(1).broadcast_to([128, B, H1]), ALU.mult))
            chain(dve, nc.vector.memset(featw, 0.0))
            chain(dve, nc.vector.memset(featw[:, 0, 0:1], SC1 / T / T))
            chain(dve, nc.vector.memset(featw[:, 1, 1:2], SC1 / T))
            nc.vector.memset(featw[:, 2, 2:3], 1.0 / T).then_inc(sem("feat_rows"), 1)
            dve.wait_ge(sem("feats"), 1)
            nc.vector.tensor_copy(feats1, P[0:3, 0, 0:BH]).then_inc(sem("feats_copied"), 1)
            dve.wait_ge(sem("mlp_made"), 3)
            chain(dve, nc.vector.tensor_scalar(logt1, P[:, 3, 0:BH], col("b3"), LOG_T_MIN, ALU.add, ALU.max))
            nc.vector.tensor_scalar(logt1, logt1, LOG_T_MAX, None, ALU.min).then_inc(sem("logt"), 1)
            dve.wait_ge(sem("temper"), 1)
            chain(dve, nc.vector.tensor_scalar(cool1, temper1, 0.5, None, ALU.mult))
            dve.sem_inc(sem("s2_evac_d"), 2)
            dve.sem_inc(sem("s2_normed"), RING)
            with dve.Fori(0, B // 2) as i:
                for j in range(2):
                    dve.wait_ge(sem("s2_mixed"), 2 * i + j + 1)
                    nc.vector.tensor_tensor(
                        heads(wts1[j], H1, T), heads(Dall[:, bass.ds(2 * i * HTK + j * HTK, HTK)], H1, T),
                        cool1[:, bass.ds(2 * i * H1 + j * H1, H1)].unsqueeze(2).broadcast_to([128, H1, T]), ALU.mult)\
                        .then_inc(sem("s2_scaled"), 1)
                for j in range(2):
                    for g in (1, 3):
                        dve.wait_ge(sem("s2_turned"), 8 * i + 4 * j + g + 1)
                        nc.vector.tensor_copy(wtT1[j][:, g * 512:(g + 1) * 512], P[:, g, :])\
                            .then_inc(sem("s2_evac_d"), 1)
                for j in range(2):
                    dve.wait_ge(sem("s2_mixed"), 2 * i + j + 1 + RING)
                    O = P[:, 4 + j, 0:H1 * (K1 + 1)].rearrange("p (h k) -> p h k", h=H1)
                    nc.vector.reciprocal(rz1[j], O[:, :, K1]).then_inc(sem("s2_rz"), 1)
                    nc.vector.memset(o1[j], 0.0).then_inc(sem("s2_rz"), 1)
                    dve.wait_ge(sem("s2_rz"), 8 * i + 4 * j + 2)
                    nc.vector.tensor_tensor(heads(raw1[j], H1, K1), O[:, :, 0:K1],
                                            rz1[j].unsqueeze(2).broadcast_to([128, H1, K1]), ALU.mult)\
                        .then_inc(sem("s2_rz"), 1)
                    dve.wait_ge(sem("s2_rz"), 8 * i + 4 * j + 3)
                    nc.vector.tensor_tensor(same1[j], raw1[j], raw1[j], ALU.is_equal).then_inc(sem("s2_rz"), 1)
                    dve.wait_ge(sem("s2_rz"), 8 * i + 4 * j + 4)
                    dve.sem_inc(sem("s2_guarded"), 1)
                    nc.vector.copy_predicated(o1[j], same1[j], raw1[j]).then_inc(sem("s2_normed"), 1)
            for h in range(2):
                dve.wait_ge(sem("stage_out"), 2 + h + 1)
                nc.vector.scalar_tensor_tensor(half(xT, h), P[:, h, :], col("bo"), half(xT, h), ALU.add, ALU.add)\
                    .then_inc(sem("x_ready"), 1)

        def pe_stage2(pe):
            pe_norm(pe, 2)
            pe.wait_ge(sem("fw_ready"), 1)

            def down(h):
                for cc in range(QC):
                    u = QC * h + cc
                    pe.wait_ge(sem("f_quant"), u + 1)
                    mm = nc.tensor.matmul(P[:, 4 + h, :], fw2q[:, cc * 128:(cc + 1) * 128], hq[:, u, :],
                                          start=(cc == 0), stop=(cc == QC - 1))
                mm.then_inc(sem("stage_out"), 1)
            for h in range(2):
                pe.wait_ge(sem("f_xq"), h + 1)
                for cc in range(QC):
                    u = QC * h + cc
                    if u >= 4:
                        pe.wait_ge(sem("f_copied"), u - 3)
                    nc.tensor.matmul(P[:, u % 4, :], fw1q[:, cc * 128:(cc + 1) * 128], half(xq, h),
                                     start=True, stop=True).then_inc(sem("f_hidden"), 1)
            down(0)
            down(1)

        def act_stage2(act):
            act_norm(act, 2)
            act.wait_ge(sem("fw_ready"), 1)
            for u in range(2 * QC):
                act.wait_ge(sem("f_hidden"), u + 1)
                if u >= 2:
                    act.wait_ge(sem("f_clipped"), u - 1)
                nc.scalar.activation(hraw[u % 2], P[:, u % 4, :], ACT.Identity, scale=1.0 / 64,
                                     bias=fbq[:, u % QC:u % QC + 1]).then_inc(sem("f_copied"), 1)

        def dve_stage2(dve):
            dve_norm(dve, 2)
            n = 0
            for h in range(2):
                dve.wait_ge(sem("xn_ready"), 4 + h + 1)
                nc.vector.tensor_scalar(half(xr, h), half(xn, h), 16.0, 127.0, ALU.mult, ALU.min)\
                    .then_inc(sem("f_step"), 1)
                dve.wait_ge(sem("f_step"), n + 1)
                nc.vector.tensor_scalar(half(xr, h), half(xr, h), -128.0, ROUND, ALU.max, ALU.add)\
                    .then_inc(sem("f_step"), 1)
                dve.wait_ge(sem("f_step"), n + 2)
                nc.vector.tensor_scalar(half(xq, h), half(xr, h), ROUND, None, ALU.subtract)\
                    .then_inc(sem("f_xq"), 1)
                n += 2
            for u in range(2 * QC):
                dve.wait_ge(sem("f_copied"), u + 1)
                nc.vector.tensor_scalar(hclip[u % 2], hraw[u % 2], 127.0, 0.0, ALU.min, ALU.max)\
                    .then_inc(sem("f_clipped"), 1)
                dve.wait_ge(sem("f_clipped"), u + 1)
                nc.vector.tensor_scalar(hq[:, u, :], hclip[u % 2], ROUND, ROUND, ALU.add, ALU.subtract)\
                    .then_inc(sem("f_quant"), 1)
            for h in range(2):
                dve.wait_ge(sem("stage_out"), 4 + h + 1)
                nc.vector.tensor_scalar(half(yq, h), P[:, 4 + h, :], 1.0 / 1024, fbq[:, QC:QC + 1],
                                        ALU.mult, ALU.add).then_inc(sem("f_out"), 1)
                dve.wait_ge(sem("f_out"), h + 1)
                nc.vector.tensor_tensor(half(xT, h), half(xT, h), half(yq, h), ALU.add)\
                    .then_inc(sem("x_ready"), 1)

        def sp_stage3(sp):
            sp.wait_ge(sem("dbl_copied"), 2)
            for k, r in enumerate((64, 0, 32)):
                sp.dma_start(scratch[k].rearrange("b s t -> s b t"), heads(dbl[r:r + NS, :], B, T))\
                    .then_inc(sem("dbl_stored"), 16)
            sp.wait_ge(sem("dbl_stored"), 48)
            for k, dst in enumerate((dtst, Bst, Cst)):
                sp.dma_start(dst, scratch[k].rearrange("b s t -> (b s) t")).then_inc(sem("states_loaded"), 16)

        def pe_stage3(pe):
            pe_norm(pe, 3)
            pe.wait_ge(sem("wd_loaded"), 16)
            for cc in range(2 * DC):
                for h in range(2):
                    u = 2 * cc + h
                    if u < 2:
                        pe.wait_ge(sem("xn_ready"), 6 + h + 1)
                    if u >= 4:
                        pe.wait_ge(sem("xz_copied"), u - 3)
                    nc.tensor.matmul(P[:, u % 4, :], w("wd", "Win")[:, cc * 128:(cc + 1) * 128], half(xn, h),
                                     start=True, stop=True).then_inc(sem("xz_made"), 1)
            pe.wait_ge(sem("conv_act"), DC)
            pe.wait_ge(sem("ln_rstd"), 8)
            for h in range(2):
                for cc in range(DC):
                    mm = nc.tensor.matmul(P[0:80, 4 + h, :], w("wd", "Wx")[:, cc * 80:(cc + 1) * 80],
                                          xcv[:, cc * N + h * HALF:cc * N + (h + 1) * HALF],
                                          start=(cc == 0), stop=(cc == DC - 1))
                mm.then_inc(sem("dbl_made"), 1)
            pe.wait_ge(sem("xz_copied"), 4 * DC)

            def turn_back(g):
                pe.wait_ge(sem("ysum_copied"), g + 1)
                if g:
                    pe.wait_ge(sem("y3_copied"), g)
                for cc in range(DC):
                    mm = nc.tensor.transpose(P[:, 6, cc * 128:(cc + 1) * 128],
                                             ysum3[g % 2][:, cc * 128:(cc + 1) * 128], ident)
                mm.then_inc(sem("ysum_turned"), 1)

            def spread(t):
                if t >= LOOK:
                    pe.wait_ge(sem("u_made"), t - LOOK + 1)
                if by_act(t):
                    pe.wait_ge(sem("x_repeated_a"), t // 3 + 1)
                else:
                    pe.wait_ge(sem("x_repeated_p"), t - (t + 1) // 3 + 1)
                for cc in range(DC):
                    mm = nc.tensor.transpose(P[:, t % LOOK, cc * 128:(cc + 1) * 128],
                                             xe3[t % LOOK][:, cc * 128:(cc + 1) * 128], ident)
                mm.then_inc(sem("x_spread"), 1)
            for t in range(LOOK):
                spread(t)
            for t in range(T):
                if t == 0:
                    pe.wait_ge(sem("dbl_copied"), 2)
                g, k = divmod(t, STEPS)
                if k == 0 and g >= 2:
                    pe.wait_ge(sem("ysum_copied"), g - 1)
                if k % PLACED == 0:
                    pe.wait_ge(sem("c_placed"), t // PLACED + 1 + 1)
                pe.wait_ge(sem("h_clipped"), DC * (t + 1))
                nc.tensor.matmul(P[:, 4 + g % 2, 0:DI], Cpad[:, k * 128:(k + 1) * 128], h3[t % 4],
                                 start=(k == 0), stop=(k == STEPS - 1)).then_inc(sem("y_step"), 1)
                if t + LOOK < T:
                    spread(t + LOOK)
                if k == STEPS // 2 and g >= 1:
                    turn_back(g - 1)
            turn_back(T // STEPS - 1)
            pe.wait_ge(sem("y3_gated"), DC)
            for h in range(2):
                for cc in range(DC):
                    mm = nc.tensor.matmul(P[:, 6 + h, :], w("wd", "Wout")[:, cc * 128:(cc + 1) * 128],
                                          yg3[1][:, cc * N + h * HALF:cc * N + (h + 1) * HALF],
                                          start=(cc == 0), stop=(cc == DC - 1))
                mm.then_inc(sem("stage_out"), 1)

        def pool_stage3(pool):
            pool.wait_ge(sem("x_ready"), 8)
            nc.gpsimd.memset(Cpad, 0.0).then_inc(sem("c_placed"), 1)
            pool.wait_ge(sem("conv_act"), DC)
            for t in range(LOOK):
                if not by_act(t):
                    repeat(pool, nc.gpsimd.tensor_copy, t)
            pool.wait_ge(sem("c_placed"), 1)
            pool.wait_ge(sem("states_loaded"), 48)
            for n in range(STEPS // PLACED):
                place(pool, n)
            for t in range(LOOK, T):
                if not by_act(t):
                    repeat(pool, nc.gpsimd.tensor_copy, t)
                if t % PLACED == 0 and t >= STEPS:
                    place(pool, t // PLACED)

        def place(pool, n):
            if n >= STEPS // PLACED:
                pool.wait_ge(sem("y_step"), n * PLACED - STEPS + PLACED)
            k = n * PLACED % STEPS
            nc.gpsimd.tensor_tensor(Cdiag[:, k:k + PLACED, :],
                                    Cst[:, n * PLACED:(n + 1) * PLACED].unsqueeze(2).broadcast_to([128, PLACED, B]),
                                    c("batch").unsqueeze(1).broadcast_to([128, PLACED, B]), ALU.mult)\
                .then_inc(sem("c_placed"), 1)

        def by_act(t):
            return t % 3 == 2

        def repeat(eng, copy, t):
            if t >= LOOK:
                eng.wait_ge(sem("x_spread"), t - LOOK + 1)
            copy(xe3[t % LOOK].rearrange("p (m s) -> p m s", s=NS),
                 xcv.rearrange("p (m t) -> p m t", t=T)[:, :, t:t + 1].broadcast_to([128, DC * B, NS]))\
                .then_inc(sem("x_repeated_a" if by_act(t) else "x_repeated_p"), 1)

        def act_stage3(act):
            act_norm(act, 3)
            for cc in range(2 * DC):
                for h in range(2):
                    u = 2 * cc + h
                    act.wait_ge(sem("xz_made"), u + 1)
                    if cc < DC:
                        nc.scalar.copy(xpad[:, cc, h * HB:(h + 1) * HB, 3:PADT],
                                       P[:, u % 4, :].rearrange("p (b t) -> p b t", b=HB)).then_inc(sem("xz_copied"), 1)
                    else:
                        at = (cc - DC) * N + h * HALF
                        nc.scalar.activation(sz[:, at:at + HALF], P[:, u % 4, :], ACT.Silu)\
                            .then_inc(sem("xz_copied"), 1)
            for cc in range(DC):
                act.wait_ge(sem("conv_done"), cc + 1)
                nc.scalar.activation(xcv[:, cc * N:(cc + 1) * N].rearrange("p (b t) -> p b t", b=B),
                                     conv[1][:, cc, :, :], ACT.Silu).then_inc(sem("conv_act"), 1)
            for h in range(2):
                act.wait_ge(sem("dbl_made"), h + 1)
                nc.scalar.copy(half(dbl, h), P[0:80, 4 + h, :]).then_inc(sem("dbl_copied"), 1)
            act.wait_ge(sem("states_loaded"), 48)
            nc.scalar.activation(dstep[0], dtst, ACT.Exp).then_inc(sem("dt_exp"), 1)
            nc.scalar.activation(negA, col("alog"), ACT.Exp).then_inc(sem("dt_exp"), 1)
            act.wait_ge(sem("decay"), 1)
            nc.scalar.activation(Abar, dstep[3], ACT.Exp).then_inc(sem("abar"), 1)
            act.wait_ge(sem("bbar"), 1)
            repeat(act, nc.scalar.copy, 2)
            for t in range(T):
                act.wait_ge(sem("x_spread"), t + 1)
                if t >= LOOK:
                    act.wait_ge(sem("h_raw"), DC * (t - LOOK + 1))
                nc.scalar.activation(U3[t % LOOK], P[:, t % LOOK, 0:DI], ACT.Copy, scale=Bbar[:, t:t + 1])\
                    .then_inc(sem("u_made"), 1)
                if by_act(t + LOOK) and t + LOOK < T:
                    repeat(act, nc.scalar.copy, t + LOOK)
                g, k = divmod(t - STEPS, STEPS)
                if k == LOOK and g >= 0:
                    sums(act, g)
                if k == STEPS - LOOK and g >= 0:
                    collect(act, g)
            sums(act, T // STEPS - 1)
            collect(act, T // STEPS - 1)

        def sums(act, g):
            act.wait_ge(sem("y_step"), (g + 1) * STEPS)
            if g >= 2:
                act.wait_ge(sem("ysum_turned"), g - 1)
            nc.scalar.copy(ysum3[g % 2], P[:, 4 + g % 2, 0:DI]).then_inc(sem("ysum_copied"), 1)

        def collect(act, g):
            act.wait_ge(sem("ysum_turned"), g + 1)
            nc.scalar.copy(yT3.rearrange("p (c b t) -> p c b t", c=DC, b=B)[:, :, :, g * STEPS:(g + 1) * STEPS],
                           P[:, 6, 0:DI].rearrange("p (c t b) -> p c b t", c=DC, b=B))\
                .then_inc(sem("y3_copied"), 1)

        def dve_stage3(dve):
            dve_norm(dve, 3)
            chain(dve, nc.vector.memset(xpad[:, :, :, 0:3], 0.0))
            for cc in range(DC):
                dve.wait_ge(sem("xz_copied"), 2 * cc + 2)
                wv = col("conv_w")[:, 4 * cc:4 * cc + 4]
                chain(dve, nc.vector.tensor_scalar(conv[0][:, cc, :, :], xpad[:, cc, :, 0:T], wv[:, 0:1],
                                              col("conv_b")[:, cc:cc + 1], ALU.mult, ALU.add))
                for k in range(1, 4):
                    ins = nc.vector.scalar_tensor_tensor(conv[k % 2][:, cc, :, :], xpad[:, cc, :, k:k + T], wv[:, k:k + 1],
                                                         conv[(k + 1) % 2][:, cc, :, :], ALU.mult, ALU.add)
                    if k < 3:
                        chain(dve, ins)
                    else:
                        ins.then_inc(sem("conv_done"), 1)
            dve.wait_ge(sem("dt_exp"), 2)
            e, acc, tmp, dec = dstep
            chain(dve, nc.vector.tensor_scalar(e, e, 0.12, None, ALU.min))
            chain(dve, nc.vector.tensor_scalar(acc, e, -1.0 / 8, 1.0 / 7, ALU.mult, ALU.add))
            for k in range(6, 0, -1):
                chain(dve, nc.vector.tensor_tensor(tmp, acc, e, ALU.mult))
                chain(dve, nc.vector.tensor_scalar(acc, tmp, -1.0, 1.0 / k, ALU.mult, ALU.add))
            chain(dve, nc.vector.tensor_tensor(tmp, acc, e, ALU.mult))
            chain(dve, nc.vector.tensor_scalar(acc, tmp, DT_MIN, DT_MAX, ALU.max, ALU.min))
            chain(dve, nc.vector.tensor_scalar(tmp, acc, negA, -1.0, ALU.mult, ALU.mult))
            nc.vector.tensor_scalar(dec, tmp, -20.0, 0.0, ALU.max, ALU.min).then_inc(sem("decay"), 1)
            chain(dve, nc.vector.tensor_tensor(e, acc, Bst, ALU.mult))
            nc.vector.tensor_scalar(Bbar, e, -10.0, 10.0, ALU.max, ALU.min).then_inc(sem("bbar"), 1)
            chain(dve, nc.vector.memset(h3[3], 0.0))
            dve.wait_ge(sem("abar"), 1)
            for t in range(T):
                dve.wait_ge(sem("u_made"), t + 1)
                for cc in range(DC):
                    cs = slice(cc * 128, (cc + 1) * 128)
                    if t:
                        dve.wait_ge(sem("h_clipped"), DC * (t - 1) + cc + 1)
                    nc.vector.scalar_tensor_tensor(hraw3[t % 2][:, cs], h3[(t - 1) % 4][:, cs], Abar[:, t:t + 1],
                                                   U3[t % LOOK][:, cs], ALU.mult, ALU.add).then_inc(sem("h_raw"), 1)
                if t >= 4:
                    dve.wait_ge(sem("y_step"), t - 3)
                for cc in range(DC):
                    cs = slice(cc * 128, (cc + 1) * 128)
                    dve.wait_ge(sem("h_raw"), DC * t + cc + 1)
                    nc.vector.tensor_scalar(h3[t % 4][:, cs], hraw3[t % 2][:, cs], 100.0, -100.0, ALU.min, ALU.max)\
                        .then_inc(sem("h_clipped"), 1)
            dve.wait_ge(sem("y3_copied"), T // STEPS)
            for cc in range(DC):
                cs = slice(cc * N, (cc + 1) * N)
                chain(dve, nc.vector.tensor_tensor(yg3[0][:, cs], yT3[:, cs], sz[:, cs], ALU.mult))
                nc.vector.scalar_tensor_tensor(yg3[1][:, cs], xcv[:, cs], col("dskip")[:, cc:cc + 1], yg3[0][:, cs],
                                               ALU.mult, ALU.add).then_inc(sem("y3_gated"), 1)
            for h in range(2):
                dve.wait_ge(sem("stage_out"), 6 + h + 1)
                nc.vector.tensor_tensor(half(xT, h), half(xT, h), P[:, 6 + h, :], ALU.add)\
                    .then_inc(sem("x_ready"), 1)

        def slot_head(g, k):
            tile = 4 * (g // 2) + k
            return tile, 64 * (g % 2), 2 * tile + g % 2

        QBANK = (2, 7)
        OH = 6

        def pe_stage4(pe):
            pe.wait_ge(sem("we_loaded"), 16)
            pe.wait_ge(sem("y3_gated"), DC)
            pe.wait_ge(sem("x_ready"), 8 + 2)
            for u in range(4 * HT):
                if u >= 4:
                    pe.wait_ge(sem("kv_copied_a" if u % 2 == 0 else "kv_copied_d"), (u - 4) // 2 + 1)
                if u < 2 * HT:
                    nc.tensor.matmul(P[:, u % 4, :], Xk[:, (u // 2) * 128:(u // 2 + 1) * 128], half(ctxT, u % 2),
                                     start=True, stop=True).then_inc(sem("kv_made"), 1)
                else:
                    b, r = divmod(u - 2 * HT, 2)
                    nc.tensor.matmul(P[:, u % 4, :], ctxT[:, b * T:(b + 1) * T], Xv[:, r * 512:(r + 1) * 512],
                                     start=True, stop=True).then_inc(sem("kv_made"), 1)
            pe_norm(pe, 4)
            pe.wait_ge(sem("kv_copied_a"), 2 * HT)
            pe.wait_ge(sem("kv_copied_d"), 2 * HT)
            pe.wait_ge(sem("ln_rstd"), 10)
            pe.wait_ge(sem("xn_ready"), 10)
            pe.sem_inc(sem("s4_scored"), 8)

            def queries(i, k):
                for r in range(2):
                    if r == 0:
                        pe.wait_ge(sem("s4_evac_a"), 4 * i + 2 * k + 1)
                    else:
                        pe.wait_ge(sem("s4_added"), 2 * i + k)
                    for m in range(4):
                        tile = 4 * r + m
                        mm = nc.tensor.matmul(P[:, QBANK[r], m * T:(m + 1) * T], Xq[:, tile * 128:(tile + 1) * 128],
                                              xn[:, bass.ds(2 * i * T + k * T, T)], start=True, stop=True)
                    mm.then_inc(sem("q4_made"), 1)

            def scores(i, k, g):
                pe.wait_ge(sem("q4_ready"), 4 * i + 2 * k + g // 2 + 1)
                pe.wait_ge(sem("s4_shifted"), 8 * i + 4 * k + g + 1)
                if g == 0:
                    pe.wait_ge(sem("k4_staged"), 2 * i + k + 1)
                for m in range(4):
                    tile, row, _ = slot_head(g, m)
                    mm = nc.tensor.matmul(P[:, g % 2, m * T:(m + 1) * T],
                                          q4[k % 2][row:row + K2, tile * T:(tile + 1) * T],
                                          ks4[k % 2][row:row + K2, tile * T:(tile + 1) * T], start=True, stop=True)
                mm.then_inc(sem("s4_scored"), 1)

            def turn(i, k, g):
                freed = sem("s4_evac_a") if g % 2 == 0 else sem("s4_evac_d")
                pe.wait_ge(sem("s4_exp"), 8 * i + 4 * k + g + 1)
                pe.wait_ge(freed, 4 * i + 2 * k + g // 2 + 1)
                for m in range(4):
                    s = 4 * g + m
                    mm = nc.tensor.transpose(P[:, 2 + g % 2, m * T:(m + 1) * T], wts4[k % 2][:, s * T:(s + 1) * T],
                                             ident)
                mm.then_inc(sem("s4_turned"), 1)

            def mix(i, k, g):
                if g == 0:
                    pe.wait_ge(sem("s4_evac_a"), 4 * i + 2 * k + 2 + 1)
                    pe.wait_ge(sem("s4_evac_d"), 4 * i + 2 * k + 2 + 1)
                    pe.wait_ge(sem("s4_normed"), 2 * i + k + 1)
                for s in range(4 * g, 4 * g + 4):
                    h = slot_head(s // 4, s % 4)[2]
                    at = (h % OH) * (K2 + 1)
                    mm = nc.tensor.matmul(P[:, 4 + h // OH, at:at + K2 + 1], wtT4[k % 2][:, s * T:(s + 1) * T],
                                          V4[:, bass.ds(2 * i * VW + k * VW + h * (K2 + 1), K2 + 1)],
                                          start=True, stop=True)
                if g == 3:
                    mm.then_inc(sem("s4_mixed"), 1)

            def turn_outs(i, k, r, bank_read=None):
                if r == 0:
                    pe.wait_ge(sem("s4_normed"), 2 * i + k + 1 + 1)
                    pe.wait_ge(sem("q4_ready"), bank_read)
                else:
                    pe.wait_ge(sem("s4_ocopied"), 4 * i + 2 * k + 1)
                for m in range(4):
                    tile = 4 * r + m
                    mm = nc.tensor.transpose(P[:, 7, m * T:(m + 1) * T], o4[k % 2][:, tile * T:(tile + 1) * T], ident)
                mm.then_inc(sem("s4_oturned"), 1)

            def project(i, k):
                pe.wait_ge(sem("s4_ocopied"), 4 * i + 2 * k + 2)
                for tile in range(HT):
                    mm = nc.tensor.matmul(P[:, 7, 0:T], Xo[:, tile * 128:(tile + 1) * 128],
                                          oT4[k % 2][:, tile * T:(tile + 1) * T], start=(tile == 0),
                                          stop=(tile == HT - 1))
                mm.then_inc(sem("y4"), 1)

            def batch(i, k):
                scores(i, k, 0)
                mix(i, k - 1, 0)
                scores(i, k, 1)
                mix(i, k - 1, 1)
                scores(i, k, 2)
                mix(i, k - 1, 2)
                mix(i, k - 1, 3)
                turn(i, k, 0)
                scores(i, k, 3)
                turn(i, k, 1)
                turn_outs(i, k - 1, 0, 4 * i + 2 * k + 2)
                turn(i, k, 2)
                turn_outs(i, k - 1, 1)
                turn(i, k, 3)
                project(i, k - 1)

            for r in range(2):
                for m in range(4):
                    tile = 4 * r + m
                    mm = nc.tensor.matmul(P[:, QBANK[r], m * T:(m + 1) * T], Xq[:, tile * 128:(tile + 1) * 128], xn[:, 0:T],
                                          start=True, stop=True)
                mm.then_inc(sem("q4_made"), 1)
            scores(0, 0, 0)
            scores(0, 0, 1)
            scores(0, 0, 2)
            turn(0, 0, 0)
            scores(0, 0, 3)
            turn(0, 0, 1)
            turn(0, 0, 2)
            turn(0, 0, 3)
            queries(0, 1)
            with pe.Fori(0, B // 2 - 1) as i:
                for k in (1, 2):
                    batch(i, k)
                    queries(i, k + 1)
            batch(B // 2 - 1, 1)
            for g in range(4):
                mix(B // 2 - 1, 1, g)
            turn_outs(B // 2 - 1, 1, 0, 2 * B)
            turn_outs(B // 2 - 1, 1, 1)
            project(B // 2 - 1, 1)

        def pool_stage4(pool):
            pool.wait_ge(sem("kv_copied_a"), HT)
            pool.wait_ge(sem("kv_copied_d"), HT)
            with pool.Fori(0, B // 2) as i:
                for j in range(2):
                    pool.wait_ge(sem("s4_scored"), 8 * i + 4 * j + 4)
                    nc.gpsimd.tensor_copy(heads(ks4[j][:, :], HT, T), kT4[:, :, bass.ds(2 * i * T + j * T, T)])\
                        .then_inc(sem("k4_staged"), 1)

        def kv_copy(copy, u):
            if u < 2 * HT:
                copy(kT4[:, u // 2, (u % 2) * HALF:(u % 2 + 1) * HALF], P[:, u % 4, :])
            else:
                b, r = divmod(u - 2 * HT, 2)
                dst = V4.rearrange("p (b h k) -> p b h k", b=B, h=H2)[:, b, r * 8:(r + 1) * 8, 0:K2]
                copy(dst, heads(P[:, u % 4, :], 8, K2))

        def act_stage4(act):
            for u in range(0, 4 * HT, 2):
                act.wait_ge(sem("kv_made"), u + 1)
                if u == 0:
                    act.wait_ge(sem("v4_ones"), 1)
                kv_copy(lambda o, i: nc.scalar.copy(o, i).then_inc(sem("kv_copied_a"), 1), u)
            act_norm(act, 4)
            act.wait_ge(sem("xn_ready"), 10)
            act.sem_inc(sem("s4_evac_a"), 1)

            def queries(i, k):
                for r in range(2):
                    act.wait_ge(sem("q4_made"), 4 * i + 2 * k + r + 1)
                    nc.scalar.copy(q4[k % 2][:, r * 512:(r + 1) * 512], P[:, QBANK[r], :]).then_inc(sem("q4_ready"), 1)

            def exps(i, k, g):
                act.wait_ge(sem("s4_shifted"), 8 * i + 4 * k + g + 1 + 2)
                wts = wts4[k % 2][:, g * 512:(g + 1) * 512]
                nc.scalar.activation(wts, wts, ACT.Exp, scale=SC2).then_inc(sem("s4_exp"), 1)

            def evac(i, k, g):
                act.wait_ge(sem("s4_turned"), 8 * i + 4 * k + g + 1)
                nc.scalar.copy(wtT4[k % 2][:, g * 512:(g + 1) * 512], P[:, 2, :]).then_inc(sem("s4_evac_a"), 1)

            def outs(i, k, r):
                act.wait_ge(sem("s4_oturned"), 4 * i + 2 * k + r + 1)
                nc.scalar.copy(oT4[k % 2][:, r * 512:(r + 1) * 512], P[:, 7, :]).then_inc(sem("s4_ocopied"), 1)

            def batch(i, k, before=True):
                exps(i, k, 0)
                exps(i, k, 1)
                exps(i, k, 2)
                evac(i, k, 0)
                if before:
                    outs(i, k - 1, 0)
                exps(i, k, 3)
                evac(i, k, 2)
                if before:
                    outs(i, k - 1, 1)
            queries(0, 0)
            batch(0, 0, before=False)
            queries(0, 1)
            with act.Fori(0, B // 2 - 1) as i:
                for k in (1, 2):
                    batch(i, k)
                    queries(i, k + 1)
            batch(B // 2 - 1, 1)
            outs(B // 2 - 1, 1, 0)
            outs(B // 2 - 1, 1, 1)

        def dve_stage4(dve):
            dve.wait_ge(sem("y3_gated"), DC)
            nc.vector.memset(V4.rearrange("p (n k) -> p n k", k=K2 + 1)[:, :, K2:K2 + 1], 1.0).then_inc(sem("v4_ones"), 1)
            for u in range(1, 4 * HT, 2):
                dve.wait_ge(sem("kv_made"), u + 1)
                kv_copy(lambda o, i: nc.vector.tensor_copy(o, i).then_inc(sem("kv_copied_d"), 1), u)
            dve_norm(dve, 4)
            dve.sem_inc(sem("s4_shifted"), 2)
            dve.sem_inc(sem("s4_evac_d"), 1)
            dve.sem_inc(sem("s4_normed"), 1)
            dve.sem_inc(sem("s4_added"), 1)

            def shift(i, k, g):
                dve.wait_ge(sem("s4_scored"), 8 * i + 4 * k + g + 1 + 8)
                S = heads(P[:, g % 2, :], 4, T)
                mx = smax4[k % 2][:, 4 * g:4 * g + 4]
                nc.vector.tensor_reduce(mx, S, AX, ALU.max).then_inc(sem("s4_max"), 1)
                dve.wait_ge(sem("s4_max"), 8 * i + 4 * k + g + 1)
                nc.vector.tensor_tensor(heads(wts4[k % 2][:, g * 512:(g + 1) * 512], 4, T), S,
                                        mx.unsqueeze(2).broadcast_to([128, 4, T]), ALU.subtract)\
                    .then_inc(sem("s4_shifted"), 1)

            def evac(i, k, g):
                dve.wait_ge(sem("s4_turned"), 8 * i + 4 * k + g + 1)
                nc.vector.tensor_copy(wtT4[k % 2][:, g * 512:(g + 1) * 512], P[:, 3, :]).then_inc(sem("s4_evac_d"), 1)

            def norm(i, k):
                dve.wait_ge(sem("s4_mixed"), 2 * i + k + 1)
                parts = [(p, min(OH, H2 - p * OH)) for p in range(3)]
                for p, n in parts:
                    O = P[:, 4 + p, 0:n * (K2 + 1)].rearrange("p (h k) -> p h k", h=n)
                    nc.vector.reciprocal(rz4[k % 2][:, p * OH:p * OH + n], O[:, :, K2]).then_inc(sem("s4_rz"), 1)
                for p, n in parts:
                    dve.wait_ge(sem("s4_rz"), 10 * i + 5 * k + p + 1)
                    O = P[:, 4 + p, 0:n * (K2 + 1)].rearrange("p (h k) -> p h k", h=n)
                    ins = nc.vector.tensor_tensor(heads(o4[k % 2][:, p * OH * K2:(p * OH + n) * K2], n, K2), O[:, :, 0:K2],
                                                  rz4[k % 2][:, p * OH:p * OH + n].unsqueeze(2).broadcast_to([128, n, K2]),
                                                  ALU.mult)
                    ins.then_inc(sem("s4_normed" if p == 2 else "s4_rz"), 1)

            def add(i, k):
                dve.wait_ge(sem("y4"), 2 * i + k + 1)
                xb = xT[:, bass.ds(2 * i * T + k * T, T)]
                nc.vector.tensor_tensor(xb, xb, P[:, 7, 0:T], ALU.add).then_inc(sem("s4_added"), 1)
            def batch(i, k, before=True):
                shift(i, k, 0)
                shift(i, k, 1)
                shift(i, k, 2)
                if before:
                    norm(i, k - 1)
                shift(i, k, 3)
                evac(i, k, 1)
                evac(i, k, 3)
                if before:
                    add(i, k - 1)
            batch(0, 0, before=False)
            with dve.Fori(0, B // 2 - 1) as i:
                batch(i, 1)
                batch(i, 2)
            batch(B // 2 - 1, 1)
            norm(B // 2 - 1, 1)
            add(B // 2 - 1, 1)
            dve.drain().then_inc(sem("x_ready"), 2)

        def sp_stage5(sp):
            sp.wait_ge(sem("x_ready"), 12)
            for i in range(E2 // RW):
                for k in range(RW // 2):
                    e = RW * i + 2 * k
                    if i:
                        sp.wait_ge(sem("e5_out"), e - RW + 2)
                    sp.dma_start(wring[:, 2 * k:2 * k + 2, :], d["moe"][e:e + 2].rearrange("e p n -> p e n"))\
                        .then_inc(sem(f"moe_loaded{k}"), 16)
            sp.wait_ge(sem("zero5"), 1)
            sp.dma_start(slots_dram[SLOTS:SLOTS + 1, :], zero5[0:1, :]).then_inc(sem("slots_stored"), 16)
            for i in range(2):
                ne = E2 // 2
                sp.wait_ge(sem("e5_kept"), ne * (i + 1))
                sp.dma_start(slots_dram[i * ne * CAP:(i + 1) * ne * CAP, :].rearrange("(e s) d -> s e d", s=CAP),
                             eo5[:, i * ne:(i + 1) * ne, :]).then_inc(sem("slots_stored"), 16)

        def pe_stage5(pe):
            pe_norm(pe, 5)
            for b in range(B):
                if b % HB == 0:
                    pe.wait_ge(sem("xn_ready"), 10 + b // HB + 1)
                mm = nc.tensor.matmul(heads(P[:, 0, 0:B * E2], B, E2)[:, b, :], xn[:, b * T:(b + 1) * T],
                                      w("wf", "gate"), start=True, stop=True)
            mm.then_inc(sem("gates"), 1)
            for b in range(B):
                mm = nc.tensor.transpose(P[:, 3 + b // HB, (b % HB) * T:(b % HB + 1) * T], xn[:, b * T:(b + 1) * T], ident)
            mm.then_inc(sem("tokens"), 1)
            pe.wait_ge(sem("top1"), 1)
            nc.tensor.matmul(P[:, 1, 0:B * E2], c("tri"), g5[3].rearrange("p b e -> p (b e)"), start=True, stop=True)\
                .then_inc(sem("counts"), 1)
            nc.tensor.matmul(P[:, 2, 0:B * E2], mean128[:, :], g5[3].rearrange("p b e -> p (b e)"), start=True, stop=True)\
                .then_inc(sem("counts"), 1)
            pe.wait_ge(sem("xpart"), 3)
            chunks = [(0, 512), (512, 512), (1024, SLOTS - 1024)]
            for b in range(B):
                pe.wait_ge(sem("hot"), b + 1)
                for part in range(3):
                    lhs = xpart[:, part * N + b * T:part * N + (b + 1) * T]
                    for k, (a, n) in enumerate(chunks):
                        mm = nc.tensor.matmul(P[:, 5 + k, 0:n], lhs, hot5[b % 4][:, a:a + n],
                                              start=(b == 0 and part == 0), stop=(b == B - 1 and part == 2))
                mm.then_inc(sem("hot_used"), 1)

            def up(e):
                pe.wait_ge(sem(f"moe_loaded{e % RW // 2}"), 16 * (e // RW + 1))
                if e == 0:
                    pe.wait_ge(sem("dispatched"), 3)
                if e >= 2:
                    pe.wait_ge(sem("e5_act"), e - 1)
                for k in range(FC):
                    mm = nc.tensor.matmul(P[:, e % 2, k * CAP:(k + 1) * CAP], w1r[e % RW][:, k * 128:(k + 1) * 128],
                                          dT5[:, e * CAP:(e + 1) * CAP], start=True, stop=True)
                mm.then_inc(sem("e5_hidden"), 1)

            def down(e):
                pe.wait_ge(sem("e5_act"), e + 1)
                if e >= 2:
                    pe.wait_ge(sem("e5_kept"), e - 1)
                for k in range(FC):
                    mm = nc.tensor.matmul(P[0:CAP, 2 + e % 2, 0:D], hT5[e % 2][:, k * CAP:(k + 1) * CAP],
                                          w2r[e % RW][:, k * D:(k + 1) * D], start=(k == 0), stop=(k == FC - 1))
                mm.then_inc(sem("e5_out"), 1)
            up(0)
            for e in range(E2):
                if e + 1 < E2:
                    up(e + 1)
                down(e)
            for b in range(B):
                mm = nc.tensor.transpose(P[:, 5 + b // HB, (b % HB) * T:(b % HB + 1) * T], xT[:, b * T:(b + 1) * T], ident)
            mm.then_inc(sem("out_turned"), 1)

        def act_stage5(act):
            act_norm(act, 5)
            act.wait_ge(sem("gate_shift"), 1)
            nc.scalar.activation(g5[5], g5[4], ACT.Exp).then_inc(sem("gate_exp"), 1)
            for part in range(3):
                if part == 0:
                    act.wait_ge(sem("tokens"), 1)
                    for r in range(2):
                        nc.scalar.copy(xpart[:, r * HALF:(r + 1) * HALF], P[:, 3 + r, :])
                    act.drain().then_inc(sem("xpart"), 1)
                else:
                    act.wait_ge(sem("xrest"), part)
                    nc.scalar.copy(xpart[:, part * N:(part + 1) * N], xrest[part - 1]).then_inc(sem("xpart"), 1)
            for k, (a, n) in enumerate([(0, 512), (512, 512), (1024, SLOTS - 1024)]):
                act.wait_ge(sem("hot_used"), B)
                nc.scalar.copy(dT5[:, a:a + n], P[:, 5 + k, 0:n]).then_inc(sem("dispatched"), 1)
            for e in range(E2):
                act.wait_ge(sem("e5_hidden"), e + 1)
                if e >= 2:
                    act.wait_ge(sem("e5_out"), e - 1)
                nc.scalar.activation(hT5[e % 2], P[:, e % 2, 0:FC * CAP], ACT.Gelu_apprx_tanh).then_inc(sem("e5_act"), 1)

        def dve_stage5(dve):
            dve_norm(dve, 5)

            def per(v, n=E2):
                return v.unsqueeze(2).broadcast_to([128, B, n])

            def row(name):
                return c(name).unsqueeze(1).broadcast_to([128, B, E2])
            nc.vector.memset(zero5, 0.0).then_inc(sem("zero5"), 1)
            dve.wait_ge(sem("gates"), 1)
            G = heads(P[:, 0, 0:B * E2], B, E2)
            chain(dve, nc.vector.tensor_reduce(v5[0], G, AX, ALU.max))
            nc.vector.tensor_tensor(g5[4], G, per(v5[0]), ALU.subtract).then_inc(sem("gate_shift"), 1)
            dve.wait_ge(sem("gate_shift"), 1)
            chain(dve, nc.vector.tensor_scalar(g5[0], g5[4], 0.0, None, ALU.is_equal))
            chain(dve, nc.vector.tensor_tensor(g5[1], g5[0], row("prio16"), ALU.mult))
            chain(dve, nc.vector.tensor_reduce(v5[1], g5[1], AX, ALU.max))
            nc.vector.tensor_tensor(g5[3], g5[1], per(v5[1]), ALU.is_equal).then_inc(sem("top1"), 1)
            dve.wait_ge(sem("xpart"), 1)
            for r in range(2):
                nc.vector.tensor_tensor(half(xrest[0], r), P[:, 3 + r, :], half(xpart, r), ALU.subtract)
            dve.drain().then_inc(sem("xrest"), 1)
            dve.wait_ge(sem("counts"), 2)
            chain(dve, nc.vector.memset(g5[2][:, 0, :], 0.0))
            M = heads(P[:, 2, 0:B * E2], B, E2)
            for b in range(1, B):
                chain(dve, nc.vector.scalar_tensor_tensor(g5[2][:, b, :], M[:, b - 1, :], float(D), g5[2][:, b - 1, :],
                                                     ALU.mult, ALU.add))
            chain(dve, nc.vector.tensor_tensor(g5[6], heads(P[:, 1, 0:B * E2], B, E2), g5[2], ALU.add))
            chain(dve, nc.vector.tensor_tensor(g5[7], g5[6], g5[3], ALU.mult))
            chain(dve, nc.vector.tensor_reduce(v5[2], g5[7], AX, ALU.add))
            chain(dve, nc.vector.tensor_tensor(g5[6], row("ebase"), g5[3], ALU.mult))
            chain(dve, nc.vector.tensor_reduce(v5[3], g5[6], AX, ALU.add))
            chain(dve, nc.vector.tensor_scalar(v5[4], v5[2], float(CAP), 2.0 * SLOTS, ALU.is_gt, ALU.mult))
            chain(dve, nc.vector.scalar_tensor_tensor(v5[5], v5[2], -1.0, v5[3], ALU.add, ALU.add))
            chain(dve, nc.vector.tensor_tensor(v5[6], v5[5], v5[4], ALU.add))
            nc.vector.tensor_scalar(idx5, v5[6], float(SLOTS), None, ALU.min).then_inc(sem("slots"), 1)
            dve.wait_ge(sem("xpart"), 2)
            chain(dve, nc.vector.tensor_tensor(xrest[1], xrest[0], xpart[:, N:2 * N], ALU.subtract))
            dve.drain().then_inc(sem("xrest"), 1)
            for b in range(B):
                if b >= 4:
                    dve.wait_ge(sem("hot_used"), b - 3)
                nc.vector.tensor_scalar(hot5[b % 4], c("iota"), v5[6][:, b:b + 1], None, ALU.is_equal)\
                    .then_inc(sem("hot"), 1)
            dve.wait_ge(sem("gate_exp"), 1)
            chain(dve, nc.vector.tensor_reduce(v5[0], g5[5], AX, ALU.add))
            chain(dve, nc.vector.reciprocal(v5[7], v5[0]))
            for e in range(E2):
                dve.wait_ge(sem("e5_out"), e + 1)
                nc.vector.tensor_copy(eo5[:, e, :], P[0:CAP, 2 + e % 2, 0:D]).then_inc(sem("e5_kept"), 1)
            dve.wait_ge(sem("out_turned"), 1)
            for b in range(B):
                if b == 0:
                    dve.wait_ge(sem("gathered"), 16 * B)
                ins = nc.vector.scalar_tensor_tensor(
                    final[:, b * D:(b + 1) * D], yg5[:, b * D:(b + 1) * D], v5[7][:, b:b + 1],
                    P[:, 5 + b // HB, (b % HB) * D:(b % HB + 1) * D], ALU.mult, ALU.add)
            dve.drain().then_inc(sem("out_ready"), 1)

        def pool_stage5(pool):
            pool.wait_ge(sem("slots"), 1)
            pool.wait_ge(sem("slots_stored"), 48)
            for b in range(B):
                pool.indirect_dma_start(yg5[:, b * D:(b + 1) * D], None, slots_dram,
                                        bass.IndirectOffsetOnAxis(ap=idx5[:, b:b + 1], axis=0)).then_inc(sem("gathered"), 16)

        nothing = lambda engine: None
        pe_stages = [pe_stage0, pe_stage1, pe_stage2, pe_stage3, pe_stage4, pe_stage5]
        act_stages = [act_stage0, act_stage1, act_stage2, act_stage3, act_stage4, act_stage5]
        dve_stages = [dve_stage0, dve_stage1, dve_stage2, dve_stage3, dve_stage4, dve_stage5]
        pool_stages = [pool_stage0 if stop > 1 else nothing, pool_stage1, nothing, pool_stage3, pool_stage4, pool_stage5]

        @block.sync
        def _(sp):
            sp.dma_start(heads(xtok, B, D), d["x"].rearrange("b t d -> t b d")).then_inc(sem("x_loaded"), 16)
            sp.dma_start(packs["consts"][:, :], d["consts"]).then_inc(sem("consts_loaded"), 16)
            sp.dma_start(packs["small"][:, :], d["small"]).then_inc(sem("small_loaded"), 16)
            sp.dma_start(packs["wa"][:, :], d["wa"]).then_inc(sem("wa_loaded"), 16)
            sp.dma_start(heads(ctok, B, D), d["ctx"].rearrange("b t d -> t b d")).then_inc(sem("ctx_loaded"), 16)
            for k in ("wb", "wc", "wd", "wf"):
                sp.dma_start(packs[k][:, :], d[k]).then_inc(sem(k + "_loaded"), 16)
            if stop > 3:
                sp_stage3(sp)
            if stop > 4:
                sp.wait_ge(sem("conv_act"), DC)
                sp.dma_start(we, d["we"]).then_inc(sem("we_loaded"), 16)
            if stop > 5:
                sp_stage5(sp)
            sp.wait_ge(sem("out_ready"), 1)
            sp.dma_start(out.rearrange("b t d -> t b d"), heads(final if stop > 5 else xc, B, D))\
                .then_inc(sem("stored"), 16)
            sp.wait_ge(sem("stored"), 16)

        @block.tensor
        def _(pe):
            pe.wait_ge(sem("consts_loaded"), 16)
            pe.wait_ge(sem("x_loaded"), 16)
            for b in range(B):
                mm = nc.tensor.transpose(P[:, b // HB, (b % HB) * T:(b % HB + 1) * T], xtok[:, b * D:(b + 1) * D], ident)
                if b % HB == HB - 1:
                    mm.then_inc(sem("x_turned"), 1)
            pe.wait_ge(sem("ctx_loaded"), 16)
            for b in range(B):
                mm = nc.tensor.transpose(P[:, 2 + b // HB, (b % HB) * T:(b % HB + 1) * T], ctok[:, b * D:(b + 1) * D], ident)
                if b % HB == HB - 1:
                    mm.then_inc(sem("ctx_turned"), 1)
            pe.wait_ge(sem("means_set"), 3)
            if stop > 1:
                pe_keys1(pe)
            for f in pe_stages[:stop]:
                f(pe)
            if stop > 5:
                return
            for h in range(2):
                pe.wait_ge(sem("x_ready"), 2 * stop + h + 1)
            for b in range(B):
                mm = nc.tensor.transpose(P[:, b // HB, (b % HB) * T:(b % HB + 1) * T], xT[:, b * T:(b + 1) * T], ident)
            mm.then_inc(sem("out_turned"), 1)

        @block.scalar
        def _(act):
            act.wait_ge(sem("small_loaded"), 16)
            act.wait_ge(sem("means_set"), 3)
            for h in range(2):
                act.wait_ge(sem("ctx_turned"), h + 1)
                nc.scalar.copy(half(ctxT, h), P[:, 2 + h, :]).then_inc(sem("ctx_ready"), 1)
            if stop > 1:
                act_keys1(act)
            for f in act_stages[:stop]:
                f(act)
            if stop > 5:
                return
            act.wait_ge(sem("out_turned"), 1)
            act.wait_ge(sem("ln_rstd"), 2 * stop)
            for h in range(2):
                nc.scalar.copy(half(xc, h), P[:, h, :])
            act.drain().then_inc(sem("out_ready"), 1)

        @block.vector
        def _(dve):
            nc.vector.memset(mean128[:, :], 1.0 / D).then_inc(sem("means_set"), 1)
            nc.vector.memset(mean64[:, :], 1.0 / R0).then_inc(sem("means_set"), 1)
            nc.vector.memset(eps[:, :], EPS).then_inc(sem("means_set"), 1)
            dve.wait_ge(sem("small_loaded"), 16)
            for h in range(2):
                dve.wait_ge(sem("x_turned"), h + 1)
                nc.vector.tensor_copy(half(xT, h), P[:, h, :]).then_inc(sem("x_ready"), 1)
            if stop > 1:
                dve_keys1(dve)
            for f in dve_stages[:stop]:
                f(dve)

        @block.gpsimd
        def _(pool):
            for f in pool_stages[:stop]:
                f(pool)


_INS = ["x", "ctx", "consts", "small", "wa", "wb", "wc", "wd", "we", "wf", "moe"]


def constants():
    p = np.arange(128)
    c = {
        "ident": np.eye(128), "head": p[:, None] // K1 == np.arange(H1), "batch": p[:, None] // NS == np.arange(B),
        "tri": p[:, None] <= p[None, :], "prio6": np.tile(E0 - np.arange(E0), (128, 1)),
        "prio16": np.tile(E2 - np.arange(E2), (128, 1)), "ebase": np.tile(CAP * np.arange(E2), (128, 1)),
        "iota": np.tile(np.arange(SLOTS), (128, 1)),
    }
    owner = np.repeat(ORDER, F0)
    c["select"] = p[:, None] == owner[None, :]
    return np.concatenate([np.asarray(c[n], np.float32).reshape(128, k) for n, k in CONSTS], 1)


def pack(pieces):
    return np.concatenate([np.pad(a, ((0, 128 - a.shape[0]), (0, 0))) for a in pieces], 1)


def kernel(**inputs):
    import concourse.bacc as _bacc
    from concourse.bass_utils import run_bass_kernel_spmd as _run
    i = {k: np.asarray(v) for k, v in inputs.items()}

    def v(name):
        a = i[name].reshape(-1)
        return a.reshape(-1, min(128, a.size)).T

    def r(name):
        return np.broadcast_to(i[name].reshape(1, -1), (128, i[name].size))

    def tiles(a):
        return a.reshape(-1, 128, a.shape[1]).transpose(1, 0, 2).reshape(128, -1)
    W1 = i["L0_attn_W1"][ORDER]
    cw = i["L1_attn_conv_w"].reshape(DC, 128, 4).transpose(1, 0, 2).reshape(128, -1)
    Wx = i["L1_attn_W_xproj"]
    zx = np.zeros((16, DI), np.float32)
    wx = np.concatenate([Wx[0:NS], zx, Wx[NS:2 * NS], zx, np.broadcast_to(Wx[2 * NS:], (NS, DI))], 0)
    arrays = {
        "x": i["x"], "ctx": i["ctx_1024"], "consts": constants(),
        "small": pack([v("L0_attn_r1_b"), v("L0_attn_ln_g"), v("L0_attn_ln_b"),
                       i["L0_attn_b1"][ORDER].reshape(C0, 128).T, v("L0_xattn_bq"), v("L0_xattn_bk"),
                       v("L0_xattn_bo"), v("L0_xattn_b1"), v("L0_xattn_b2"), v("L0_ffn_b1"), v("L0_ffn_b2"),
                       cw, v("L1_attn_conv_b"), v("L1_attn_D_param"),
                       np.tile(i["L1_attn_A_log"], B).reshape(128, 1),
                       r("L0_attn_r2_b"), r("L0_attn_route_bias"), r("L0_attn_temp"), r("L0_xattn_bv"),
                       r("L0_xattn_b3")]),
        "wa": pack([i["L0_attn_r1_w"], i["L0_attn_r2_w"], W1.transpose(1, 0, 2).reshape(D, -1),
                    tiles(i["L0_attn_W2"][ORDER].reshape(-1, D)), i["L0_attn_b2"]]),
        "wb": pack([i["L0_xattn_Wq"].T, i["L0_xattn_Wk"].T, i["L0_xattn_Wv"].T, i["L0_xattn_Wo"].T,
                    i["L0_xattn_w1"].T, i["L0_xattn_w2"].T, np.broadcast_to(i["L0_xattn_w3"].T, (M1, 128))]),
        "wc": pack([i["L0_ffn_w1"].T, tiles(i["L0_ffn_w2"].T)]),
        "wd": pack([i["L1_attn_W_in"].T, tiles(wx.T), tiles(i["L1_attn_W_out"].T)]),
        "we": pack([i["L1_xattn_" + n].reshape(D, -1) for n in ("Wq", "Wk", "Wv")]
                   + [tiles(i["L1_xattn_Wo"].reshape(-1, D))]),
        "wf": pack([i["L1_ffn_gate_w"].T]),
        "moe": np.concatenate([i["L1_ffn_w1"], i["L1_ffn_w2"].reshape(E2, FC, 128, D).transpose(0, 2, 1, 3)
                               .reshape(E2, 128, FC * D)], 2),
    }
    nc = _bacc.Bacc("TRN2", target_bir_lowering=False, num_devices=1)
    feed, d = {}, {}
    for name in _INS:
        feed[f"in_{name}_dram"] = np.ascontiguousarray(arrays[name])
        d[name] = nc.dram_tensor(f"in_{name}_dram", feed[f"in_{name}_dram"].shape, F32, kind="ExternalInput").ap()
    out = nc.dram_tensor("out_0_dram", (B, T, D), F32, kind="ExternalOutput").ap()
    program(nc, d, out, 6)
    res = _run(nc, [feed], core_ids=[0])
    return res.results[0]["out_0_dram"]
```

```python
from contextlib import ExitStack

import concourse.bass as bass
from concourse import mybir
import numpy as np

F32 = mybir.dt.float32
BF16 = mybir.dt.bfloat16
I32 = mybir.dt.int32
ALU = mybir.AluOpType
ACT = mybir.ActivationFunctionType
AX = mybir.AxisListType.X

B, T, D = 8, 128, 128
N = B * T
HALF = N // 2
HB = B // 2
EPS = 1e-5

E0, F0, R0 = 6, 192, 64
C0 = E0 * F0 // 128
MIXED = C0 // 2
ORDER = [0, 2, 4, 1, 3, 5]

H1, K1 = 16, 8
M1 = 64
SC1 = float(K1) ** -0.5
FQ = 512
QC = FQ // 128
ROUND = 12582912.0

DI, NS = 256, 16
DC = DI // 128
DT_MIN, DT_MAX = 0.001, 0.1
LOOK = 4
STEPS = 16
PLACED = 8

H2, K2 = 16, 64
SC2 = float(K2) ** -0.5
HT = H2 * K2 // 128

E2, F2, CAP = 16, 512, 80
FC = F2 // 128
SLOTS = E2 * CAP

LOG_T_MIN, LOG_T_MAX = float(np.log(0.1)), float(np.log(10.0))

CONSTS = [("head", H1), ("batch", B), ("tri", 128), ("prio6", E0), ("prio16", E2),
          ("ebase", E2), ("select", C0 * 128), ("iota", SLOTS)]
COLS = [("r1_b", 1), ("ln_g", 1), ("ln_b", 1), ("b1", C0), ("bq", 1), ("bk", 1), ("bo", 1), ("m1", 1),
        ("m2", 1), ("fb1", QC), ("fb2", 1), ("conv_w", 4 * DC), ("conv_b", DC), ("dskip", DC), ("alog", 1)]
ROWS = [("r2_b", E0), ("route", E0), ("temp", 1), ("bv", D), ("b3", 1), ("ident", 128)]
WA = [("r1_w", R0), ("r2_w", E0), ("W1", C0 * 128), ("W2", C0 * 128), ("b2", D)]
WB = [("Wq", D), ("Wk", D), ("Wv", D), ("Wo", D), ("mw1", M1), ("mw2", M1), ("mw3", 128)]
WC = [("fw1", FQ), ("fw2", QC * 128)]
WD = [("Win", 2 * DI), ("Wx", DC * 80), ("Wout", DC * 128)]
WE = [("Xq", H2 * K2), ("Xk", H2 * K2), ("Xv", H2 * K2), ("Xo", HT * 128)]
WF = [("gate", E2)]
PACKS = {"consts": CONSTS, "small": COLS + ROWS, "wa": WA, "wb": WB, "wc": WC, "wd": WD, "we": WE, "wf": WF}


FB_AT = sum(n for _, n in COLS[:[k for k, _ in COLS].index("fb1")])


def width(pack):
    return sum(n for _, n in PACKS[pack])


def program(nc, d, out, stop):
    with ExitStack() as ctx:
        def sb(name, shape, dt=F32):
            return ctx.enter_context(nc.sbuf_tensor(name, shape, dt))

        sems = {}

        def sem(name):
            if name not in sems:
                sems[name] = ctx.enter_context(nc.semaphore(name))
            return sems[name]

        P = ctx.enter_context(nc.psum_tensor("P", [128, 8, 512], F32))

        arena1 = sb("arena1", [128, 16640])
        arena2 = sb("arena2", [128, 16384])
        packs = {k: sb("pack_" + k, [128, width(k)]) for k in ("consts", "small", "wa", "wb", "wc", "wd", "wf")}
        if stop >= 5:
            pass

        def w(pack, name, rows=128):
            at = 0
            for n, k in PACKS[pack]:
                if n == name:
                    return packs[pack][0:rows, at:at + k]
                at += k
            raise KeyError(name)

        def c(name, rows=128):
            return w("consts", name, rows)

        def col(name, rows=128):
            return w("small", name, rows)

        ident = col("ident")
        mean128 = sb("mean128", [128, 128])
        mean64 = sb("mean64", [R0, R0])
        eps = sb("eps", [128, 1])
        early = sb("early", [128, 8])
        xT = sb("xT", [128, N])
        xn = sb("xn", [128, N])
        lnbuf = sb("lnbuf", [128, 2 * N])
        xc = lnbuf[:, 0:N]
        sq = lnbuf[:, N:2 * N]
        dev = sb("dev", [128, B])
        rstd = sb("rstd", [128, B])
        ctxT = sb("ctxT", [128, N])

        def half(t, h):
            return t[:, h * HALF:(h + 1) * HALF]

        def heads(t, k, n):
            return t.rearrange("p (k n) -> p k n", k=k)

        at1 = [0]

        def a1(n, dt=F32):
            t = arena1[:, at1[0]:at1[0] + n]
            at1[0] += n
            return t
        xtok = a1(N)
        ctok = a1(N)
        rh = a1(N)[0:R0, :]
        rc = a1(N)[0:R0, :]
        rs = a1(N)[0:R0, :]
        rg = a1(N)[0:R0, :]
        lg = [heads(a1(B * E0), B, E0) for _ in range(12)]
        red = [a1(B).unsqueeze(2) for _ in range(6)]
        rtemp = a1(1)
        probsT = a1(N)[0:E0, :]
        act0 = [a1(HALF) for _ in range(3)]
        wact0 = [a1(HALF) for _ in range(3)]
        W1 = heads(w("wa", "W1"), C0, 128)
        W2 = heads(w("wa", "W2"), C0, 128)
        PR = 96 + E0
        probs4 = heads(a1(B * PR), B, PR)
        cast0 = [heads(a1(B * E0 // 2).bitcast(BF16), B, E0) for _ in range(2)]
        parts0 = a1(N // 2).bitcast(BF16)[0:PR, :]
        select0 = a1(C0 * 64).bitcast(BF16)[0:PR, :]
        SEL = heads(select0, C0, 128)

        Kexp = arena2[:, :]
        Dall = arena1[:, 0:16384]
        kT1 = sb("kT1", [128, N])
        qT1 = sb("qT1", [128, N])
        V1 = sb("V1", [128, N])
        qs1 = [sb(f"qs1_{j}", [128, T]) for j in range(2)]
        HTK = H1 * T
        exp1 = [packs["wa"][:, 0:HTK], lnbuf[:, :]]
        st1 = [sb(f"st1_{j}", [128, H1, 6]) for j in range(2)]
        BH = B * H1
        stats1 = sb("stats1", [128, BH, 6])
        max1 = sb("max1", [128, BH])
        smax1 = [sb(f"smax1_{j}", [128, H1]) for j in range(2)]
        nmax1 = [sb(f"nmax1_{j}", [128, H1]) for j in range(2)]
        SHIFT_D = 8
        wts1 = [arena2[:, j * HTK:(j + 1) * HTK] for j in range(2)]
        wtT1 = [arena2[:, (2 + j) * HTK:(3 + j) * HTK] for j in range(2)]
        at2 = [4 * HTK]

        def a2(n):
            t = arena2[:, at2[0]:at2[0] + n]
            at2[0] += n
            return t
        tmp1 = [a2(BH) for _ in range(6)]
        ent1 = a2(BH)
        simrow1 = sb("simrow1", [128, BH])
        qsum1, ksum1, sim1 = (sb(n, [128, B]) for n in ("qsum1", "ksum1", "sim1"))
        featw = sb("featw", [128, 3, 3])
        feats1, hid1, hid2 = a2(BH)[0:3, :], a2(BH)[0:M1, :], a2(BH)[0:M1, :]
        logt1, temper1, cool1 = a2(BH), a2(BH), a2(BH)
        rz1 = [a2(H1) for _ in range(2)]
        z1 = [a2(H1) for _ in range(2)]
        vslots = exp1
        raw1 = [a2(D) for _ in range(2)]
        same1 = [a2(D).bitcast(I32) for _ in range(2)]
        o1 = [a2(D) for _ in range(2)]
        oT1 = a2(N)

        fw1q = sb("fw1q", [128, FQ], BF16)
        fw2q = sb("fw2q", [128, QC * 128], BF16)
        fbq = sb("fbq", [128, QC + 1])
        ftmp = [sb(f"ftmp{k}", [128, FQ]) for k in range(2)]
        xq = arena1[:, 0:N // 2].bitcast(BF16)
        xr = arena1[:, N:2 * N]
        hraw = [arena1[:, (4 + u) * HALF:(5 + u) * HALF] for u in range(2)]
        hclip = [arena1[:, (6 + u) * HALF:(7 + u) * HALF] for u in range(2)]
        hq = arena1[:, 8 * HALF:12 * HALF].bitcast(BF16).rearrange("p (u n) -> p u n", u=2 * QC)
        yq = arena1[:, 12 * HALF:14 * HALF]

        at3 = [0]
        KEYS_AT, KEY_STEPS = 8, 7

        def key_step(t):
            return divmod(t - KEYS_AT, KEY_STEPS)

        def a3(n, cols=None):
            t = arena2[:, at3[0]:at3[0] + n]
            at3[0] += n
            return t
        PADT = T + 3
        xpad = a3(DC * B * PADT).rearrange("p (c b t) -> p c b t", c=DC, b=B)
        conv = [a3(DC * N).rearrange("p (c b t) -> p c b t", c=DC, b=B) for _ in range(2)]
        xcv = a3(DC * N)
        sz = a3(DC * N)
        dbl = a3(N)[0:80, :]
        Bst, Cst, dtst = a3(T), a3(T), a3(T)
        dstep = [a3(T) for _ in range(4)]
        Abar, Bbar = a3(T), a3(T)
        negA = a3(1)
        C_AT = 11264
        yg3 = [arena1[:, C_AT + k * DC * N:C_AT + (k + 1) * DC * N] for k in range(2)]
        cbuf = yg3[0]
        Cpad = cbuf[:, 0:STEPS * 128]
        Cdiag = arena1[:, C_AT:C_AT + STEPS * (128 + B)].rearrange("p (k r) -> p k r", k=STEPS)[:, :, 0:B]
        ysum3 = [yg3[1][:, (k + 1) * DI:(k + 2) * DI] for k in range(2)]
        xe3 = [a3(DI) for _ in range(LOOK)]
        U3 = [a3(DI) for _ in range(4)]
        hraw3 = [a3(DI) for _ in range(2)]
        h3 = [arena1[:, 15360 + k * DI:15360 + (k + 1) * DI] for k in range(4)]
        yT3 = arena1[:, 9216:9216 + DC * N]
        scratch = nc.dram_tensor("states_scratch", (3, B, NS, T), F32, kind="Internal").ap()

        kT4 = arena1[:, 0:HT * N].rearrange("p (m n) -> p m n", m=HT)
        VW = H2 * (K2 + 1)
        V4 = arena1[:, HT * N:HT * N + B * VW]
        we = arena2[:, 0:width("we")]
        Xq, Xk, Xv, Xo = (we[:, k * 1024:(k + 1) * 1024] for k in range(4))
        at4 = [width("we")]

        def a4(n):
            t = arena2[:, at4[0]:at4[0] + n]
            at4[0] += n
            return t
        q4 = [lnbuf[:, j * N:(j + 1) * N] for j in range(2)]
        ks4 = [kT1, qT1]
        wts4 = [a4(H2 * T) for _ in range(2)]
        wtT4 = [a4(H2 * T) for _ in range(2)]
        o4 = [a4(H2 * K2) for _ in range(2)]
        oT4 = [a4(H2 * K2) for _ in range(2)]
        smax4 = [sb(f"smax4_{j}", [128, H2]) for j in range(2)]
        rz4 = [sb(f"rz4_{j}", [128, H2]) for j in range(2)]

        RW = 8
        wring = heads(arena1[:, 0:RW * 1024], RW, 1024)
        w1r = [arena1[:, k * 1024:k * 1024 + F2] for k in range(RW)]
        w2r = [arena1[:, k * 1024 + F2:(k + 1) * 1024] for k in range(RW)]
        at5 = [RW * 1024]

        def a5(n):
            t = arena1[:, at5[0]:at5[0] + n]
            at5[0] += n
            return t
        g5 = [heads(a5(B * E2), B, E2) for _ in range(8)]
        v5 = [a5(B) for _ in range(8)]
        idx5 = a5(B).bitcast(mybir.dt.uint32)
        zero5 = a5(128)
        xrest = [arena2[:, k * N:(k + 1) * N] for k in range(2)]
        xpart = arena2[:, 2 * N:2 * N + 3 * N // 2].bitcast(BF16)
        hot5 = [arena2[:, 4096 + k * SLOTS // 2:4096 + (k + 1) * SLOTS // 2].bitcast(BF16) for k in range(4)]
        dT5 = arena2[:, 7168:7168 + SLOTS]
        hT5 = [arena2[:, 8704 + k * FC * CAP:8704 + (k + 1) * FC * CAP] for k in range(2)]
        eo5 = arena2[0:CAP, 10240:10240 + E2 * D].rearrange("p (e d) -> p e d", e=E2)
        yg5 = arena2[:, 12288:12288 + N]
        final = arena2[:, 13312:13312 + N]
        slots_dram = nc.dram_tensor("slots_scratch", (SLOTS + 1, D), F32, kind="Internal").ap()

        block = ctx.enter_context(nc.Block())

        def pe_norm(pe, k):
            for h in range(2):
                pe.wait_ge(sem("x_ready"), 2 * k + h + 1)
                nc.tensor.matmul(P[:, 4 + h, :], mean128[:, :], half(xT, h), start=True, stop=True)\
                    .then_inc(sem("ln_mean"), 1)
            for h in range(2):
                pe.wait_ge(sem("ln_squared"), 2 * k + h + 1)
                for m in range(HB):
                    mm = nc.tensor.matmul(P[:, 6 + h, m:m + 1], half(sq, h)[:, m * 128:(m + 1) * 128], mean128[:, 0:1],
                                          start=True, stop=True)
                mm.then_inc(sem("ln_var"), 1)
            for h in range(2):
                pe.wait_ge(sem("ln_rstd"), 2 * k + h + 1)
                for m in range(HB):
                    at = h * HB + m
                    mm = nc.tensor.matmul(P[:, 6 + h, m * 128:(m + 1) * 128],
                                          rstd[:, at:at + 1].broadcast_to([128, 128]), ident, start=True, stop=True)
                mm.then_inc(sem("ln_spread"), 1)

        def act_norm(act, k):
            nc.scalar.activation(early[:, k:k + 1], eps[:, :], ACT.Sqrt)
            for h in range(2):
                act.wait_ge(sem("ln_centred"), 2 * k + h + 1)
                nc.scalar.activation(half(sq, h), half(xc, h), ACT.Square).then_inc(sem("ln_squared"), 1)
            for h in range(2):
                act.wait_ge(sem("ln_var"), 2 * k + h + 1)
                nc.scalar.activation(dev[:, h * HB:(h + 1) * HB], P[:, 6 + h, 0:HB], ACT.Sqrt, bias=eps[:, :])\
                    .then_inc(sem("ln_std"), 1)

        def dve_norm(dve, k):
            for h in range(2):
                dve.wait_ge(sem("ln_mean"), 2 * k + h + 1)
                nc.vector.tensor_tensor(half(xc, h), half(xT, h), P[:, 4 + h, :], ALU.subtract)\
                    .then_inc(sem("ln_centred"), 1)
            for h in range(2):
                dve.wait_ge(sem("ln_std"), 2 * k + h + 1)
                nc.vector.reciprocal(rstd[:, h * HB:(h + 1) * HB], dev[:, h * HB:(h + 1) * HB])\
                    .then_inc(sem("ln_rstd"), 1)
            for h in range(2):
                dve.wait_ge(sem("ln_spread"), 2 * k + h + 1)
                nc.vector.tensor_tensor(half(xn, h), half(xc, h), P[:, 6 + h, :], ALU.mult)\
                    .then_inc(sem("xn_ready"), 1)

        steps = [0]

        def chain(dve, ins):
            steps[0] += 1
            ins.then_inc(sem("dve_step"), 1)
            dve.wait_ge(sem("dve_step"), steps[0])

        UNITS = [(cc, h) for cc in range(C0) for h in range(2)]

        def pe_stage0(pe):
            pe_norm(pe, 0)
            pe.wait_ge(sem("wa_loaded"), 16)
            for h in range(2):
                pe.wait_ge(sem("xn_ready"), h + 1)
                nc.tensor.matmul(P[0:R0, h, :], w("wa", "r1_w"), half(xn, h), start=True, stop=True)\
                    .then_inc(sem("r_hidden"), 1)
            for h in range(2):
                pe.wait_ge(sem("r_biased"), h + 1)
                nc.tensor.matmul(P[0:R0, 2 + h, :], mean64[:, :], half(rh, h), start=True, stop=True)\
                    .then_inc(sem("r_sums"), 1)
            for h in range(2):
                pe.wait_ge(sem("r_squared"), h + 1)
                for m in range(HB):
                    mm = nc.tensor.matmul(P[:, 4 + h, m:m + 1], half(rs, h)[:, m * 128:(m + 1) * 128], mean64[:, 0:1],
                                          start=True, stop=True)
                mm.then_inc(sem("r_sums"), 1)
            for h in range(2):
                pe.wait_ge(sem("r_vector"), 2 + h + 1)
                for m in range(HB):
                    at = h * HB + m
                    mm = nc.tensor.matmul(P[0:R0, 4 + h, m * 128:(m + 1) * 128],
                                          rstd[:, at:at + 1].broadcast_to([128, R0]), ident, start=True, stop=True)
                mm.then_inc(sem("r_sums"), 1)
            LGT = heads(P[:, 0, 0:B * E0], B, E0)
            for b in range(B):
                if b % HB == 0:
                    pe.wait_ge(sem("r_act"), b // HB + 1)
                mm = nc.tensor.matmul(LGT[:, b, :], rg[:, b * T:(b + 1) * T], w("wa", "r2_w", R0),
                                      start=True, stop=True)
            mm.then_inc(sem("logits"), 1)
            pe.wait_ge(sem("probs"), 1)
            for b in range(B):
                mm = nc.tensor.transpose(P[0:PR, 6 + b // HB, (b % HB) * T:(b % HB + 1) * T], probs4[:, b, :], ident)
                if b % HB == HB - 1:
                    mm.then_inc(sem("probs_turned"), 1)

            def down(u):
                cc, h = UNITS[u]
                pe.wait_ge(sem("e_weighted"), u + 1)
                if u == 0:
                    pe.wait_ge(sem("probs_copied"), 4)
                nc.tensor.matmul(P[:, 6 + h, :], W2[:, cc, :], wact0[u % 3], start=(cc == 0), stop=False)\
                    .then_inc(sem("e_used"), 1)
            for u, (cc, h) in enumerate(UNITS):
                if u >= 3:
                    pe.wait_ge(sem("e_act"), u - 2)
                nc.tensor.matmul(P[:, u % 3, :], W1[:, cc, :], half(xn, h), start=True, stop=True)\
                    .then_inc(sem("e_hidden"), 1)
                if u >= 3:
                    pe.wait_ge(sem("e_weighted"), u - 2)
                if u == 0:
                    pe.wait_ge(sem("select_cast"), 1)
                if u < 2:
                    pe.wait_ge(sem("probs_copied"), u + 1)
                nc.tensor.matmul(P[:, 3 + u % 3, :], SEL[:, cc, :], half(parts0, h), start=True, stop=True)\
                    .then_inc(sem("e_prob"), 1)
                if u >= 2:
                    down(u - 2)
            down(len(UNITS) - 2)
            down(len(UNITS) - 1)
            for h in range(2):
                nc.tensor.matmul(P[:, 6 + h, :], w("wa", "b2", E0), half(probsT, h), start=False, stop=True)\
                    .then_inc(sem("stage_out"), 1)

        def act_stage0(act):
            act_norm(act, 0)
            for h in range(2):
                act.wait_ge(sem("r_hidden"), h + 1)
                nc.scalar.activation(half(rh, h), P[0:R0, h, :], ACT.Identity, bias=col("r1_b", R0))\
                    .then_inc(sem("r_biased"), 1)
            for h in range(2):
                act.wait_ge(sem("r_vector"), h + 1)
                nc.scalar.activation(half(rs, h), half(rc, h), ACT.Square).then_inc(sem("r_squared"), 1)
            for h in range(2):
                act.wait_ge(sem("r_sums"), 2 + h + 1)
                nc.scalar.activation(dev[:, h * HB:(h + 1) * HB], P[:, 4 + h, 0:HB], ACT.Sqrt, bias=eps[:, :])\
                    .then_inc(sem("r_std"), 1)
            for h in range(2):
                act.wait_ge(sem("r_vector"), 4 + h + 1)
                nc.scalar.activation(half(rg, h), half(rg, h), ACT.Gelu, bias=col("ln_b", R0),
                                     scale=col("ln_g", R0)).then_inc(sem("r_act"), 1)
            act.wait_ge(sem("route_shift"), 1)
            nc.scalar.activation(lg[3], lg[2], ACT.Exp).then_inc(sem("route_exp"), 1)
            for h in range(2):
                act.wait_ge(sem("probs_turned"), h + 1)
                nc.scalar.copy(half(parts0, h), P[0:PR, 6 + h, :]).then_inc(sem("probs_copied"), 1)
            for h in range(2):
                nc.scalar.copy(half(probsT, h), P[0:E0, 6 + h, :]).then_inc(sem("probs_copied"), 1)

            def unit(u, fn, lo, hi, last=True):
                cc, h = UNITS[u]
                ins = nc.scalar.activation(act0[u % 3][lo:hi, :], P[lo:hi, u % 3, :], fn,
                                           bias=col("b1")[lo:hi, cc:cc + 1])
                if last:
                    ins.then_inc(sem("e_act"), 1)
            for u, (cc, h) in enumerate(UNITS):
                if cc == MIXED and h == 1:
                    continue
                act.wait_ge(sem("e_hidden"), u + 1 + (cc == MIXED))
                if u >= 3:
                    act.wait_ge(sem("e_weighted"), u - 2 + (cc == MIXED))
                if cc == MIXED:
                    unit(u, ACT.Gelu, 0, 64, False)
                    unit(u + 1, ACT.Gelu, 0, 64, False)
                    unit(u, ACT.Silu, 64, 128)
                    unit(u + 1, ACT.Silu, 64, 128)
                else:
                    unit(u, ACT.Gelu if cc < MIXED else ACT.Silu, 0, 128)

        def dve_stage0(dve):
            dve_norm(dve, 0)
            for h in range(2):
                dve.wait_ge(sem("r_sums"), h + 1)
                nc.vector.tensor_tensor(half(rc, h), half(rh, h), P[0:R0, 2 + h, :], ALU.subtract)\
                    .then_inc(sem("r_vector"), 1)
            for h in range(2):
                dve.wait_ge(sem("r_std"), h + 1)
                nc.vector.reciprocal(rstd[:, h * HB:(h + 1) * HB], dev[:, h * HB:(h + 1) * HB])\
                    .then_inc(sem("r_vector"), 1)
            for h in range(2):
                dve.wait_ge(sem("r_sums"), 4 + h + 1)
                nc.vector.tensor_tensor(half(rg, h), half(rc, h), P[0:R0, 4 + h, :], ALU.mult)\
                    .then_inc(sem("r_vector"), 1)
            LGT = heads(P[:, 0, 0:B * E0], B, E0)

            def row(name):
                return col(name).unsqueeze(1).broadcast_to([128, B, E0])

            def per_token(i):
                return red[i].broadcast_to([128, B, E0])
            prio = c("prio6").unsqueeze(1).broadcast_to([128, B, E0])
            chain(dve, nc.vector.memset(probs4, 0.0))
            chain(dve, nc.vector.reciprocal(rtemp, col("temp")))
            dve.wait_ge(sem("consts_loaded"), 16)
            dve.wait_ge(sem("logits"), 1)
            chain(dve, nc.vector.tensor_tensor(lg[0], LGT, row("r2_b"), ALU.add))
            chain(dve, nc.vector.scalar_tensor_tensor(lg[1], lg[0], rtemp, row("route"), ALU.mult, ALU.add))
            chain(dve, nc.vector.tensor_reduce(red[0], lg[1], AX, ALU.max))
            nc.vector.tensor_tensor(lg[2], lg[1], per_token(0), ALU.subtract).then_inc(sem("route_shift"), 1)
            dve.wait_ge(sem("route_exp"), 1)
            chain(dve, nc.vector.tensor_reduce(red[1], lg[3], AX, ALU.add))
            chain(dve, nc.vector.reciprocal(red[1], red[1]))
            chain(dve, nc.vector.tensor_tensor(lg[4], lg[3], per_token(1), ALU.mult))
            src = lg[4]
            for r in range(2):
                hit, mark, best = lg[5 + r], lg[7 + r], lg[9 + r]
                chain(dve, nc.vector.tensor_reduce(red[2 + r], src, AX, ALU.max))
                chain(dve, nc.vector.tensor_tensor(hit, src, per_token(2 + r), ALU.is_equal))
                chain(dve, nc.vector.tensor_tensor(mark, hit, prio, ALU.mult))
                chain(dve, nc.vector.tensor_reduce(red[4 + r], mark, AX, ALU.max))
                chain(dve, nc.vector.tensor_tensor(best, mark, per_token(4 + r), ALU.is_equal))
                if r == 0:
                    chain(dve, nc.vector.scalar_tensor_tensor(lg[2], best, -2.0, src, ALU.mult, ALU.add))
                    src = lg[2]
            chain(dve, nc.vector.tensor_tensor(lg[5], lg[9], lg[10], ALU.add))
            whole, rest = probs4[:, :, 0:E0], lg[11]
            chain(dve, nc.vector.tensor_tensor(whole, lg[4], lg[5], ALU.mult))
            chain(dve, nc.vector.tensor_copy(cast0[0], whole))
            nc.vector.tensor_copy(probs4[:, :, 32:32 + E0], cast0[0])
            chain(dve, nc.vector.tensor_tensor(rest, whole, cast0[0], ALU.subtract))
            chain(dve, nc.vector.tensor_copy(cast0[1], rest))
            nc.vector.tensor_copy(probs4[:, :, 64:64 + E0], cast0[1])
            nc.vector.tensor_tensor(probs4[:, :, 96:96 + E0], rest, cast0[1], ALU.subtract)
            dve.drain().then_inc(sem("probs"), 1)
            for u, (cc, h) in enumerate(UNITS):
                dve.wait_ge(sem("e_act"), u + 1)
                dve.wait_ge(sem("e_prob"), u + 1)
                if u >= 3:
                    dve.wait_ge(sem("e_used"), u - 2)
                nc.vector.tensor_tensor(wact0[u % 3], act0[u % 3], P[:, 3 + u % 3, :], ALU.mult)\
                    .then_inc(sem("e_weighted"), 1)
            for h in range(2):
                dve.wait_ge(sem("stage_out"), h + 1)
                nc.vector.tensor_tensor(half(xT, h), half(xT, h), P[:, 6 + h, :], ALU.add)\
                    .then_inc(sem("x_ready"), 1)


        def pe_keys1(pe):
            pe.wait_ge(sem("wb_loaded"), 16)
            pe.wait_ge(sem("x_ready"), 2)
            for h in range(2):
                pe.wait_ge(sem("ctx_ready"), h + 1)
                nc.tensor.matmul(P[:, h, :], w("wb", "Wk"), half(ctxT, h), start=True, stop=True)\
                    .then_inc(sem("k1_made"), 1)
            for b in range(B):
                mm = nc.tensor.matmul(P[:, 2 + b // HB, (b % HB) * D:(b % HB + 1) * D],
                                      ctxT[:, b * T:(b + 1) * T], w("wb", "Wv"), start=True, stop=True)
            mm.then_inc(sem("v1_made"), 1)
            pe.wait_ge(sem("k1_ready"), 2)
            pe.wait_ge(sem("v1_ready"), 1)

        def act_keys1(act):
            for h in range(2):
                act.wait_ge(sem("k1_made"), h + 1)
                nc.scalar.activation(half(kT1, h), P[:, h, :], ACT.Identity, bias=col("bk"))\
                    .then_inc(sem("k1_ready"), 1)

        def dve_keys1(dve):
            dve.wait_ge(sem("v1_made"), 1)
            for h in range(2):
                ins = nc.vector.tensor_tensor(
                    heads(half(V1, h), HB, D), heads(P[:, 2 + h, :], HB, D),
                    col("bv").unsqueeze(1).broadcast_to([128, HB, D]), ALU.add)
            dve.drain().then_inc(sem("v1_ready"), 1)

        def pool_stage0(pool):
            pool.wait_ge(sem("consts_loaded"), 16)
            nc.gpsimd.tensor_copy(select0, c("select", PR)).then_inc(sem("select_cast"), 1)
            pool.wait_ge(sem("k1_ready"), 2)
            with pool.Fori(0, B) as b:
                nc.gpsimd.tensor_tensor(
                    heads(Kexp[:, bass.ds(b * HTK, HTK)], H1, T),
                    kT1[:, bass.ds(b * T, T)].unsqueeze(1).broadcast_to([128, H1, T]),
                    c("head").unsqueeze(2).broadcast_to([128, H1, T]), ALU.mult)
            pool.drain().then_inc(sem("k1_spread"), 1)

        def pool_stage1(pool):
            pool.wait_ge(sem("q1_ready"), 2)
            with pool.Fori(0, B // 2) as i:
                for j in range(2):
                    pool.wait_ge(sem("s1_scored"), 2 * i + j + 1)
                    nc.gpsimd.tensor_copy(qs1[j][:, :], qT1[:, bass.ds(2 * i * T + j * T, T)])\
                        .then_inc(sem("s1_staged"), 1)
            pool.wait_ge(sem("wc_loaded"), 16)
            n = 0
            for src, dst in ((w("wc", "fw1"), fw1q[:, :]), (w("wc", "fw2"), fw2q[:, :])):
                nc.gpsimd.tensor_scalar(ftmp[0][:, :], src, 64.0, 127.0, ALU.mult, ALU.min)\
                    .then_inc(sem("fw_step"), 1)
                pool.wait_ge(sem("fw_step"), n + 1)
                nc.gpsimd.tensor_scalar(ftmp[1][:, :], ftmp[0][:, :], -128.0, ROUND, ALU.max, ALU.add)\
                    .then_inc(sem("fw_step"), 1)
                pool.wait_ge(sem("fw_step"), n + 2)
                nc.gpsimd.tensor_scalar(dst, ftmp[1][:, :], ROUND, None, ALU.subtract).then_inc(sem("fw_step"), 1)
                pool.wait_ge(sem("fw_step"), n + 3)
                n += 3
            nb = QC + 1
            fb = packs["small"][:, FB_AT:FB_AT + nb]
            nc.gpsimd.tensor_scalar(ftmp[0][:, 0:nb], fb, 64.0, 127.0, ALU.mult, ALU.min).then_inc(sem("fw_step"), 1)
            pool.wait_ge(sem("fw_step"), n + 1)
            nc.gpsimd.tensor_scalar(ftmp[1][:, 0:nb], ftmp[0][:, 0:nb], -128.0, ROUND, ALU.max, ALU.add)\
                .then_inc(sem("fw_step"), 1)
            pool.wait_ge(sem("fw_step"), n + 2)
            nc.gpsimd.tensor_scalar(fbq[:, 0:QC], ftmp[1][:, 0:QC], ROUND, 16.0 / 64, ALU.subtract, ALU.mult)
            nc.gpsimd.tensor_scalar(fbq[:, QC:nb], ftmp[1][:, QC:nb], ROUND, 1.0 / 64, ALU.subtract, ALU.mult)
            pool.drain().then_inc(sem("fw_ready"), 1)
            pool.wait_ge(sem("s1_stats"), B + RING)
            for j in range(2):
                nc.gpsimd.memset(vslots[j], 0.0).then_inc(sem("fw_step"), 1)
            pool.wait_ge(sem("fw_step"), n + 4)
            with pool.Fori(0, B // 2) as i:
                for j in range(2):
                    pool.wait_ge(sem("s2_mixed"), 2 * i + j + 1)
                    m, at = H1 - 1, (H1 - 1) * (128 + K1)
                    nc.gpsimd.tensor_copy(heads(vslots[j][:, 0:at], m, 128 + K1)[:, :, 0:K1],
                                          heads(V1[:, bass.ds(2 * i * D + j * D, m * K1)], m, K1))
                    nc.gpsimd.tensor_copy(vslots[j][:, at:at + K1], V1[:, bass.ds(2 * i * D + j * D + m * K1, K1)])
                    pool.wait_ge(sem("s2_rz"), 2 * i + j + 1)
                    nc.gpsimd.tensor_tensor(heads(wts1[j], H1, T), heads(wts1[j], H1, T),
                                            rz1[j].unsqueeze(2).broadcast_to([128, H1, T]), ALU.mult)\
                        .then_inc(sem("s2_weighted"), 1)

        RING = 2

        def pe_stage1(pe):
            pe_norm(pe, 1)
            for h in range(2):
                pe.wait_ge(sem("xn_ready"), 2 + h + 1)
                nc.tensor.matmul(P[:, h, :], w("wb", "Wq"), half(xn, h), start=True, stop=True)\
                    .then_inc(sem("q1_made"), 1)
            pe.sem_inc(sem("s1_scored"), RING)
            pe.wait_ge(sem("q1_ready"), 2)
            pe.wait_ge(sem("k1_spread"), 1)
            with pe.Fori(0, B // 2) as i:
                for j in range(2):
                    pe.wait_ge(sem("s1_staged"), 2 * i + j + 1)
                    pe.wait_ge(sem("s1_shifted"), 2 * i + j + 1)
                    pe.wait_ge(sem("s1_shifted_a"), 2 * i + j + 1)
                    for g in range(4):
                        mm = nc.tensor.matmul(P[:, 4 * j + g, :], qs1[j][:, :],
                                              Kexp[:, bass.ds(2 * i * HTK + j * HTK + g * 512, 512)],
                                              start=True, stop=True)
                    mm.then_inc(sem("s1_scored"), 1)
            pe.wait_ge(sem("s1_shifted"), B + RING)
            pe.wait_ge(sem("s1_shifted_a"), B + RING)
            pe.wait_ge(sem("feat_rows"), 1)
            for f, row in enumerate((simrow1[:, :], max1[:, :], ent1)):
                mm = nc.tensor.matmul(P[0:3, 0, 0:BH], featw[:, f, :], row, start=(f == 0), stop=(f == 2))
            mm.then_inc(sem("feats"), 1)
            pe.wait_ge(sem("feats_copied"), 1)
            nc.tensor.matmul(P[0:M1, 1, 0:BH], w("wb", "mw1", 3), feats1, start=True, stop=True)\
                .then_inc(sem("mlp_made"), 1)
            pe.wait_ge(sem("mlp_act"), 1)
            nc.tensor.matmul(P[0:M1, 2, 0:BH], w("wb", "mw2", M1), hid1, start=True, stop=True)\
                .then_inc(sem("mlp_made"), 1)
            pe.wait_ge(sem("mlp_act"), 2)
            nc.tensor.matmul(P[:, 3, 0:BH], w("wb", "mw3", M1), hid2, start=True, stop=True)\
                .then_inc(sem("mlp_made"), 1)
            pe.wait_ge(sem("logt"), 1)
            pe.sem_inc(sem("s2_mixed"), RING)
            pe.sem_inc(sem("s2_turned"), 8)
            with pe.Fori(0, B // 2) as i:
                for j in range(2):
                    pe.wait_ge(sem("s2_weighted"), 2 * i + j + 1)
                    for g in range(4):
                        pe.wait_ge(sem("s2_evac"), 8 * i + 4 * j + g + 1)
                        for k in range(4):
                            h = 4 * g + k
                            mm = nc.tensor.transpose(P[:, g, k * T:(k + 1) * T], wts1[j][:, h * T:(h + 1) * T], ident)
                        mm.then_inc(sem("s2_turned"), 1)
                    pe.wait_ge(sem("s2_normed"), 2 * i + j + 1)
                    for h in range(H1):
                        if h % 4 == 0:
                            pe.wait_ge(sem("s2_evac"), 8 * i + 4 * j + h // 4 + 1 + 4)
                        mm = nc.tensor.matmul(P[:, 4 + j, 0:T], vslots[j][:, h * 128:(h + 1) * 128],
                                              wtT1[j][:, h * T:(h + 1) * T], start=(h == 0), stop=(h == H1 - 1))
                    mm.then_inc(sem("s2_mixed"), 1)
            for h in range(2):
                pe.wait_ge(sem("s2_kept"), RING + B)
                nc.tensor.matmul(P[:, h, :], w("wb", "Wo"), half(oT1, h), start=True, stop=True)\
                    .then_inc(sem("stage_out"), 1)

        def act_stage1(act):
            act_norm(act, 1)
            for h in range(2):
                act.wait_ge(sem("q1_made"), h + 1)
                nc.scalar.activation(half(qT1, h), P[:, h, :], ACT.Identity, bias=col("bq"))\
                    .then_inc(sem("q1_ready"), 1)
            act.sem_inc(sem("s1_shifted_a"), RING)
            with act.Fori(0, B // 2) as i:
                for j in range(2):
                    act.wait_ge(sem("s1_max"), 4 * i + 2 * j + 2)
                    for h in range(SHIFT_D, H1):
                        ins = nc.scalar.activation(Dall[:, bass.ds(2 * i * HTK + j * HTK + h * T, T)],
                                                   P[:, 4 * j + h // 4, h % 4 * T:(h % 4 + 1) * T], ACT.Identity,
                                                   bias=nmax1[j][:, h:h + 1])
                    ins.then_inc(sem("s1_shifted_a"), 1)
                    act.wait_ge(sem("s1_shifted_a"), 2 * i + j + 1 + RING)
                    act.wait_ge(sem("s1_shifted"), 2 * i + j + 1 + RING)
                    act.wait_ge(sem("s1_stats"), 2 * i + j + 1)
                    nc.scalar.activation(exp1[j], Dall[:, bass.ds(2 * i * HTK + j * HTK, HTK)], ACT.Exp, scale=SC1)\
                        .then_inc(sem("s1_exp"), 1)
            act.wait_ge(sem("mlp_made"), 1)
            nc.scalar.activation(hid1, P[0:M1, 1, 0:BH], ACT.Gelu, bias=col("m1", M1)).then_inc(sem("mlp_act"), 1)
            act.wait_ge(sem("mlp_made"), 2)
            nc.scalar.activation(hid2, P[0:M1, 2, 0:BH], ACT.Gelu, bias=col("m2", M1)).then_inc(sem("mlp_act"), 1)
            act.wait_ge(sem("logt"), 1)
            nc.scalar.activation(temper1, logt1, ACT.Exp, scale=-1.0).then_inc(sem("temper"), 1)
            act.sem_inc(sem("s2_evac"), 4)
            act.sem_inc(sem("s2_kept"), RING)

            def exps(i, k):
                act.wait_ge(sem("s2_scaled"), 2 * i + k + 1)
                nc.scalar.activation(wts1[k % 2], wts1[k % 2], ACT.Exp).then_inc(sem("s2_exp"), 1)

            def evac(i, k):
                act.wait_ge(sem("s2_mixed"), 2 * i + k + 1)
                for g in range(4):
                    act.wait_ge(sem("s2_turned"), 8 * i + 4 * k + g + 1 + 8)
                    nc.scalar.copy(wtT1[k % 2][:, g * 512:(g + 1) * 512], P[:, g, :]).then_inc(sem("s2_evac"), 1)

            def keep(i, k):
                act.wait_ge(sem("s2_normed"), 2 * i + k + 1 + RING)
                nc.scalar.copy(oT1[:, bass.ds(2 * i * T + k * T, T)], o1[k % 2]).then_inc(sem("s2_kept"), 1)
            exps(0, 0)
            exps(0, 1)
            evac(0, 0)
            with act.Fori(0, B // 2 - 1) as i:
                for k in (2, 3):
                    exps(i, k)
                    evac(i, k - 1)
                    keep(i, k - 2)
            evac(0, B - 1)
            keep(0, B - 2)
            keep(0, B - 1)

        def dve_stage1(dve):
            dve_norm(dve, 1)
            chain(dve, nc.vector.tensor_reduce(ksum1[:, :], heads(kT1[:, :], B, T), AX, ALU.add))
            chain(dve, nc.vector.memset(featw[:, :, :], 0.0))
            chain(dve, nc.vector.memset(featw[:, 0, 0:1], SC1 / T / T))
            chain(dve, nc.vector.memset(featw[:, 1, 1:2], SC1 / T))
            chain(dve, nc.vector.memset(featw[:, 2, 2:3], 1.0 / T))
            dve.wait_ge(sem("q1_ready"), 2)
            chain(dve, nc.vector.tensor_reduce(qsum1[:, :], heads(qT1[:, :], B, T), AX, ALU.add))
            chain(dve, nc.vector.tensor_tensor(sim1[:, :], qsum1[:, :], ksum1[:, :], ALU.mult))
            chain(dve, nc.vector.tensor_tensor(heads(simrow1[:, :], B, H1), sim1[:, :].unsqueeze(2).broadcast_to([128, B, H1]),
                                          c("head").unsqueeze(1).broadcast_to([128, B, H1]), ALU.mult))
            dve.sem_inc(sem("s1_shifted"), RING)
            dve.sem_inc(sem("s1_stats"), RING)

            def shift(i, k):
                j = k % 2
                dve.wait_ge(sem("s1_scored"), 2 * i + k + 1 + RING)
                S = P[:, 4 * j:4 * j + 4, :].rearrange("p g (h k) -> p (g h) k", k=T)
                nc.vector.tensor_reduce(smax1[j][:, :], S, AX, ALU.max).then_inc(sem("s1_max"), 1)
                dve.wait_ge(sem("s1_max"), 4 * i + 2 * k + 1)
                nc.vector.tensor_scalar(nmax1[j][:, :], smax1[j][:, :], -1.0, None, ALU.mult)\
                    .then_inc(sem("s1_max"), 1)
                nc.vector.tensor_copy(max1[:, bass.ds(2 * i * H1 + k * H1, H1)], smax1[j][:, :])
                nc.vector.tensor_tensor(
                    heads(Dall[:, bass.ds(2 * i * HTK + k * HTK, SHIFT_D * T)], SHIFT_D, T), S[:, 0:SHIFT_D, :],
                    smax1[j][:, 0:SHIFT_D].unsqueeze(2).broadcast_to([128, SHIFT_D, T]), ALU.subtract)\
                    .then_inc(sem("s1_shifted"), 1)

            def stats(i, k):
                j = k % 2
                dve.wait_ge(sem("s1_exp"), 2 * i + k + 1)
                for h in range(H1):
                    bn = nc.vector.bn_stats(st1[j][:, h, :], exp1[j][:, h * T:(h + 1) * T])
                bn.then_inc(sem("s1_bn"), 1)
                dve.wait_ge(sem("s1_bn"), 2 * i + k + 1)
                nc.vector.tensor_copy(stats1[:, bass.ds(2 * i * H1 + k * H1, H1), :], st1[j][:, :, :])\
                    .then_inc(sem("s1_stats"), 1)
            shift(0, 0)
            shift(0, 1)
            stats(0, 0)
            with dve.Fori(0, B // 2 - 1) as i:
                for k in (2, 3):
                    shift(i, k)
                    stats(i, k - 1)
            stats(0, B - 1)
            dve.wait_ge(sem("s1_stats"), B + RING)
            me, ve, mo, vo = stats1[:, :, 1], stats1[:, :, 2], stats1[:, :, 4], stats1[:, :, 5]
            chain(dve, nc.vector.tensor_tensor(tmp1[0], me, mo, ALU.subtract))
            chain(dve, nc.vector.tensor_tensor(tmp1[0], tmp1[0], tmp1[0], ALU.mult))
            chain(dve, nc.vector.tensor_tensor(tmp1[1], ve, vo, ALU.add))
            chain(dve, nc.vector.scalar_tensor_tensor(tmp1[2], tmp1[0], T / 4.0, tmp1[1], ALU.mult, ALU.add))
            chain(dve, nc.vector.tensor_tensor(tmp1[3], me, mo, ALU.add))
            chain(dve, nc.vector.reciprocal(tmp1[4], tmp1[3]))
            chain(dve, nc.vector.tensor_tensor(tmp1[5], tmp1[2], tmp1[4], ALU.mult))
            nc.vector.scalar_tensor_tensor(ent1, tmp1[5], 4.0 / T / T / (T - 1), tmp1[4], ALU.mult, ALU.mult)\
                .then_inc(sem("feat_rows"), 1)
            dve.wait_ge(sem("feats"), 1)
            nc.vector.tensor_copy(feats1, P[0:3, 0, 0:BH]).then_inc(sem("feats_copied"), 1)
            dve.wait_ge(sem("mlp_made"), 3)
            chain(dve, nc.vector.tensor_scalar(logt1, P[:, 3, 0:BH], col("b3"), LOG_T_MIN, ALU.add, ALU.max))
            nc.vector.tensor_scalar(logt1, logt1, LOG_T_MAX, None, ALU.min).then_inc(sem("logt"), 1)
            dve.wait_ge(sem("temper"), 1)
            chain(dve, nc.vector.tensor_scalar(cool1, temper1, 0.5, None, ALU.mult))
            dve.sem_inc(sem("s2_normed"), RING)

            def scale(i, k):
                dve.wait_ge(sem("s2_turned"), 8 * i + 4 * k + 4)
                nc.vector.tensor_tensor(
                    heads(wts1[k % 2], H1, T), heads(Dall[:, bass.ds(2 * i * HTK + k * HTK, HTK)], H1, T),
                    cool1[:, bass.ds(2 * i * H1 + k * H1, H1)].unsqueeze(2).broadcast_to([128, H1, T]), ALU.mult)\
                    .then_inc(sem("s2_scaled"), 1)

            def total(i, k):
                dve.wait_ge(sem("s2_exp"), 2 * i + k + 1)
                nc.vector.tensor_reduce(z1[k % 2], heads(wts1[k % 2], H1, T), AX, ALU.add).then_inc(sem("s2_z"), 1)
                dve.wait_ge(sem("s2_z"), 2 * i + k + 1)
                nc.vector.reciprocal(rz1[k % 2], z1[k % 2]).then_inc(sem("s2_rz"), 1)

            def guard(i, k):
                j = k % 2
                dve.wait_ge(sem("s2_mixed"), 2 * i + k + 1 + RING)
                nc.vector.tensor_copy(raw1[j], P[:, 4 + j, 0:T]).then_inc(sem("s2_raw"), 1)
                dve.wait_ge(sem("s2_kept"), 2 * i + k + 1)
                nc.vector.memset(o1[j], 0.0).then_inc(sem("s2_raw"), 1)
                dve.wait_ge(sem("s2_raw"), 6 * i + 3 * k + 2)
                nc.vector.tensor_tensor(same1[j], raw1[j], raw1[j], ALU.is_equal).then_inc(sem("s2_raw"), 1)
                dve.wait_ge(sem("s2_raw"), 6 * i + 3 * k + 3)
                dve.sem_inc(sem("s2_guarded"), 1)
                nc.vector.copy_predicated(o1[j], same1[j], raw1[j]).then_inc(sem("s2_normed"), 1)
            scale(0, 0)
            scale(0, 1)
            total(0, 0)
            total(0, 1)
            with dve.Fori(0, B // 2 - 1) as i:
                for k in (2, 3):
                    scale(i, k)
                    guard(i, k - 2)
                    total(i, k)
            guard(0, B - 2)
            guard(0, B - 1)
            for h in range(2):
                dve.wait_ge(sem("stage_out"), 2 + h + 1)
                nc.vector.scalar_tensor_tensor(half(xT, h), P[:, h, :], col("bo"), half(xT, h), ALU.add, ALU.add)\
                    .then_inc(sem("x_ready"), 1)

        def pe_stage2(pe):
            pe_norm(pe, 2)
            pe.wait_ge(sem("fw_ready"), 1)

            def down(h):
                for cc in range(QC):
                    u = QC * h + cc
                    pe.wait_ge(sem("f_quant"), u + 1)
                    mm = nc.tensor.matmul(P[:, 4 + h, :], fw2q[:, cc * 128:(cc + 1) * 128], hq[:, u, :],
                                          start=(cc == 0), stop=(cc == QC - 1))
                mm.then_inc(sem("stage_out"), 1)
            for h in range(2):
                pe.wait_ge(sem("f_xq"), h + 1)
                for cc in range(QC):
                    u = QC * h + cc
                    if u >= 4:
                        pe.wait_ge(sem("f_copied"), u - 3)
                    nc.tensor.matmul(P[:, u % 4, :], fw1q[:, cc * 128:(cc + 1) * 128], half(xq, h),
                                     start=True, stop=True).then_inc(sem("f_hidden"), 1)
            down(0)
            down(1)

        def act_stage2(act):
            act_norm(act, 2)
            act.wait_ge(sem("fw_ready"), 1)
            for u in range(2 * QC):
                act.wait_ge(sem("f_hidden"), u + 1)
                if u >= 2:
                    act.wait_ge(sem("f_clipped"), u - 1)
                nc.scalar.activation(hraw[u % 2], P[:, u % 4, :], ACT.Identity, scale=1.0 / 64,
                                     bias=fbq[:, u % QC:u % QC + 1]).then_inc(sem("f_copied"), 1)

        def dve_stage2(dve):
            dve_norm(dve, 2)
            n = 0
            for h in range(2):
                dve.wait_ge(sem("xn_ready"), 4 + h + 1)
                nc.vector.tensor_scalar(half(xr, h), half(xn, h), 16.0, 127.0, ALU.mult, ALU.min)\
                    .then_inc(sem("f_step"), 1)
                dve.wait_ge(sem("f_step"), n + 1)
                nc.vector.tensor_scalar(half(xr, h), half(xr, h), -128.0, ROUND, ALU.max, ALU.add)\
                    .then_inc(sem("f_step"), 1)
                dve.wait_ge(sem("f_step"), n + 2)
                nc.vector.tensor_scalar(half(xq, h), half(xr, h), ROUND, None, ALU.subtract)\
                    .then_inc(sem("f_xq"), 1)
                n += 2
            for u in range(2 * QC):
                dve.wait_ge(sem("f_copied"), u + 1)
                nc.vector.tensor_scalar(hclip[u % 2], hraw[u % 2], 127.0, 0.0, ALU.min, ALU.max)\
                    .then_inc(sem("f_clipped"), 1)
                dve.wait_ge(sem("f_clipped"), u + 1)
                nc.vector.tensor_scalar(hq[:, u, :], hclip[u % 2], ROUND, ROUND, ALU.add, ALU.subtract)\
                    .then_inc(sem("f_quant"), 1)
            for h in range(2):
                dve.wait_ge(sem("stage_out"), 4 + h + 1)
                nc.vector.tensor_scalar(half(yq, h), P[:, 4 + h, :], 1.0 / 1024, fbq[:, QC:QC + 1],
                                        ALU.mult, ALU.add).then_inc(sem("f_out"), 1)
                dve.wait_ge(sem("f_out"), h + 1)
                nc.vector.tensor_tensor(half(xT, h), half(xT, h), half(yq, h), ALU.add)\
                    .then_inc(sem("x_ready"), 1)

        def sp_stage3(sp):
            sp.wait_ge(sem("dbl_copied"), 2)
            for k, r in enumerate((64, 0, 32)):
                sp.dma_start(scratch[k].rearrange("b s t -> s b t"), heads(dbl[r:r + NS, :], B, T))\
                    .then_inc(sem("dbl_stored"), 16)
            sp.wait_ge(sem("dbl_stored"), 48)
            for k, dst in enumerate((dtst, Bst, Cst)):
                sp.dma_start(dst, scratch[k].rearrange("b s t -> (b s) t")).then_inc(sem("states_loaded"), 16)

        def pe_stage3(pe):
            pe_norm(pe, 3)
            pe.wait_ge(sem("wd_loaded"), 16)
            for cc in range(2 * DC):
                for h in range(2):
                    u = 2 * cc + h
                    if u < 2:
                        pe.wait_ge(sem("xn_ready"), 6 + h + 1)
                    if u >= 4:
                        pe.wait_ge(sem("xz_copied"), u - 3)
                    nc.tensor.matmul(P[:, u % 4, :], w("wd", "Win")[:, cc * 128:(cc + 1) * 128], half(xn, h),
                                     start=True, stop=True).then_inc(sem("xz_made"), 1)
            pe.wait_ge(sem("conv_act"), DC)
            pe.wait_ge(sem("xn_ready"), 8)
            for h in range(2):
                for cc in range(DC):
                    mm = nc.tensor.matmul(P[0:80, 4 + h, :], w("wd", "Wx")[:, cc * 80:(cc + 1) * 80],
                                          xcv[:, cc * N + h * HALF:cc * N + (h + 1) * HALF],
                                          start=(cc == 0), stop=(cc == DC - 1))
                mm.then_inc(sem("dbl_made"), 1)
            pe.wait_ge(sem("xz_copied"), 4 * DC)

            def turn_back(g):
                pe.wait_ge(sem("ysum_copied"), g + 1)
                if g:
                    pe.wait_ge(sem("y3_copied"), g)
                for cc in range(DC):
                    mm = nc.tensor.transpose(P[:, 6, cc * 128:(cc + 1) * 128],
                                             ysum3[g % 2][:, cc * 128:(cc + 1) * 128], ident)
                mm.then_inc(sem("ysum_turned"), 1)

            def spread(t):
                if t >= LOOK:
                    pe.wait_ge(sem("u_made"), t - LOOK + 1)
                if by_act(t):
                    pe.wait_ge(sem("x_repeated_a"), t // 3 + 1)
                else:
                    pe.wait_ge(sem("x_repeated_p"), t - (t + 1) // 3 + 1)
                for cc in range(DC):
                    mm = nc.tensor.transpose(P[:, t % LOOK, cc * 128:(cc + 1) * 128],
                                             xe3[t % LOOK][:, cc * 128:(cc + 1) * 128], ident)
                mm.then_inc(sem("x_spread"), 1)
            for t in range(LOOK):
                spread(t)
            for t in range(T):
                if t == 0:
                    pe.wait_ge(sem("dbl_copied"), 2)
                g, k = divmod(t, STEPS)
                if k == 0 and g >= 2:
                    pe.wait_ge(sem("ysum_copied"), g - 1)
                if k % PLACED == 0:
                    pe.wait_ge(sem("c_placed"), t // PLACED + 1 + 1)
                pe.wait_ge(sem("h_clipped"), DC * (t + 1))
                nc.tensor.matmul(P[:, 4 + g % 2, 0:DI], Cpad[:, k * 128:(k + 1) * 128], h3[t % 4],
                                 start=(k == 0), stop=(k == STEPS - 1)).then_inc(sem("y_step"), 1)
                if t + LOOK < T:
                    spread(t + LOOK)
                if k == STEPS // 2 and g >= 1:
                    turn_back(g - 1)
                n, k = key_step(t)
                if 0 <= n < 2 * HT and k < 4:
                    if t == KEYS_AT:
                        pe.wait_ge(sem("we_loaded"), 16)
                    if k == 0 and n:
                        pe.wait_ge(sem("kv_copied_a"), n)
                    at = n % 2 * HALF + k * 128
                    mm = nc.tensor.matmul(P[:, 7, k * 128:(k + 1) * 128], Xk[:, n // 2 * 128:(n // 2 + 1) * 128],
                                          ctxT[:, at:at + 128], start=True, stop=True)
                    if k == 3:
                        mm.then_inc(sem("kv_made"), 1)
            turn_back(T // STEPS - 1)
            pe.wait_ge(sem("y3_gated"), DC)
            for h in range(2):
                for cc in range(DC):
                    mm = nc.tensor.matmul(P[:, 6 + h, :], w("wd", "Wout")[:, cc * 128:(cc + 1) * 128],
                                          yg3[1][:, cc * N + h * HALF:cc * N + (h + 1) * HALF],
                                          start=(cc == 0), stop=(cc == DC - 1))
                mm.then_inc(sem("stage_out"), 1)

        def pool_stage3(pool):
            pool.wait_ge(sem("x_ready"), 8)
            nc.gpsimd.memset(Cpad, 0.0).then_inc(sem("c_placed"), 1)
            pool.wait_ge(sem("conv_act"), DC)
            for t in range(LOOK):
                if not by_act(t):
                    repeat(pool, nc.gpsimd.tensor_copy, t)
            pool.wait_ge(sem("c_placed"), 1)
            pool.wait_ge(sem("states_loaded"), 48)
            for n in range(STEPS // PLACED):
                place(pool, n)
            for t in range(LOOK, T):
                if not by_act(t):
                    repeat(pool, nc.gpsimd.tensor_copy, t)
                if t % PLACED == 0 and t >= STEPS:
                    place(pool, t // PLACED)

        def place(pool, n):
            if n >= STEPS // PLACED:
                pool.wait_ge(sem("y_step"), n * PLACED - STEPS + PLACED)
            k = n * PLACED % STEPS
            nc.gpsimd.tensor_tensor(Cdiag[:, k:k + PLACED, :],
                                    Cst[:, n * PLACED:(n + 1) * PLACED].unsqueeze(2).broadcast_to([128, PLACED, B]),
                                    c("batch").unsqueeze(1).broadcast_to([128, PLACED, B]), ALU.mult)\
                .then_inc(sem("c_placed"), 1)

        def by_act(t):
            return t % 3 == 2

        def repeat(eng, copy, t):
            if t >= LOOK:
                eng.wait_ge(sem("x_spread"), t - LOOK + 1)
            copy(xe3[t % LOOK].rearrange("p (m s) -> p m s", s=NS),
                 xcv.rearrange("p (m t) -> p m t", t=T)[:, :, t:t + 1].broadcast_to([128, DC * B, NS]))\
                .then_inc(sem("x_repeated_a" if by_act(t) else "x_repeated_p"), 1)

        def act_stage3(act):
            act_norm(act, 3)
            for cc in range(2 * DC):
                for h in range(2):
                    u = 2 * cc + h
                    act.wait_ge(sem("xz_made"), u + 1)
                    if cc < DC:
                        nc.scalar.copy(xpad[:, cc, h * HB:(h + 1) * HB, 3:PADT],
                                       P[:, u % 4, :].rearrange("p (b t) -> p b t", b=HB)).then_inc(sem("xz_copied"), 1)
                    else:
                        at = (cc - DC) * N + h * HALF
                        nc.scalar.activation(sz[:, at:at + HALF], P[:, u % 4, :], ACT.Silu)\
                            .then_inc(sem("xz_copied"), 1)
            for cc in range(DC):
                act.wait_ge(sem("conv_done"), cc + 1)
                nc.scalar.activation(xcv[:, cc * N:(cc + 1) * N].rearrange("p (b t) -> p b t", b=B),
                                     conv[1][:, cc, :, :], ACT.Silu).then_inc(sem("conv_act"), 1)
            for h in range(2):
                act.wait_ge(sem("dbl_made"), h + 1)
                nc.scalar.copy(half(dbl, h), P[0:80, 4 + h, :]).then_inc(sem("dbl_copied"), 1)
            act.wait_ge(sem("states_loaded"), 48)
            nc.scalar.activation(dstep[0], dtst, ACT.Exp).then_inc(sem("dt_exp"), 1)
            nc.scalar.activation(negA, col("alog"), ACT.Exp).then_inc(sem("dt_exp"), 1)
            act.wait_ge(sem("gains"), 1)
            nc.scalar.activation(Abar, dstep[3], ACT.Exp).then_inc(sem("abar"), 1)
            act.wait_ge(sem("gains"), 2)
            repeat(act, nc.scalar.copy, 2)
            for t in range(T):
                act.wait_ge(sem("x_spread"), t + 1)
                if t >= LOOK:
                    act.wait_ge(sem("h_raw"), DC * (t - LOOK + 1))
                nc.scalar.activation(U3[t % LOOK], P[:, t % LOOK, 0:DI], ACT.Copy, scale=Bbar[:, t:t + 1])\
                    .then_inc(sem("u_made"), 1)
                if by_act(t + LOOK) and t + LOOK < T:
                    repeat(act, nc.scalar.copy, t + LOOK)
                g, k = divmod(t - STEPS, STEPS)
                if k == LOOK and g >= 0:
                    sums(act, g)
                if k == STEPS - LOOK and g >= 0:
                    collect(act, g)
                n, k = key_step(t - LOOK - 4)
                if 0 <= n < 2 * HT and k == 0:
                    act.wait_ge(sem("kv_made"), n + 1)
                    nc.scalar.copy(kT4[:, n // 2, n % 2 * HALF:(n % 2 + 1) * HALF], P[:, 7, :])\
                        .then_inc(sem("kv_copied_a"), 1)
            sums(act, T // STEPS - 1)
            collect(act, T // STEPS - 1)

        def sums(act, g):
            act.wait_ge(sem("y_step"), (g + 1) * STEPS)
            if g >= 2:
                act.wait_ge(sem("ysum_turned"), g - 1)
            nc.scalar.copy(ysum3[g % 2], P[:, 4 + g % 2, 0:DI]).then_inc(sem("ysum_copied"), 1)

        def collect(act, g):
            act.wait_ge(sem("ysum_turned"), g + 1)
            nc.scalar.copy(yT3.rearrange("p (c b t) -> p c b t", c=DC, b=B)[:, :, :, g * STEPS:(g + 1) * STEPS],
                           P[:, 6, 0:DI].rearrange("p (c t b) -> p c b t", c=DC, b=B))\
                .then_inc(sem("y3_copied"), 1)

        def dve_stage3(dve):
            dve_norm(dve, 3)
            chain(dve, nc.vector.memset(xpad[:, :, :, 0:3], 0.0))
            for cc in range(DC):
                dve.wait_ge(sem("xz_copied"), 2 * cc + 2)
                wv = col("conv_w")[:, 4 * cc:4 * cc + 4]
                chain(dve, nc.vector.tensor_scalar(conv[0][:, cc, :, :], xpad[:, cc, :, 0:T], wv[:, 0:1],
                                              col("conv_b")[:, cc:cc + 1], ALU.mult, ALU.add))
                for k in range(1, 4):
                    ins = nc.vector.scalar_tensor_tensor(conv[k % 2][:, cc, :, :], xpad[:, cc, :, k:k + T], wv[:, k:k + 1],
                                                         conv[(k + 1) % 2][:, cc, :, :], ALU.mult, ALU.add)
                    if k < 3:
                        chain(dve, ins)
                    else:
                        ins.then_inc(sem("conv_done"), 1)
            dve.wait_ge(sem("dt_exp"), 2)
            e, acc, tmp, dec = dstep
            chain(dve, nc.vector.tensor_scalar(e, e, 0.12, None, ALU.min))
            chain(dve, nc.vector.tensor_scalar(acc, e, -1.0 / 8, 1.0 / 7, ALU.mult, ALU.add))
            for k in range(6, 0, -1):
                chain(dve, nc.vector.tensor_tensor(tmp, acc, e, ALU.mult))
                chain(dve, nc.vector.tensor_scalar(acc, tmp, -1.0, 1.0 / k, ALU.mult, ALU.add))
            chain(dve, nc.vector.tensor_tensor(tmp, acc, e, ALU.mult))
            chain(dve, nc.vector.tensor_scalar(acc, tmp, DT_MIN, DT_MAX, ALU.max, ALU.min))
            chain(dve, nc.vector.tensor_scalar(tmp, acc, negA, -1.0, ALU.mult, ALU.mult))
            nc.vector.tensor_scalar(dec, tmp, -20.0, 0.0, ALU.max, ALU.min).then_inc(sem("gains"), 1)
            chain(dve, nc.vector.tensor_tensor(e, acc, Bst, ALU.mult))
            nc.vector.tensor_scalar(Bbar, e, -10.0, 10.0, ALU.max, ALU.min).then_inc(sem("gains"), 1)
            chain(dve, nc.vector.memset(h3[3], 0.0))
            dve.wait_ge(sem("abar"), 1)
            for t in range(T):
                dve.wait_ge(sem("u_made"), t + 1)
                for cc in range(DC):
                    cs = slice(cc * 128, (cc + 1) * 128)
                    if t:
                        dve.wait_ge(sem("h_clipped"), DC * (t - 1) + cc + 1)
                    nc.vector.scalar_tensor_tensor(hraw3[t % 2][:, cs], h3[(t - 1) % 4][:, cs], Abar[:, t:t + 1],
                                                   U3[t % LOOK][:, cs], ALU.mult, ALU.add).then_inc(sem("h_raw"), 1)
                if t >= 4:
                    dve.wait_ge(sem("y_step"), t - 3)
                for cc in range(DC):
                    cs = slice(cc * 128, (cc + 1) * 128)
                    dve.wait_ge(sem("h_raw"), DC * t + cc + 1)
                    nc.vector.tensor_scalar(h3[t % 4][:, cs], hraw3[t % 2][:, cs], 100.0, -100.0, ALU.min, ALU.max)\
                        .then_inc(sem("h_clipped"), 1)
            dve.wait_ge(sem("y3_copied"), T // STEPS)
            for cc in range(DC):
                cs = slice(cc * N, (cc + 1) * N)
                chain(dve, nc.vector.tensor_tensor(yg3[0][:, cs], yT3[:, cs], sz[:, cs], ALU.mult))
                nc.vector.scalar_tensor_tensor(yg3[1][:, cs], xcv[:, cs], col("dskip")[:, cc:cc + 1], yg3[0][:, cs],
                                               ALU.mult, ALU.add).then_inc(sem("y3_gated"), 1)
            for h in range(2):
                dve.wait_ge(sem("stage_out"), 6 + h + 1)
                nc.vector.tensor_tensor(half(xT, h), half(xT, h), P[:, 6 + h, :], ALU.add)\
                    .then_inc(sem("x_ready"), 1)

        def slot_head(g, k):
            tile = 4 * (g // 2) + k
            return tile, 64 * (g % 2), 2 * tile + g % 2

        QBANK = (2, 7)
        OH = 6

        def pe_stage4(pe):
            pe.wait_ge(sem("we_loaded"), 16)
            pe.wait_ge(sem("y3_gated"), DC)
            pe.wait_ge(sem("x_ready"), 8 + 2)
            for u in range(2 * HT):
                if u >= 4 and u % 2 == 0:
                    pe.wait_ge(sem("kv_copied_a"), 2 * HT + (u - 4) // 2 + 1)
                elif u >= 4:
                    pe.wait_ge(sem("kv_copied_d"), (u - 4) // 2 + 1)
                b, r = divmod(u, 2)
                nc.tensor.matmul(P[:, u % 4, :], ctxT[:, b * T:(b + 1) * T], Xv[:, r * 512:(r + 1) * 512],
                                 start=True, stop=True).then_inc(sem("kv_made"), 1)
            pe.sem_inc(sem("s4_scored"), 8)
            pe_norm(pe, 4)
            pe.wait_ge(sem("kv_copied_a"), 3 * HT)
            pe.wait_ge(sem("kv_copied_d"), HT)
            pe.wait_ge(sem("xn_ready"), 10)

            def queries(i, k):
                for r in range(2):
                    if r == 0:
                        pe.wait_ge(sem("s4_evac_a"), 4 * i + 2 * k + 1)
                    else:
                        pe.wait_ge(sem("s4_added"), 2 * i + k)
                    for m in range(4):
                        tile = 4 * r + m
                        mm = nc.tensor.matmul(P[:, QBANK[r], m * T:(m + 1) * T], Xq[:, tile * 128:(tile + 1) * 128],
                                              xn[:, bass.ds(2 * i * T + k * T, T)], start=True, stop=True)
                    mm.then_inc(sem("q4_made"), 1)

            def scores(i, k, g):
                pe.wait_ge(sem("q4_ready"), 4 * i + 2 * k + g // 2 + 1)
                pe.wait_ge(sem("s4_shifted"), 8 * i + 4 * k + g + 1)
                if g == 0:
                    pe.wait_ge(sem("k4_staged"), 2 * i + k + 1)
                for m in range(4):
                    tile, row, _ = slot_head(g, m)
                    mm = nc.tensor.matmul(P[:, g % 2, m * T:(m + 1) * T],
                                          q4[k % 2][row:row + K2, tile * T:(tile + 1) * T],
                                          ks4[k % 2][row:row + K2, tile * T:(tile + 1) * T], start=True, stop=True)
                mm.then_inc(sem("s4_scored"), 1)

            def turn(i, k, g):
                freed = sem("s4_evac_a") if g % 2 == 0 else sem("s4_evac_d")
                pe.wait_ge(sem("s4_exp"), 8 * i + 4 * k + g + 1)
                pe.wait_ge(freed, 4 * i + 2 * k + g // 2 + 1)
                for m in range(4):
                    s = 4 * g + m
                    mm = nc.tensor.transpose(P[:, 2 + g % 2, m * T:(m + 1) * T], wts4[k % 2][:, s * T:(s + 1) * T],
                                             ident)
                mm.then_inc(sem("s4_turned"), 1)

            def mix(i, k, g):
                if g == 0:
                    pe.wait_ge(sem("s4_evac_a"), 4 * i + 2 * k + 2 + 1)
                    pe.wait_ge(sem("s4_evac_d"), 4 * i + 2 * k + 2 + 1)
                    pe.wait_ge(sem("s4_normed"), 2 * i + k + 1)
                for s in range(4 * g, 4 * g + 4):
                    h = slot_head(s // 4, s % 4)[2]
                    at = (h % OH) * (K2 + 1)
                    mm = nc.tensor.matmul(P[:, 4 + h // OH, at:at + K2 + 1], wtT4[k % 2][:, s * T:(s + 1) * T],
                                          V4[:, bass.ds(2 * i * VW + k * VW + h * (K2 + 1), K2 + 1)],
                                          start=True, stop=True)
                if g == 3:
                    mm.then_inc(sem("s4_mixed"), 1)

            def turn_outs(i, k, r, bank_read=None):
                if r == 0:
                    pe.wait_ge(sem("s4_normed"), 2 * i + k + 1 + 1)
                    pe.wait_ge(sem("q4_ready"), bank_read)
                else:
                    pe.wait_ge(sem("s4_ocopied"), 4 * i + 2 * k + 1)
                for m in range(4):
                    tile = 4 * r + m
                    mm = nc.tensor.transpose(P[:, 7, m * T:(m + 1) * T], o4[k % 2][:, tile * T:(tile + 1) * T], ident)
                mm.then_inc(sem("s4_oturned"), 1)

            def project(i, k):
                pe.wait_ge(sem("s4_ocopied"), 4 * i + 2 * k + 2)
                for tile in range(HT):
                    mm = nc.tensor.matmul(P[:, 7, 0:T], Xo[:, tile * 128:(tile + 1) * 128],
                                          oT4[k % 2][:, tile * T:(tile + 1) * T], start=(tile == 0),
                                          stop=(tile == HT - 1))
                mm.then_inc(sem("y4"), 1)

            def batch(i, k):
                scores(i, k, 0)
                mix(i, k - 1, 0)
                scores(i, k, 1)
                mix(i, k - 1, 1)
                scores(i, k, 2)
                mix(i, k - 1, 2)
                mix(i, k - 1, 3)
                turn(i, k, 0)
                scores(i, k, 3)
                turn(i, k, 1)
                turn_outs(i, k - 1, 0, 4 * i + 2 * k + 2)
                turn(i, k, 2)
                turn_outs(i, k - 1, 1)
                turn(i, k, 3)
                project(i, k - 1)

            for r in range(2):
                for m in range(4):
                    tile = 4 * r + m
                    mm = nc.tensor.matmul(P[:, QBANK[r], m * T:(m + 1) * T], Xq[:, tile * 128:(tile + 1) * 128], xn[:, 0:T],
                                          start=True, stop=True)
                mm.then_inc(sem("q4_made"), 1)
            scores(0, 0, 0)
            scores(0, 0, 1)
            scores(0, 0, 2)
            turn(0, 0, 0)
            scores(0, 0, 3)
            turn(0, 0, 1)
            turn(0, 0, 2)
            turn(0, 0, 3)
            queries(0, 1)
            with pe.Fori(0, B // 2 - 1) as i:
                for k in (1, 2):
                    batch(i, k)
                    queries(i, k + 1)
            batch(B // 2 - 1, 1)
            for g in range(4):
                mix(B // 2 - 1, 1, g)
            turn_outs(B // 2 - 1, 1, 0, 2 * B)
            turn_outs(B // 2 - 1, 1, 1)
            project(B // 2 - 1, 1)

        def pool_stage4(pool):
            pool.wait_ge(sem("kv_copied_a"), 2 * HT)
            with pool.Fori(0, B // 2) as i:
                for j in range(2):
                    pool.wait_ge(sem("s4_scored"), 8 * i + 4 * j + 4)
                    nc.gpsimd.tensor_copy(heads(ks4[j][:, :], HT, T), kT4[:, :, bass.ds(2 * i * T + j * T, T)])\
                        .then_inc(sem("k4_staged"), 1)

        def value_copy(copy, u):
            b, r = divmod(u, 2)
            dst = V4.rearrange("p (b h k) -> p b h k", b=B, h=H2)[:, b, r * 8:(r + 1) * 8, 0:K2]
            return copy(dst, heads(P[:, u % 4, :], 8, K2))

        def act_stage4(act):
            for u in range(0, 2 * HT, 2):
                act.wait_ge(sem("kv_made"), 2 * HT + u + 1)
                if u == 0:
                    act.wait_ge(sem("v_ones"), 1)
                value_copy(nc.scalar.copy, u).then_inc(sem("kv_copied_a"), 1)
            act_norm(act, 4)
            act.wait_ge(sem("xn_ready"), 10)
            act.sem_inc(sem("s4_evac_a"), 1)

            def queries(i, k):
                for r in range(2):
                    act.wait_ge(sem("q4_made"), 4 * i + 2 * k + r + 1)
                    nc.scalar.copy(q4[k % 2][:, r * 512:(r + 1) * 512], P[:, QBANK[r], :]).then_inc(sem("q4_ready"), 1)

            def exps(i, k, g):
                act.wait_ge(sem("s4_shifted"), 8 * i + 4 * k + g + 1 + 2)
                wts = wts4[k % 2][:, g * 512:(g + 1) * 512]
                nc.scalar.activation(wts, wts, ACT.Exp, scale=SC2).then_inc(sem("s4_exp"), 1)

            def evac(i, k, g):
                act.wait_ge(sem("s4_turned"), 8 * i + 4 * k + g + 1)
                nc.scalar.copy(wtT4[k % 2][:, g * 512:(g + 1) * 512], P[:, 2, :]).then_inc(sem("s4_evac_a"), 1)

            def outs(i, k, r):
                act.wait_ge(sem("s4_oturned"), 4 * i + 2 * k + r + 1)
                nc.scalar.copy(oT4[k % 2][:, r * 512:(r + 1) * 512], P[:, 7, :]).then_inc(sem("s4_ocopied"), 1)

            def batch(i, k, before=True):
                exps(i, k, 0)
                exps(i, k, 1)
                exps(i, k, 2)
                evac(i, k, 0)
                if before:
                    outs(i, k - 1, 0)
                exps(i, k, 3)
                evac(i, k, 2)
                if before:
                    outs(i, k - 1, 1)
            queries(0, 0)
            batch(0, 0, before=False)
            queries(0, 1)
            with act.Fori(0, B // 2 - 1) as i:
                for k in (1, 2):
                    batch(i, k)
                    queries(i, k + 1)
            batch(B // 2 - 1, 1)
            outs(B // 2 - 1, 1, 0)
            outs(B // 2 - 1, 1, 1)

        def dve_stage4(dve):
            dve.wait_ge(sem("y3_gated"), DC)
            nc.vector.memset(V4.rearrange("p (n k) -> p n k", k=K2 + 1)[:, :, K2:K2 + 1], 1.0).then_inc(sem("v_ones"), 1)
            for u in range(1, 2 * HT, 2):
                dve.wait_ge(sem("kv_made"), 2 * HT + u + 1)
                value_copy(nc.vector.tensor_copy, u).then_inc(sem("kv_copied_d"), 1)
            dve_norm(dve, 4)
            dve.sem_inc(sem("s4_shifted"), 2)
            dve.sem_inc(sem("s4_evac_d"), 1)
            dve.sem_inc(sem("s4_normed"), 1)
            dve.sem_inc(sem("s4_added"), 1)

            def shift(i, k, g):
                dve.wait_ge(sem("s4_scored"), 8 * i + 4 * k + g + 1 + 8)
                S = heads(P[:, g % 2, :], 4, T)
                mx = smax4[k % 2][:, 4 * g:4 * g + 4]
                nc.vector.tensor_reduce(mx, S, AX, ALU.max).then_inc(sem("s4_max"), 1)
                dve.wait_ge(sem("s4_max"), 8 * i + 4 * k + g + 1)
                nc.vector.tensor_tensor(heads(wts4[k % 2][:, g * 512:(g + 1) * 512], 4, T), S,
                                        mx.unsqueeze(2).broadcast_to([128, 4, T]), ALU.subtract)\
                    .then_inc(sem("s4_shifted"), 1)

            def evac(i, k, g):
                dve.wait_ge(sem("s4_turned"), 8 * i + 4 * k + g + 1)
                nc.vector.tensor_copy(wtT4[k % 2][:, g * 512:(g + 1) * 512], P[:, 3, :]).then_inc(sem("s4_evac_d"), 1)

            def norm(i, k):
                dve.wait_ge(sem("s4_mixed"), 2 * i + k + 1)
                parts = [(p, min(OH, H2 - p * OH)) for p in range(3)]
                for p, n in parts:
                    O = P[:, 4 + p, 0:n * (K2 + 1)].rearrange("p (h k) -> p h k", h=n)
                    nc.vector.reciprocal(rz4[k % 2][:, p * OH:p * OH + n], O[:, :, K2]).then_inc(sem("s4_rz"), 1)
                for p, n in parts:
                    dve.wait_ge(sem("s4_rz"), 10 * i + 5 * k + p + 1)
                    O = P[:, 4 + p, 0:n * (K2 + 1)].rearrange("p (h k) -> p h k", h=n)
                    ins = nc.vector.tensor_tensor(heads(o4[k % 2][:, p * OH * K2:(p * OH + n) * K2], n, K2), O[:, :, 0:K2],
                                                  rz4[k % 2][:, p * OH:p * OH + n].unsqueeze(2).broadcast_to([128, n, K2]),
                                                  ALU.mult)
                    ins.then_inc(sem("s4_normed" if p == 2 else "s4_rz"), 1)

            def add(i, k):
                dve.wait_ge(sem("y4"), 2 * i + k + 1)
                xb = xT[:, bass.ds(2 * i * T + k * T, T)]
                nc.vector.tensor_tensor(xb, xb, P[:, 7, 0:T], ALU.add).then_inc(sem("s4_added"), 1)
            def batch(i, k, before=True):
                shift(i, k, 0)
                shift(i, k, 1)
                shift(i, k, 2)
                if before:
                    norm(i, k - 1)
                shift(i, k, 3)
                evac(i, k, 1)
                evac(i, k, 3)
                if before:
                    add(i, k - 1)
            batch(0, 0, before=False)
            with dve.Fori(0, B // 2 - 1) as i:
                batch(i, 1)
                batch(i, 2)
            batch(B // 2 - 1, 1)
            norm(B // 2 - 1, 1)
            add(B // 2 - 1, 1)
            dve.drain().then_inc(sem("x_ready"), 2)

        def sp_stage5(sp):
            sp.wait_ge(sem("x_ready"), 12)
            for i in range(E2 // RW):
                for k in range(RW // 2):
                    e = RW * i + 2 * k
                    if i:
                        sp.wait_ge(sem("e5_out"), e - RW + 2)
                    sp.dma_start(wring[:, 2 * k:2 * k + 2, :], d["moe"][e:e + 2].rearrange("e p n -> p e n"))\
                        .then_inc(sem(f"moe_loaded{k}"), 16)
            sp.wait_ge(sem("zero5"), 1)
            sp.dma_start(slots_dram[SLOTS:SLOTS + 1, :], zero5[0:1, :]).then_inc(sem("slots_stored"), 16)
            for i in range(2):
                ne = E2 // 2
                sp.wait_ge(sem("e5_kept"), ne * (i + 1))
                sp.dma_start(slots_dram[i * ne * CAP:(i + 1) * ne * CAP, :].rearrange("(e s) d -> s e d", s=CAP),
                             eo5[:, i * ne:(i + 1) * ne, :]).then_inc(sem("slots_stored"), 16)

        def pe_stage5(pe):
            pe_norm(pe, 5)
            for b in range(B):
                if b % HB == 0:
                    pe.wait_ge(sem("xn_ready"), 10 + b // HB + 1)
                mm = nc.tensor.matmul(heads(P[:, 0, 0:B * E2], B, E2)[:, b, :], xn[:, b * T:(b + 1) * T],
                                      w("wf", "gate"), start=True, stop=True)
            mm.then_inc(sem("gates"), 1)
            for b in range(B):
                mm = nc.tensor.transpose(P[:, 3 + b // HB, (b % HB) * T:(b % HB + 1) * T], xn[:, b * T:(b + 1) * T], ident)
            mm.then_inc(sem("tokens"), 1)
            pe.wait_ge(sem("top1"), 1)
            nc.tensor.matmul(P[:, 1, 0:B * E2], c("tri"), g5[3].rearrange("p b e -> p (b e)"), start=True, stop=True)\
                .then_inc(sem("counts"), 1)
            nc.tensor.matmul(P[:, 2, 0:B * E2], mean128[:, :], g5[3].rearrange("p b e -> p (b e)"), start=True, stop=True)\
                .then_inc(sem("counts"), 1)
            pe.wait_ge(sem("xpart"), 3)
            chunks = [(0, 512), (512, 512), (1024, SLOTS - 1024)]
            for b in range(B):
                pe.wait_ge(sem("hot"), b + 1)
                for part in range(3):
                    lhs = xpart[:, part * N + b * T:part * N + (b + 1) * T]
                    for k, (a, n) in enumerate(chunks):
                        mm = nc.tensor.matmul(P[:, 5 + k, 0:n], lhs, hot5[b % 4][:, a:a + n],
                                              start=(b == 0 and part == 0), stop=(b == B - 1 and part == 2))
                mm.then_inc(sem("hot_used"), 1)

            def up(e):
                pe.wait_ge(sem(f"moe_loaded{e % RW // 2}"), 16 * (e // RW + 1))
                if e == 0:
                    pe.wait_ge(sem("dispatched"), 3)
                if e >= 2:
                    pe.wait_ge(sem("e5_act"), e - 1)
                for k in range(FC):
                    mm = nc.tensor.matmul(P[:, e % 2, k * CAP:(k + 1) * CAP], w1r[e % RW][:, k * 128:(k + 1) * 128],
                                          dT5[:, e * CAP:(e + 1) * CAP], start=True, stop=True)
                mm.then_inc(sem("e5_hidden"), 1)

            def down(e):
                pe.wait_ge(sem("e5_act"), e + 1)
                if e >= 2:
                    pe.wait_ge(sem("e5_kept"), e - 1)
                for k in range(FC):
                    mm = nc.tensor.matmul(P[0:CAP, 2 + e % 2, 0:D], hT5[e % 2][:, k * CAP:(k + 1) * CAP],
                                          w2r[e % RW][:, k * D:(k + 1) * D], start=(k == 0), stop=(k == FC - 1))
                mm.then_inc(sem("e5_out"), 1)
            up(0)
            for e in range(E2):
                if e + 1 < E2:
                    up(e + 1)
                down(e)
            for b in range(B):
                mm = nc.tensor.transpose(P[:, 5 + b // HB, (b % HB) * T:(b % HB + 1) * T], xT[:, b * T:(b + 1) * T], ident)
            mm.then_inc(sem("out_turned"), 1)

        def act_stage5(act):
            act_norm(act, 5)
            act.wait_ge(sem("gate_shift"), 1)
            nc.scalar.activation(g5[5], g5[4], ACT.Exp).then_inc(sem("gate_exp"), 1)
            for part in range(3):
                if part == 0:
                    act.wait_ge(sem("tokens"), 1)
                    for r in range(2):
                        nc.scalar.copy(xpart[:, r * HALF:(r + 1) * HALF], P[:, 3 + r, :])
                    act.drain().then_inc(sem("xpart"), 1)
                else:
                    act.wait_ge(sem("xrest"), part)
                    nc.scalar.copy(xpart[:, part * N:(part + 1) * N], xrest[part - 1]).then_inc(sem("xpart"), 1)
            for k, (a, n) in enumerate([(0, 512), (512, 512), (1024, SLOTS - 1024)]):
                act.wait_ge(sem("hot_used"), B)
                nc.scalar.copy(dT5[:, a:a + n], P[:, 5 + k, 0:n]).then_inc(sem("dispatched"), 1)
            for e in range(E2):
                act.wait_ge(sem("e5_hidden"), e + 1)
                if e >= 2:
                    act.wait_ge(sem("e5_out"), e - 1)
                nc.scalar.activation(hT5[e % 2], P[:, e % 2, 0:FC * CAP], ACT.Gelu_apprx_tanh).then_inc(sem("e5_act"), 1)

        def dve_stage5(dve):
            dve_norm(dve, 5)

            def per(v, n=E2):
                return v.unsqueeze(2).broadcast_to([128, B, n])

            def row(name):
                return c(name).unsqueeze(1).broadcast_to([128, B, E2])
            nc.vector.memset(zero5, 0.0).then_inc(sem("zero5"), 1)
            dve.wait_ge(sem("gates"), 1)
            G = heads(P[:, 0, 0:B * E2], B, E2)
            chain(dve, nc.vector.tensor_reduce(v5[0], G, AX, ALU.max))
            nc.vector.tensor_tensor(g5[4], G, per(v5[0]), ALU.subtract).then_inc(sem("gate_shift"), 1)
            dve.wait_ge(sem("gate_shift"), 1)
            chain(dve, nc.vector.tensor_scalar(g5[0], g5[4], 0.0, None, ALU.is_equal))
            chain(dve, nc.vector.tensor_tensor(g5[1], g5[0], row("prio16"), ALU.mult))
            chain(dve, nc.vector.tensor_reduce(v5[1], g5[1], AX, ALU.max))
            nc.vector.tensor_tensor(g5[3], g5[1], per(v5[1]), ALU.is_equal).then_inc(sem("top1"), 1)
            dve.wait_ge(sem("xpart"), 1)
            for r in range(2):
                nc.vector.tensor_tensor(half(xrest[0], r), P[:, 3 + r, :], half(xpart, r), ALU.subtract)
            dve.drain().then_inc(sem("xrest"), 1)
            dve.wait_ge(sem("counts"), 2)
            chain(dve, nc.vector.memset(g5[2][:, 0, :], 0.0))
            M = heads(P[:, 2, 0:B * E2], B, E2)
            for b in range(1, B):
                chain(dve, nc.vector.scalar_tensor_tensor(g5[2][:, b, :], M[:, b - 1, :], float(D), g5[2][:, b - 1, :],
                                                     ALU.mult, ALU.add))
            chain(dve, nc.vector.tensor_tensor(g5[6], heads(P[:, 1, 0:B * E2], B, E2), g5[2], ALU.add))
            chain(dve, nc.vector.tensor_tensor(g5[7], g5[6], g5[3], ALU.mult))
            chain(dve, nc.vector.tensor_reduce(v5[2], g5[7], AX, ALU.add))
            chain(dve, nc.vector.tensor_tensor(g5[6], row("ebase"), g5[3], ALU.mult))
            chain(dve, nc.vector.tensor_reduce(v5[3], g5[6], AX, ALU.add))
            chain(dve, nc.vector.tensor_scalar(v5[4], v5[2], float(CAP), 2.0 * SLOTS, ALU.is_gt, ALU.mult))
            chain(dve, nc.vector.scalar_tensor_tensor(v5[5], v5[2], -1.0, v5[3], ALU.add, ALU.add))
            chain(dve, nc.vector.tensor_tensor(v5[6], v5[5], v5[4], ALU.add))
            nc.vector.tensor_scalar(idx5, v5[6], float(SLOTS), None, ALU.min).then_inc(sem("slots"), 1)
            dve.wait_ge(sem("xpart"), 2)
            chain(dve, nc.vector.tensor_tensor(xrest[1], xrest[0], xpart[:, N:2 * N], ALU.subtract))
            dve.drain().then_inc(sem("xrest"), 1)
            for b in range(B):
                if b >= 4:
                    dve.wait_ge(sem("hot_used"), b - 3)
                nc.vector.tensor_scalar(hot5[b % 4], c("iota"), v5[6][:, b:b + 1], None, ALU.is_equal)\
                    .then_inc(sem("hot"), 1)
            dve.wait_ge(sem("gate_exp"), 1)
            chain(dve, nc.vector.tensor_reduce(v5[0], g5[5], AX, ALU.add))
            chain(dve, nc.vector.reciprocal(v5[7], v5[0]))
            for e in range(E2):
                dve.wait_ge(sem("e5_out"), e + 1)
                nc.vector.tensor_copy(eo5[:, e, :], P[0:CAP, 2 + e % 2, 0:D]).then_inc(sem("e5_kept"), 1)
            dve.wait_ge(sem("out_turned"), 1)
            for b in range(B):
                if b == 0:
                    dve.wait_ge(sem("gathered"), 16 * B)
                ins = nc.vector.scalar_tensor_tensor(
                    final[:, b * D:(b + 1) * D], yg5[:, b * D:(b + 1) * D], v5[7][:, b:b + 1],
                    P[:, 5 + b // HB, (b % HB) * D:(b % HB + 1) * D], ALU.mult, ALU.add)
            dve.drain().then_inc(sem("out_ready"), 1)

        def pool_stage5(pool):
            pool.wait_ge(sem("slots"), 1)
            pool.wait_ge(sem("slots_stored"), 48)
            for b in range(B):
                pool.indirect_dma_start(yg5[:, b * D:(b + 1) * D], None, slots_dram,
                                        bass.IndirectOffsetOnAxis(ap=idx5[:, b:b + 1], axis=0)).then_inc(sem("gathered"), 16)

        nothing = lambda engine: None
        pe_stages = [pe_stage0, pe_stage1, pe_stage2, pe_stage3, pe_stage4, pe_stage5]
        act_stages = [act_stage0, act_stage1, act_stage2, act_stage3, act_stage4, act_stage5]
        dve_stages = [dve_stage0, dve_stage1, dve_stage2, dve_stage3, dve_stage4, dve_stage5]
        pool_stages = [pool_stage0 if stop > 1 else nothing, pool_stage1, nothing, pool_stage3, pool_stage4, pool_stage5]

        @block.sync
        def _(sp):
            sp.dma_start(heads(xtok, B, D), d["x"].rearrange("b t d -> t b d")).then_inc(sem("x_loaded"), 16)
            sp.dma_start(packs["small"][:, :], d["small"]).then_inc(sem("small_loaded"), 16)
            sp.dma_start(heads(ctok, B, D), d["ctx"].rearrange("b t d -> t b d")).then_inc(sem("ctx_loaded"), 16)
            for k in ("wb", "wa", "consts", "wc", "wd", "wf"):
                sp.dma_start(packs[k][:, :], d[k]).then_inc(sem(k + "_loaded"), 16)
            if stop > 3:
                sp_stage3(sp)
            if stop > 4:
                sp.wait_ge(sem("conv_act"), DC)
                sp.dma_start(we, d["we"]).then_inc(sem("we_loaded"), 16)
            if stop > 5:
                sp_stage5(sp)
            sp.wait_ge(sem("out_ready"), 1)
            sp.dma_start(out.rearrange("b t d -> t b d"), heads(final if stop > 5 else xc, B, D))\
                .then_inc(sem("stored"), 16)
            sp.wait_ge(sem("stored"), 16)

        @block.tensor
        def _(pe):
            pe.wait_ge(sem("small_loaded"), 16)
            pe.wait_ge(sem("x_loaded"), 16)
            for b in range(B):
                mm = nc.tensor.transpose(P[:, b // HB, (b % HB) * T:(b % HB + 1) * T], xtok[:, b * D:(b + 1) * D], ident)
                if b % HB == HB - 1:
                    mm.then_inc(sem("x_turned"), 1)
            pe.wait_ge(sem("ctx_loaded"), 16)
            for b in range(B):
                mm = nc.tensor.transpose(P[:, 2 + b // HB, (b % HB) * T:(b % HB + 1) * T], ctok[:, b * D:(b + 1) * D], ident)
                if b % HB == HB - 1:
                    mm.then_inc(sem("ctx_turned"), 1)
            pe.wait_ge(sem("means_set"), 3)
            if stop > 1:
                pe_keys1(pe)
            for f in pe_stages[:stop]:
                f(pe)
            if stop > 5:
                return
            for h in range(2):
                pe.wait_ge(sem("x_ready"), 2 * stop + h + 1)
            for b in range(B):
                mm = nc.tensor.transpose(P[:, b // HB, (b % HB) * T:(b % HB + 1) * T], xT[:, b * T:(b + 1) * T], ident)
            mm.then_inc(sem("out_turned"), 1)

        @block.scalar
        def _(act):
            act.wait_ge(sem("small_loaded"), 16)
            act.wait_ge(sem("means_set"), 3)
            for h in range(2):
                act.wait_ge(sem("ctx_turned"), h + 1)
                nc.scalar.copy(half(ctxT, h), P[:, 2 + h, :]).then_inc(sem("ctx_ready"), 1)
            if stop > 1:
                act_keys1(act)
            for f in act_stages[:stop]:
                f(act)
            if stop > 5:
                return
            act.wait_ge(sem("out_turned"), 1)
            act.wait_ge(sem("xn_ready"), 2 * stop)
            for h in range(2):
                nc.scalar.copy(half(xc, h), P[:, h, :])
            act.drain().then_inc(sem("out_ready"), 1)

        @block.vector
        def _(dve):
            nc.vector.memset(mean128[:, :], 1.0 / D).then_inc(sem("means_set"), 1)
            nc.vector.memset(mean64[:, :], 1.0 / R0).then_inc(sem("means_set"), 1)
            nc.vector.memset(eps[:, :], EPS).then_inc(sem("means_set"), 1)
            dve.wait_ge(sem("small_loaded"), 16)
            for h in range(2):
                dve.wait_ge(sem("x_turned"), h + 1)
                nc.vector.tensor_copy(half(xT, h), P[:, h, :]).then_inc(sem("x_ready"), 1)
            if stop > 1:
                dve_keys1(dve)
            for f in dve_stages[:stop]:
                f(dve)

        @block.gpsimd
        def _(pool):
            for f in pool_stages[:stop]:
                f(pool)


_INS = ["x", "ctx", "consts", "small", "wa", "wb", "wc", "wd", "we", "wf", "moe"]


def constants():
    p = np.arange(128)
    c = {
        "head": p[:, None] // K1 == np.arange(H1), "batch": p[:, None] // NS == np.arange(B),
        "tri": p[:, None] <= p[None, :], "prio6": np.tile(E0 - np.arange(E0), (128, 1)),
        "prio16": np.tile(E2 - np.arange(E2), (128, 1)), "ebase": np.tile(CAP * np.arange(E2), (128, 1)),
        "iota": np.tile(np.arange(SLOTS), (128, 1)),
    }
    owner = np.repeat(ORDER, F0)
    c["select"] = (p[:, None] % 32 == owner[None, :]) & (p[:, None] >= 32)
    return np.concatenate([np.asarray(c[n], np.float32).reshape(128, k) for n, k in CONSTS], 1)


def pack(pieces):
    return np.concatenate([np.pad(a, ((0, 128 - a.shape[0]), (0, 0))) for a in pieces], 1)


def kernel(**inputs):
    import concourse.bacc as _bacc
    from concourse.bass_utils import run_bass_kernel_spmd as _run
    i = {k: np.asarray(v) for k, v in inputs.items()}

    def v(name):
        a = i[name].reshape(-1)
        return a.reshape(-1, min(128, a.size)).T

    def r(name):
        return np.broadcast_to(i[name].reshape(1, -1), (128, i[name].size))

    def tiles(a):
        return a.reshape(-1, 128, a.shape[1]).transpose(1, 0, 2).reshape(128, -1)
    W1 = i["L0_attn_W1"][ORDER]
    cw = i["L1_attn_conv_w"].reshape(DC, 128, 4).transpose(1, 0, 2).reshape(128, -1)
    Wx = i["L1_attn_W_xproj"]
    zx = np.zeros((16, DI), np.float32)
    wx = np.concatenate([Wx[0:NS], zx, Wx[NS:2 * NS], zx, np.broadcast_to(Wx[2 * NS:], (NS, DI))], 0)
    arrays = {
        "x": i["x"], "ctx": i["ctx_1024"], "consts": constants(),
        "small": pack([v("L0_attn_r1_b"), v("L0_attn_ln_g"), v("L0_attn_ln_b"),
                       i["L0_attn_b1"][ORDER].reshape(C0, 128).T, v("L0_xattn_bq"), v("L0_xattn_bk"),
                       v("L0_xattn_bo"), v("L0_xattn_b1"), v("L0_xattn_b2"), v("L0_ffn_b1"), v("L0_ffn_b2"),
                       cw, v("L1_attn_conv_b"), v("L1_attn_D_param"),
                       np.tile(i["L1_attn_A_log"], B).reshape(128, 1),
                       r("L0_attn_r2_b"), r("L0_attn_route_bias"), r("L0_attn_temp"), r("L0_xattn_bv"),
                       r("L0_xattn_b3"), np.eye(128, dtype=np.float32)]),
        "wa": pack([i["L0_attn_r1_w"], i["L0_attn_r2_w"], W1.transpose(1, 0, 2).reshape(D, -1),
                    tiles(i["L0_attn_W2"][ORDER].reshape(-1, D)), i["L0_attn_b2"]]),
        "wb": pack([i["L0_xattn_Wq"].T, i["L0_xattn_Wk"].T, i["L0_xattn_Wv"].T, i["L0_xattn_Wo"].T,
                    i["L0_xattn_w1"].T, i["L0_xattn_w2"].T, np.broadcast_to(i["L0_xattn_w3"].T, (M1, 128))]),
        "wc": pack([i["L0_ffn_w1"].T, tiles(i["L0_ffn_w2"].T)]),
        "wd": pack([i["L1_attn_W_in"].T, tiles(wx.T), tiles(i["L1_attn_W_out"].T)]),
        "we": pack([i["L1_xattn_" + n].reshape(D, -1) for n in ("Wq", "Wk", "Wv")]
                   + [tiles(i["L1_xattn_Wo"].reshape(-1, D))]),
        "wf": pack([i["L1_ffn_gate_w"].T]),
        "moe": np.concatenate([i["L1_ffn_w1"], i["L1_ffn_w2"].reshape(E2, FC, 128, D).transpose(0, 2, 1, 3)
                               .reshape(E2, 128, FC * D)], 2),
    }
    nc = _bacc.Bacc("TRN2", target_bir_lowering=False, num_devices=1)
    feed, d = {}, {}
    for name in _INS:
        feed[f"in_{name}_dram"] = np.ascontiguousarray(arrays[name])
        d[name] = nc.dram_tensor(f"in_{name}_dram", feed[f"in_{name}_dram"].shape, F32, kind="ExternalInput").ap()
    out = nc.dram_tensor("out_0_dram", (B, T, D), F32, kind="ExternalOutput").ap()
    program(nc, d, out, 6)
    res = _run(nc, [feed], core_ids=[0])
    return res.results[0]["out_0_dram"]
```
